# Optimizing a Trainium2 kernel written in Bass

```python
import numpy as np
import jax
import jax.numpy as jnp

def _softmax(x, axis=-1):
    return jax.nn.softmax(x, axis=axis)

def _gelu(x):
    return jax.nn.gelu(x, approximate=True)

def _silu(x):
    return jax.nn.silu(x)

def _sigmoid(x):
    return jax.nn.sigmoid(x)

def _layernorm(x, axis=-1, eps=1e-05):
    m = jnp.mean(x, axis=axis, keepdims=True)
    v = jnp.var(x, axis=axis, keepdims=True)
    return (x - m) / jnp.sqrt(v + eps)

def _scatter_add(tgt, idx, src, axis=0):
    return tgt.at[idx].add(src)

def _segment_sum(src, seg, n):
    return jax.ops.segment_sum(src, seg, n)
kernel_name = 'mk_prb_d2_jaxref_r4_b24995'

def setup_inputs(seed: int=0):
    np.random.seed(seed)
    _w = jnp.asarray

    def _L0_attn_setup():
        import jax, jax.numpy as jnp
        import numpy as np
        B_, S_, D_, N_ = (4, 512, 256, 16)

        def _layernorm(y, w, b, eps=1e-05):
            mu = jnp.mean(y, axis=-1, keepdims=True)
            var = jnp.mean((y - mu) ** 2, axis=-1, keepdims=True)
            return (y - mu) * jax.lax.rsqrt(var + eps) * w + b
        key = jax.random.key(seed)
        ks = jax.random.split(key, 8)
        x = jax.random.normal(ks[0], (B_, S_, D_), dtype=jnp.float32)
        A = jax.random.normal(ks[1], (D_, N_, N_), dtype=jnp.float32) * 0.1
        Bm = jax.random.normal(ks[2], (D_, N_), dtype=jnp.float32) * 0.1
        Cm = jax.random.normal(ks[3], (D_, N_), dtype=jnp.float32) * 0.1
        Dm = jax.random.normal(ks[4], (D_,), dtype=jnp.float32) * 0.1
        ln_w = jnp.ones((D_,), dtype=jnp.float32)
        ln_b = jnp.zeros((D_,), dtype=jnp.float32)
        W_out = jax.random.normal(ks[5], (D_, D_), dtype=jnp.float32) * (1.0 / np.sqrt(D_))
        b_out = jnp.zeros((D_,), dtype=jnp.float32)
        return {'x': x, 'A': A, 'Bm': Bm, 'Cm': Cm, 'Dm': Dm, 'ln_w': ln_w, 'ln_b': ln_b, 'W_out': W_out, 'b_out': b_out}
    _L0_attn_in = _L0_attn_setup()

    def _L0_ffn_setup():
        import jax, jax.numpy as jnp
        import numpy as np
        B, S, H = (2, 1024, 256)
        I = 128
        E = 8
        TOPK = 2
        NGROUP = 2
        TOPK_GROUP = 1
        ROUTED_SCALE = 1.0

        def _silu(x):
            return x * jax.nn.sigmoid(x)
        key = jax.random.key(seed)
        ks = jax.random.split(key, 9)

        def w(k, shape, s=0.05):
            return jax.random.normal(k, shape, dtype=jnp.float32) * s
        return {'hidden_states': jax.random.normal(ks[0], (B, S, H), dtype=jnp.float32), 'router_weight': w(ks[1], (E, H)), 'correction_bias': w(ks[2], (E,)), 'w_gate': w(ks[3], (E, H, I)), 'w_up': w(ks[4], (E, H, I)), 'w_down': w(ks[5], (E, I, H)), 'sw_gate': w(ks[6], (H, I)), 'sw_up': w(ks[7], (H, I)), 'sw_down': w(ks[8], (I, H))}
    _L0_ffn_in = _L0_ffn_setup()

    def _L1_attn_setup():
        import jax, jax.numpy as jnp
        import numpy as np
        N_HEADS = 1
        LATENT_DIM = 256
        SCALE = 1.0 / float(np.sqrt(LATENT_DIM * N_HEADS))
        key = jax.random.key(seed)
        kx, kq, ko = jax.random.split(key, 3)
        B, S, D = (4, 1024, 256)
        x = jax.random.normal(kx, (B, S, D), dtype=jnp.float32)
        w_qkv = jax.random.normal(kq, (3 * N_HEADS * (LATENT_DIM // N_HEADS), D), dtype=jnp.float32) * 0.02
        w_o = jax.random.normal(ko, (LATENT_DIM, N_HEADS * (LATENT_DIM // N_HEADS)), dtype=jnp.float32) * 0.02
        return {'x': x, 'w_qkv': w_qkv, 'w_o': w_o}
    _L1_attn_in = _L1_attn_setup()

    def _L1_ffn_setup():
        import jax, jax.numpy as jnp
        import numpy as np
        E = 8
        K = 2
        CAP_FACTOR = 1.0
        key = jax.random.key(seed)
        k0, k1, k2, k3 = jax.random.split(key, 4)
        B, S, M, H = (4, 512, 256, 1024)
        x = jax.random.normal(k0, (B, S, M), jnp.float32)
        wg = jax.random.normal(k1, (M, E), jnp.float32) * 0.02
        w1 = jax.random.normal(k2, (E, M, H), jnp.float32) * 0.02
        b1 = jnp.zeros((E, H), jnp.float32)
        w2 = jax.random.normal(k3, (E, H, M), jnp.float32) * 0.02
        b2 = jnp.zeros((E, M), jnp.float32)
        return {'x': x, 'wg': wg, 'w1': w1, 'b1': b1, 'w2': w2, 'b2': b2}
    _L1_ffn_in = _L1_ffn_setup()
    _d = {'L0_attn_x': _L0_attn_in['x'], 'L0_attn_A': _L0_attn_in['A'], 'L0_attn_Bm': _L0_attn_in['Bm'], 'L0_attn_Cm': _L0_attn_in['Cm'], 'L0_attn_Dm': _L0_attn_in['Dm'], 'L0_attn_ln_w': _L0_attn_in['ln_w'], 'L0_attn_ln_b': _L0_attn_in['ln_b'], 'L0_attn_W_out': _L0_attn_in['W_out'], 'L0_attn_b_out': _L0_attn_in['b_out'], 'L0_ffn_router_weight': _L0_ffn_in['router_weight'], 'L0_ffn_correction_bias': _L0_ffn_in['correction_bias'], 'L0_ffn_w_gate': _L0_ffn_in['w_gate'], 'L0_ffn_w_up': _L0_ffn_in['w_up'], 'L0_ffn_w_down': _L0_ffn_in['w_down'], 'L0_ffn_sw_gate': _L0_ffn_in['sw_gate'], 'L0_ffn_sw_up': _L0_ffn_in['sw_up'], 'L0_ffn_sw_down': _L0_ffn_in['sw_down'], 'L1_attn_w_qkv': _L1_attn_in['w_qkv'], 'L1_attn_w_o': _L1_attn_in['w_o'], 'L1_ffn_wg': _L1_ffn_in['wg'], 'L1_ffn_w1': _L1_ffn_in['w1'], 'L1_ffn_b1': _L1_ffn_in['b1'], 'L1_ffn_w2': _L1_ffn_in['w2'], 'L1_ffn_b2': _L1_ffn_in['b2']}
    _x0 = _d['L0_attn_x']
    _d['L0_attn_x'] = jax.random.normal(jax.random.fold_in(jax.random.key(seed), 1), (8, 1024, 256), dtype=_x0.dtype)
    del _x0
    return _d

def reference(L0_attn_x, L0_attn_A, L0_attn_Bm, L0_attn_Cm, L0_attn_Dm, L0_attn_ln_w, L0_attn_ln_b, L0_attn_W_out, L0_attn_b_out, L0_ffn_router_weight, L0_ffn_correction_bias, L0_ffn_w_gate, L0_ffn_w_up, L0_ffn_w_down, L0_ffn_sw_gate, L0_ffn_sw_up, L0_ffn_sw_down, L1_attn_w_qkv, L1_attn_w_o, L1_ffn_wg, L1_ffn_w1, L1_ffn_b1, L1_ffn_w2, L1_ffn_b2):

    def _L0_attn_ref(x, A, Bm, Cm, Dm, ln_w, ln_b, W_out, b_out):
        import jax, jax.numpy as jnp
        import numpy as np
        B_, S_, D_, N_ = (4, 512, 256, 16)

        def _layernorm(y, w, b, eps=1e-05):
            mu = jnp.mean(y, axis=-1, keepdims=True)
            var = jnp.mean((y - mu) ** 2, axis=-1, keepdims=True)
            return (y - mu) * jax.lax.rsqrt(var + eps) * w + b
        bsz = x.shape[0]
        h0 = jnp.zeros((bsz, A.shape[0], A.shape[1]), dtype=x.dtype)

        def step(h, x_t):
            h = jnp.einsum('dnm,bdm->bdn', A, h) + Bm[None] * x_t[..., None]
            y_t = jnp.einsum('dn,bdn->bd', Cm, h) + Dm * x_t
            return (h, y_t)
        _, y = jax.lax.scan(step, h0, jnp.swapaxes(x, 0, 1))
        y = jnp.swapaxes(y, 0, 1)
        y = _layernorm(y, ln_w, ln_b)
        y = jax.nn.gelu(y, approximate=False)
        y = y @ W_out.T + b_out
        return x + y

    def _L0_ffn_ref(hidden_states, router_weight, correction_bias, w_gate, w_up, w_down, sw_gate, sw_up, sw_down):
        import jax, jax.numpy as jnp
        import numpy as np
        B, S, H = (2, 1024, 256)
        I = 128
        E = 8
        TOPK = 2
        NGROUP = 2
        TOPK_GROUP = 1
        ROUTED_SCALE = 1.0

        def _silu(x):
            return x * jax.nn.sigmoid(x)
        b, s, h = hidden_states.shape
        x = hidden_states.reshape(-1, h)
        logits = x @ router_weight.T
        scores = jax.nn.sigmoid(logits)
        scores_for_choice = scores + correction_bias[None, :]
        e_per_g = E // NGROUP
        group_scores = jax.lax.top_k(scores_for_choice.reshape(-1, NGROUP, e_per_g), 2)[0].sum(-1)
        group_idx = jax.lax.top_k(group_scores, TOPK_GROUP)[1]
        group_mask = jax.nn.one_hot(group_idx, NGROUP, dtype=scores.dtype).sum(1)
        score_mask = jnp.repeat(group_mask, e_per_g, axis=1)
        masked = jnp.where(score_mask > 0, scores_for_choice, 0.0)
        topk_idx = jax.lax.top_k(masked, TOPK)[1]
        topk_w = jnp.take_along_axis(scores, topk_idx, axis=1)
        topk_w = topk_w / (topk_w.sum(-1, keepdims=True) + 1e-20)
        topk_w = topk_w * ROUTED_SCALE
        comb = (jax.nn.one_hot(topk_idx, E, dtype=x.dtype) * topk_w[..., None]).sum(1)
        g = jnp.einsum('th,ehi->tei', x, w_gate)
        u = jnp.einsum('th,ehi->tei', x, w_up)
        y = jnp.einsum('tei,eih->teh', _silu(g) * u, w_down)
        routed = jnp.einsum('teh,te->th', y, comb).reshape(b, s, h)
        shared = _silu(hidden_states @ sw_gate) * (hidden_states @ sw_up) @ sw_down
        return routed + shared

    def _L1_attn_ref(x, w_qkv, w_o):
        import jax, jax.numpy as jnp
        import numpy as np
        N_HEADS = 1
        LATENT_DIM = 256
        SCALE = 1.0 / float(np.sqrt(LATENT_DIM * N_HEADS))
        B, S, _ = x.shape
        qkv = jnp.einsum('bsd,fd->bsf', x, w_qkv)
        qkv = qkv.reshape(B, S, N_HEADS, 3 * LATENT_DIM).transpose(0, 2, 1, 3)
        q, k, v = jnp.split(qkv, 3, axis=-1)
        attn_logits = jnp.einsum('bhqd,bhkd->bhqk', q, k) * SCALE
        attention = jax.nn.softmax(attn_logits, axis=1)
        values = jnp.einsum('bhqk,bhkd->bhqd', attention, v)
        values = values.transpose(0, 2, 1, 3).reshape(B, S, N_HEADS * LATENT_DIM)
        return jnp.einsum('bsf,of->bso', values, w_o)

    def _L1_ffn_ref(x, wg, w1, b1, w2, b2):
        import jax, jax.numpy as jnp
        import numpy as np
        E = 8
        K = 2
        CAP_FACTOR = 1.0
        B, S, M = x.shape
        N = B * S
        capacity = int(CAP_FACTOR * K * N // E)
        xt = x.reshape(N, M)
        logits = xt @ wg
        scores = jax.nn.softmax(logits, axis=-1)
        topv, topi = jax.lax.top_k(scores, K)
        topv = topv / jnp.sum(topv, axis=-1, keepdims=True)
        masks = jax.nn.one_hot(topi.T, E, dtype=jnp.int32)
        flat = masks.reshape(K * N, E)
        locs = jnp.cumsum(flat, axis=0) - 1
        pos = jnp.sum(locs * flat, axis=-1).reshape(K, N).T
        valid = pos < capacity
        gate = topv * valid.astype(topv.dtype)
        pos_c = jnp.where(valid, pos, 0)
        xk = xt[:, None, :] * valid[..., None].astype(xt.dtype)
        disp = jnp.zeros((E, capacity, M), xt.dtype)
        disp = disp.at[topi, pos_c].add(xk)
        h = jax.nn.relu(jnp.einsum('ecm,emh->ech', disp, w1) + b1[:, None, :])
        y = jnp.einsum('ech,ehm->ecm', h, w2) + b2[:, None, :]
        out = jnp.sum(gate[..., None] * y[topi, pos_c], axis=1)
        return out.reshape(B, S, M)
    x = L0_attn_x
    xn = _layernorm(x, axis=-1)
    x = x + _L0_attn_ref(xn, L0_attn_A, L0_attn_Bm, L0_attn_Cm, L0_attn_Dm, L0_attn_ln_w, L0_attn_ln_b, L0_attn_W_out, L0_attn_b_out) + _L0_ffn_ref(xn, L0_ffn_router_weight, L0_ffn_correction_bias, L0_ffn_w_gate, L0_ffn_w_up, L0_ffn_w_down, L0_ffn_sw_gate, L0_ffn_sw_up, L0_ffn_sw_down)
    xn = _layernorm(x, axis=-1)
    x = x + _L1_attn_ref(xn, L1_attn_w_qkv, L1_attn_w_o) + _L1_ffn_ref(xn, L1_ffn_wg, L1_ffn_w1, L1_ffn_b1, L1_ffn_w2, L1_ffn_b2)
    return x

_drawn_inputs = setup_inputs


def setup_inputs(seed=0):
    import zlib

    import numpy as np

    out = dict(_drawn_inputs(seed))
    spreads = {'L0_attn_ln_w': (1.0, 0.2),
     'L0_attn_ln_b': (0.0, 0.1),
     'L0_attn_b_out': (0.0, 0.1),
     'L1_ffn_b1': (0.0, 0.8),
     'L1_ffn_b2': (0.0, 0.8)}
    factors = {'L0_ffn_router_weight': 3.95,
     'L0_ffn_correction_bias': 8.0,
     'L0_ffn_w_gate': 3.033,
     'L0_ffn_w_up': 2.825,
     'L0_ffn_w_down': 2.876,
     'L1_ffn_wg': 8.0,
     'L1_ffn_w1': 8.0,
     'L1_ffn_w2': 8.0}
    for name, (base, spread) in spreads.items():
        noise = np.random.default_rng([zlib.crc32(name.encode()), seed]).standard_normal(out[name].shape)
        drawn = base * np.exp(spread * noise) if base else spread * noise
        out[name] = jnp.asarray(drawn.astype(out[name].dtype))
    for name, factor in factors.items():
        out[name] = (out[name] * factor).astype(out[name].dtype)
    return out
```

```python
import concourse.bass as bass
from concourse import mybir
from contextlib import ExitStack


class Steps:

    def __init__(self, eng, sem):
        self.eng, self.sem, self.n, self.trip, self.per, self.base, self.first = eng, sem, 0, None, 0, 0, 0

    def mark(self, ins):
        ins.then_inc(self.sem, 1)
        self.n += 1

    def value(self):
        return self.n if self.trip is None else self.trip * self.per + (self.n - self.first * self.per)

    def settle(self):
        self.eng.wait_ge(self.sem, self.value())

    def run(self, ins):
        self.mark(ins)
        self.settle()

    def enter(self, trip, per, first=0):
        self.trip, self.per, self.base, self.first = trip, per, self.n, first

    def leave(self, trips):
        assert self.n == self.base + self.per, (self.n, self.base, self.per)
        self.n, self.trip = self.base + self.per * trips, None


def bass_ssm_moe_then_attention_moe(
    nc, x_in, A_in, Bm_in, Cm_in, Dm_in, lnw_in, lnb_in, Wout_in, bout_in, rw_in, cb_in, wg_in, wu_in,
    wd_in, swg_in, swu_in, swd_in, wqkv_in, wo_in, wgate_in, w1_in, b1_in, w2_in, b2_in, out,
):
    f32, f32r, bf16 = mybir.dt.float32, mybir.dt.float32r, mybir.dt.bfloat16
    u32, i32 = mybir.dt.uint32, mybir.dt.int32
    ALU, ACT, AX = mybir.AluOpType, mybir.ActivationFunctionType, mybir.AxisListType
    ds = bass.ds

    P = 128
    NB, S, D = x_in.shape
    TB = S // P
    NT = NB * TB
    N = NB * S
    ST = A_in.shape[1]
    CG = P // ST
    NG = D // CG
    DK = D // P
    E, _, I = wg_in.shape
    H = w1_in.shape[2]
    HK = H // P
    EPS = 1e-5
    ROW = D + 2
    Q0 = 2 * NT + E
    CAP = 2 * N // E
    CT = CAP // P
    TRASH = Q0 * P
    BIG = 3e38
    TR = 4

    x_v = x_in.rearrange("b (t p) d -> b p t d", p=P)
    x_h = x_in.rearrange("b (u t p) d -> (b u) p t d", p=P, t=4)
    o_h = out.rearrange("b (u t p) d -> (b u) p t d", p=P, t=4)
    w1_v = w1_in.rearrange("e (k p) h -> e p k h", p=P)
    w2_v = w2_in.rearrange("e (k p) d -> e p k d", p=P)
    kpad = nc.dram_tensor("conv_kernels", [D, 2 * P], f32).ap()
    disp = nc.dram_tensor("dispatched", [TRASH + 2 * N, ROW], f32).ap()
    yexp = nc.dram_tensor("expert_rows", [2 * N + Q0 * P, D], f32).ap()

    y_h = yexp[0:2 * N, :].rearrange("(h t p k) d -> h p t k d", p=P, t=4, k=2)
    disp1 = disp[0:E * CAP, :].rearrange("(n t p) c -> n p t c", p=P, t=4)
    NBLK = E * CT // 4

    ctx = ExitStack()
    with ctx:
        def sb(name, shape, dt=f32, c=ctx):
            return c.enter_context(nc.sbuf_tensor(name, shape, dt))

        def pb(name, shape, dt=f32, c=ctx):
            return c.enter_context(nc.psum_tensor(name, shape, dt))

        sems = {}

        def sem(name):
            if name not in sems:
                sems[name] = ctx.enter_context(nc.semaphore(name))
            return sems[name]

        ident = sb("ident", [P, P])
        flip = sb("flip", [P, P])
        tri = sb("tri", [P, P], bf16)
        ones_b = sb("ones_b", [P, P], bf16)
        mask8 = sb("mask8", [P, CG])
        warm = sb("warm", [P, 1])
        half_neg = sb("half_neg", [P, TB])
        zeros = sb("zeros", [P, 2 * ROW])
        part = sb("part", [P, 1])
        w8 = sb("w8", [P, E])
        iota8 = sb("iota8", [P, E])
        cb = sb("cb", [P, E])
        rw = sb("rw", [P, DK, E])
        cols = sb("cols", [P, 16])
        gates = sb("gates", [P, NT, 2])
        slot_u = sb("slot_u", [P, NT, 2], u32)
        tile_e = sb("tile_e", [1, Q0], i32)
        ef = sb("ef", [P, Q0])
        vq = sb("vq", [P, Q0])
        tq = sb("tq", [P, Q0])
        mv = sb("mv", [P, 2, TB, 2])
        bst = sb("bst", [P, 2, TB, 6])
        vare = sb("vare", [P, 2, TB])
        rstd = sb("rstd", [P, 2, TB])

        cB = ExitStack()
        ub = sb("ub", [P, NG, 2 * P], f32, cB)
        vb = sb("vb", [P, NG, 2 * P], f32, cB)
        a_in = vb[:, :, 0:ST]
        pt = ub[:, :, P:2 * P]
        gt = ub[:, :, 0:NT]
        gm = ub[:, :, NT:2 * NT].rearrange("p (r c) t -> p r t c", c=CG)
        kev = vb[0:CG, :, 0:P]
        cB.close()
        yb = sb("yb", [P, NT, D])
        rdiff = sb("rdiff", [P, NT])
        valid1 = sb("valid1", [P, NT, 2])
        gates1 = sb("gates1", [P, NT, 2])
        vq1 = sb("vq1", [P, E * CT])
        tq1 = sb("tq1", [P, E * CT])
        idx = sb("idx", [P, 4])
        eidx = sb("eidx", [P, 2, 4, 1], u32)
        idf = sb("idf", [P, 2, 4])
        idxu = sb("idxu", [P, 4, 1], u32)
        cX = ExitStack()
        xn = sb("xn", [P, NT, ROW], f32, cX)
        sgu = sb("sgu", [P, DK, 2 * I], f32, cX)
        sdn = sb("sdn", [P, D], f32, cX)
        bo = sb("bo", [P, D], f32, cX)
        cW = ExitStack()
        xl = sb("xl", [P, 2, TB, D], f32, cW)
        cW.close()
        cW = ExitStack()
        q8 = sb("q8", [P, Q0, E], f32, cW)
        cW.close()
        cW = ExitStack()
        wgu = sb("wgu", [P, E * DK, 2 * I], f32, cW)

        cW.close()
        cE1 = ExitStack()
        yl = sb("yl", [P, 2, 4, 2, D], f32, cE1)

        cS = ExitStack()
        vv = sb("vv", [P, NG, P], f32, cS)
        bcg = sb("bcg", [2 * NG, P], f32, cS)
        bc = sb("bc", [P, 2 * NG], f32, cS)
        bbd = sb("bbd", [P, NG, CG], f32, cS)
        dcg = sb("dcg", [CG, NG], f32, cS)
        cR = ExitStack()
        nst = sb("nst", [P, 2, TB, D], f32, cR)
        xt = sb("xt", [P, 2, 2, DK, P], f32, cR)
        cR.close()
        hs = sb("hs", [P, NG, NB, TB], f32, cS)
        cQ = ExitStack()
        rt = [sb(f"rt{i}", [P, NT, E], f32, cQ) for i in range(7)]
        mb = sb("mb", [P, NT, E], bf16, cQ)
        r1 = [sb(f"r1_{i}", [P, NT, 2], f32, cQ) for i in range(6)]
        iq = sb("iq", [P, Q0], f32, cQ)
        iq128 = sb("iq128", [P, Q0], f32, cQ)
        trq = sb("trq", [P, Q0], f32, cQ)
        nvq = sb("nvq", [P, Q0], f32, cQ)
        i64 = sb("i64", [P, NT], f32, cQ)
        se = [sb(f"se{i}", [P, E], f32, cQ) for i in range(6)]
        cQ.close()
        th = sb("th", [P, TR, CG, P], f32, cS)
        vst = sb("vst", [P, 2, P], f32, cS)
        hb = sb("hb", [P, 2, CG, NT], f32, cS)
        cS.close()

        woT = sb("woT", [P, DK, D], f32, cE1)
        wvT = sb("wvT", [P, DK, D], f32, cE1)
        waT = sb("waT", [P, DK, D], f32, cE1)
        cM = ExitStack()
        wdn = sb("wdn", [P, E, D], f32, cM)
        er = sb("er", [P, 2, 4, ROW], f32, cM)
        eT = sb("eT", [P, 2, DK, P], f32, cM)
        esg = sb("esg", [P, 2, I], f32, cM)
        eh = sb("eh", [P, 2, I], f32, cM)
        ehT = sb("ehT", [P, 2, P], f32, cM)
        ey = sb("ey", [P, 2, 4, D], f32, cM)
        wraw = sb("wraw", [P, 3, DK, D], f32, cM)
        cM.close()

        cE = ExitStack()
        xg = sb("xg", [P, 4, D], f32, cE)
        xs4 = sb("xs4", [P, 4, D], f32, cE)
        z4 = sb("z4", [P, 4, D], f32, cE)
        n4 = sb("n4", [P, 4, D], f32, cE)
        pair = sb("pair", [P, 2, DK, 4 * P], f32, cE)
        xT4, gT4 = pair[:, 0, :, :], pair[:, 1, :, :]
        vrep = pair[:, :, :, :].rearrange("p a k c -> p (a k c)").rearrange("p (k b m) -> p k b m", k=DK, b=NB)
        sl4 = sb("sl4", [P, 4 * P], f32, cE)
        hT4 = sb("hT4", [P, 4 * P], f32, cE)
        nT = sb("nT", [P, 2, DK, 2 * P], f32, cE)
        wg1 = sb("wg1", [P, DK, E], f32, cE)
        xsum = sb("xsum", [P, DK, NB, TB // 2], f32, cE)
        xtot = sb("xtot", [P, DK, NB], f32, cE)
        val = sb("val", [P, DK, NB], f32, cE)
        est = sb("est", [P, 4, 6], f32, cE)
        emv = sb("emv", [P, 4, 2], f32, cE)
        evar = sb("evar", [P, 2, 4], f32, cE)
        erstd = sb("erstd", [P, 2, 4], f32, cE)
        lg1 = sb("lg1", [P, TB, E], f32, cE)
        q1 = [sb(f"q1_{i}", [P, TB, E], f32, cE) for i in range(9)]
        k1 = [sb(f"k1_{i}", [P, TB], f32, cE) for i in range(8)]
        mb1 = sb("mb1", [P, 2, TB, E], bf16, cE)
        oh1s = sb("oh1s", [P, NT, E], f32, cE)
        key1s = sb("key1s", [P, NT], f32, cE)
        pos1s = sb("pos1s", [P, NT], f32, cE)
        carry = sb("carry", [P, 2, E], f32, cE)
        one64 = sb("one64", [P, E * TB], f32, cE)
        slot1 = sb("slot1", [P, NT, 2], u32, cE)
        f64 = [sb(f"f64_{i}", [P, NT], f32, cE) for i in range(3)]
        g64 = z4[:, :, :].rearrange("p a d -> p (a d)")[:, 0:NT * E].rearrange("p (t e) -> p t e", e=E)
        t128 = sb("t128", [P, E, CT], f32, cE)
        c8 = sb("c8", [P, E], f32, cE)
        cE.close()
        cE1.close()
        cX.close()

        cF = ExitStack()
        hTh = sb("hTh", [P, HK, 4 * P], f32r, cF)
        hTl = sb("hTl", [P, HK, 4 * P], f32r, cF)
        hf = sb("hf", [P, 2, 4 * P], f32, cF)
        w1h = sb("w1h", [P, 2, DK, H], f32r, cF)
        w1l = sb("w1l", [P, 2, DK, H], f32r, cF)
        w2h = sb("w2h", [P, 2, HK, D], f32r, cF)
        w2l = sb("w2l", [P, 2, HK, D], f32r, cF)
        wr = sb("wr", [P, HK * D], f32, cF)
        fr = sb("fr", [P, 2, 4, ROW], f32, cF)
        fTh = sb("fTh", [P, DK, 4 * P], f32r, cF)
        fTl = sb("fTl", [P, DK, 4 * P], f32r, cF)
        fy = sb("fy", [P, 4, D], f32, cF)
        b1c = sb("b1c", [P, E, HK], f32, cF)
        b2r = sb("b2r", [P, 2, D], f32, cF)
        cF.close()
        cO = ExitStack()
        ol = sb("ol", [P, 2, 4, 2, D], f32, cO)
        oo = sb("oo", [P, 2, 4, D], f32, cO)
        cO.close()

        bank = [pb(f"bank{i}", [P, 512]) for i in range(8)]

        def view(i, pat, **k):
            return bank[i][:, :].rearrange(pat, **k)

        LV = 7
        chunks = []
        for lv in range(LV):
            gr = 512 // ((1 << lv) + P)
            chunks += [(lv, g, min(gr, NG - g)) for g in range(0, NG, gr)]

        def level(lv):
            return [(n, g, gr) for n, (l, g, gr) in enumerate(chunks) if l == lv]

        def before(n):
            lv, g, gr = chunks[n]
            own = [i for i, g0, gr0 in level(lv - 1) if g0 < g + gr] if lv else []
            return max(own + [n - 2, -1]) + 1

        plan = [("batch", 0), ("batch", 1)]
        for b in range(2, NB - 1):
            plan += [("level", b - 2), ("batch", b)]
        plan += [("batch", NB - 1), ("level", LV - 2), ("level", LV - 1)]

        block = ctx.enter_context(nc.Block())
        disp_fill = disp[0:TRASH, :].rearrange("(a p) c -> p a c", p=P)

        @block.sync
        def _(sp):
            sp.dma_start(bcg[0:NG, :], Bm_in.rearrange("(g l) n -> g (l n)", l=CG)).then_inc(sem("state_in"), 16)
            sp.dma_start(bcg[NG:2 * NG, :], Cm_in.rearrange("(g l) n -> g (l n)", l=CG)).then_inc(sem("state_in"), 16)
            sp.dma_start(cb[:, :], cb_in.partition_broadcast(P)).then_inc(sem("cb_in"), 16)
            with nc.allow_non_contiguous_dma(reason="small"):
                for k in range(DK):
                    sp.dma_start(rw[:, k, :], rw_in[:, k * P:(k + 1) * P].rearrange("e p -> p e")).then_inc(sem("rw_in"), 16)
                for j, v in enumerate((lnw_in, lnb_in)):
                    sp.dma_start(cols[:, 2 * j:2 * j + 2], v.rearrange("(k p) -> p k", p=P)).then_inc(sem("cols_in"), 16)
                with sp.Fori(0, NB // 2) as t:
                    for r in range(2):
                        sp.wait_ge(sem(f"x_free{r}"), t + 1)
                        sp.dma_start(xl[:, r, :, :], x_v[ds(2 * t + r, 1)].rearrange("o p t d -> p (o t) d")).then_inc(sem(f"x_in{r}"), 16)
                sp.dma_start(dcg[:, :], Dm_in.rearrange("(g l) -> l g", l=CG)).then_inc(sem("dcg_in"), 16)
                for k, wd in ((0, swg_in), (1, swu_in)):
                    sp.dma_start(sgu[:, :, k * I:(k + 1) * I], wd.rearrange("(k p) i -> p k i", p=P)).then_inc(sem("shared_in"), 16)
                sp.dma_start(sdn[:, :], swd_in).then_inc(sem("shared_in"), 16)
                sp.dma_start(bo[:, :], bout_in.partition_broadcast(P)).then_inc(sem("shared_in"), 16)
                sp.wait_ge(sem("zeros"), 1)
                with sp.Fori(0, Q0 // 2) as j:
                    sp.dma_start(disp_fill[:, ds(2 * j, 2), :], zeros[:, :].rearrange("p (a c) -> p a c", a=2)).then_inc(sem("filled0"), 16)
                sp.dma_start(kpad.rearrange("(a p) c -> p a c", p=P), zeros[:, 0:4 * P].rearrange("p (a c) -> p a c", a=2)).then_inc(sem("kpad_zero"), 16)
                sp.wait_ge(sem("kpad_zero"), 16)
                sp.wait_ge(sem("kernels"), 1)
                sp.dma_start(kpad[:, 0:P].rearrange("(g l) j -> l g j", l=CG), kev[:, :, :]).then_inc(sem("kpad_in"), 16)
                sp.wait_ge(sem("kpad_in"), 16)
                sp.wait_ge(sem("routed0"), 2)
                for k, wd in ((0, wg_in), (1, wu_in)):
                    sp.dma_start(wgu[:, :, k * I:(k + 1) * I], wd.rearrange("e (k p) i -> p (e k) i", p=P)).then_inc(sem("wgu_in"), 16)
                toep = bass.AP(kpad.tensor, 0, [[CG * 2 * P, NG], [1, P], [2 * P, CG], [1, P]])
                for r in range(TR):
                    sp.dma_start(th[:, r, :, :], toep[r]).then_inc(sem(f"th_in{r}"), 16)
                with sp.Fori(1, NG // TR) as t:
                    for r in range(TR):
                        sp.wait_ge(sem("y_ps"), t * TR + (r - TR + 1))
                        sp.dma_start(th[:, r, :, :], toep[ds(t * TR + r, 1)].rearrange("o s l i -> s (o l) i")).then_inc(sem(f"th_in{r}"), 16)
                sp.wait_ge(sem("y_ps"), NG)
                for j, w in enumerate((Wout_in, wqkv_in[2 * D:3 * D, :], wo_in)):
                    sp.dma_start(wraw[:, j, :, :], w.rearrange("(k p) d -> p k d", p=P)).then_inc(sem("wraw_in"), 16)
                sp.dma_start(wdn[:, :, :], wd_in.rearrange("e i d -> i e d")).then_inc(sem("wdn_in"), 16)
                sp.wait_ge(sem("scattered0"), 1)
                disp0 = disp[0:TRASH, :].rearrange("(u a p) c -> u p a c", p=P, a=4)
                for r in range(2):
                    sp.dma_start(er[:, r, :, :], disp0[r]).then_inc(sem(f"er_in{r}"), 16)
                with sp.Fori(1, Q0 // 8) as t:
                    for r in range(2):
                        sp.wait_ge(sem("eT_ps"), t * 8 + (4 * r - 4))
                        sp.wait_ge(sem("e_idx"), t * 2 + (r - 1))
                        sp.dma_start(er[:, r, :, :], disp0[ds(t * 2 + r, 1)].rearrange("o p a c -> p (o a) c")).then_inc(sem(f"er_in{r}"), 16)
                sp.wait_ge(sem("e_stored"), 1)
                sp.dma_start(wg1[:, :, :], wgate_in.rearrange("(k p) e -> p k e", p=P)).then_inc(sem("wg1_in"), 16)

                def end_load(t, r):
                    if not isinstance(t, int) or r:
                        sp.wait_ge(sem("x1_sum"), t * 2 + r)
                    sp.dma_start(xg[:, :, :], x_h[ds(t * 2 + r, 1)].rearrange("o p t d -> p (o t) d")).then_inc(sem("xg_in"), 16)
                    sp.dma_start(yl[:, r, :, :, :], y_h[ds(t * 2 + r, 1)].rearrange("o p t k d -> p (o t) k d")).then_inc(sem(f"yl_in{r}"), 16)

                for r in range(2):
                    end_load(0, r)
                with sp.Fori(1, NB) as t:
                    for r in range(2):
                        end_load(t, r)
                sp.wait_ge(sem("dispatch1_done"), 1)
                sp.wait_ge(sem("att_add"), NB)
                sp.dma_start(b1c[:, :, :], b1_in.rearrange("e (k p) -> p e k", p=P)).then_inc(sem("b1_in"), 16)

                def rows(n, r, first):
                    if not first:
                        sp.wait_ge(sem("fT_ps"), n - 1)
                        sp.wait_ge(sem("f_idx"), n - 1)
                    sp.dma_start(fr[:, r, :, :], disp1[ds(n, 1)].rearrange("o p t c -> p (o t) c")).then_inc(sem(f"fr_in{r}"), 16)

                rows(0, 0, True)
                rows(1, 1, True)
                with sp.Fori(1, NBLK // 2) as n:
                    for r in range(2):
                        rows(n * 2 + r, r, False)
                sp.wait_ge(sem("f_stored"), 1)

                def out_load(t, r):
                    sp.dma_start(ol[:, r, :, :, :], y_h[ds(t * 2 + r, 1)].rearrange("o p t k d -> p (o t) k d")).then_inc(sem(f"ol_in{r}"), 16)

                for r in range(2):
                    out_load(0, r)
                with sp.Fori(1, NB) as t:
                    for r in range(2):
                        sp.wait_ge(sem("oo"), t * 2 + (r - 1))
                        out_load(t, r)

        @block.gpsimd
        def _(pool):
            for j, (ap, v) in enumerate(((ident, 0.0), (flip, 0.0), (tri, 1.0), (ones_b, 1.0), (mask8, 1.0), (half_neg, -0.5), (zeros, 0.0))):
                last = nc.gpsimd.memset(ap[:, :], v)
                if ap is zeros:
                    last.then_inc(sem("zeros"), 1)
                else:
                    last.then_inc(sem("consts0"), 1)
            pool.wait_ge(sem("consts0"), 6)
            nc.gpsimd.affine_select(out=ident[:, :], in_=ident[:, :], compare_op=ALU.not_equal, fill=1.0, base=0,
                                    pattern=[[-1, P]], channel_multiplier=1).then_inc(sem("consts"), 1)
            nc.gpsimd.affine_select(out=flip[:, :], in_=flip[:, :], compare_op=ALU.not_equal, fill=1.0, base=1 - P,
                                    pattern=[[1, P]], channel_multiplier=1).then_inc(sem("consts"), 1)
            nc.gpsimd.affine_select(out=tri[:, :], in_=tri[:, :], compare_op=ALU.is_gt, fill=0.0, base=0,
                                    pattern=[[1, P]], channel_multiplier=-1).then_inc(sem("consts"), 1)
            nc.gpsimd.affine_select(out=mask8[:, :], in_=mask8[:, :], compare_op=ALU.is_ge, fill=0.0, base=0,
                                    pattern=[[-ST, CG]], channel_multiplier=1).then_inc(sem("consts"), 1)
            pool.wait_ge(sem("consts"), 4)
            nc.gpsimd.affine_select(out=mask8[:, :], in_=mask8[:, :], compare_op=ALU.is_gt, fill=0.0, base=ST,
                                    pattern=[[ST, CG]], channel_multiplier=-1).then_inc(sem("consts"), 1)
            io = dict(allow_small_or_imprecise_dtypes=True)
            nc.gpsimd.iota(part[:, :], [[0, 1]], base=0, channel_multiplier=1, **io).then_inc(sem("consts"), 1)
            nc.gpsimd.iota(iota8[:, :], [[1, E]], base=0, channel_multiplier=0, **io).then_inc(sem("consts"), 1)
            nc.gpsimd.iota(w8[:, :], [[-1, E]], base=E, channel_multiplier=0, **io).then_inc(sem("consts"), 1)
            nc.gpsimd.iota(xn[:, :, D:D + 1], [[2 * P, NT], [0, 1]], base=0, channel_multiplier=2, **io).then_inc(sem("consts"), 1)
            for b in range(NB):
                pool.wait_ge(sem("ln0_var"), b + 1)
                nc.gpsimd.tensor_tensor(rstd[:, b % 2, :], vare[:, b % 2, :], half_neg[:, :], ALU.pow).then_inc(sem("ln0_rstd"), 1)
            pool.wait_ge(sem("k_out"), NG // 4)
            pool.wait_ge(sem("dcg_in"), 16)
            nc.gpsimd.tensor_tensor(kev[:, :, P - 1], kev[:, :, P - 1], dcg[:, :], ALU.add).then_inc(sem("kernels"), 1)
            pool.wait_ge(sem("xn_done"), NB)
            nc.gpsimd.memset(hs[:, :, :, 0], 0.0).then_inc(sem("states"), 1)
            nc.gpsimd.iota(iq[:, :], [[1, Q0]], base=0, channel_multiplier=0, **io).then_inc(sem("iotas"), 1)
            nc.gpsimd.iota(iq128[:, :], [[P, Q0]], base=0, channel_multiplier=0, **io).then_inc(sem("iotas"), 1)
            nc.gpsimd.iota(trq[:, :], [[P, Q0]], base=2 * N, channel_multiplier=1, **io).then_inc(sem("iotas"), 1)
            nc.gpsimd.iota(i64[:, :], [[P, NT]], base=0, channel_multiplier=0, **io).then_inc(sem("iotas"), 1)
            pool.wait_ge(sem("routed0"), 1)
            pool.wait_ge(sem("xn_done"), NB)
            pool.wait_ge(sem("filled0"), 16 * (Q0 // 2))
            for i in range(NT):
                for k in range(2):
                    nc.gpsimd.indirect_dma_start(disp, bass.IndirectOffsetOnAxis(ap=slot_u[:, i, k:k + 1], axis=0),
                                                 xn[:, i, :], None).then_inc(sem("dispatched0"), 16)
            pool.wait_ge(sem("dispatched0"), 16 * 2 * NT)
            pool.sem_inc(sem("scattered0"), 1)

            with pool.Fori(0, Q0 // 8) as t:
                for r in range(2):
                    pool.wait_ge(sem("e_idxu"), t * 2 + (r + 1))
                    for a in range(4):
                        pool.wait_ge(sem("ey"), t * 8 + (4 * r + a + 1))
                        pool.sem_inc(sem("pool_passed"), 1)
                        nc.gpsimd.indirect_dma_start(yexp, bass.IndirectOffsetOnAxis(ap=eidx[:, r, a, :], axis=0), ey[:, r, a, :], None).then_inc(sem(f"e_out{r}"), 16)
            for r in range(2):
                pool.wait_ge(sem(f"e_out{r}"), 64 * (Q0 // 8))
            pool.sem_inc(sem("e_stored"), 1)

            nc.gpsimd.memset(one64[:, :], 1.0).then_inc(sem("consts1"), 1)
            nc.gpsimd.memset(carry[:, :, :], 0.0).then_inc(sem("consts1"), 1)
            nc.gpsimd.iota(f64[2][:, :], [[P, NT]], base=TRASH, channel_multiplier=1, **io).then_inc(sem("consts1"), 1)
            nc.gpsimd.iota(t128[:, :, :], [[0, E], [P, CT]], base=0, channel_multiplier=1, **io).then_inc(sem("consts1"), 1)
            nc.gpsimd.iota(tq1[:, :], [[P, E * CT]], base=2 * N, channel_multiplier=1, **io).then_inc(sem("consts1"), 1)
            nc.gpsimd.iota(ef[:, 0:E * CT], [[1, E], [0, CT]], base=0, channel_multiplier=0, **io).then_inc(sem("consts1"), 1)

            def pows(k, n):
                pool.wait_ge(sem(("z_var", "x1_var")[k]), n + 1)
                nc.gpsimd.tensor_tensor(erstd[:, k, :], evar[:, k, :], half_neg[:, 0:4], ALU.pow).then_inc(sem(("z_rstd", "x1_rstd")[k]), 1)

            def put1(b, half):
                pool.wait_ge(sem("slot1"), b + 1)
                for i in range(b * TB + half * 4, b * TB + half * 4 + 4):
                    nc.gpsimd.indirect_dma_start(disp, bass.IndirectOffsetOnAxis(ap=slot1[:, i, 0:1], axis=0),
                                                 xn[:, i, :], None).then_inc(sem("dispatched1"), 16)

            pows(0, 0)
            for n in range(2 * NB):
                pool.wait_ge(sem("xg_in"), 16 * (n + 1))
                nc.gpsimd.tensor_tensor(xg[:, :, :], xg[:, :, :], xn[:, 4 * n:4 * n + 4, 0:D], ALU.add).then_inc(sem("xg_sum"), 1)
                pool.wait_ge(sem("xg_sum"), 2 * n + 1)
                nc.gpsimd.tensor_tensor(xg[:, :, :], xg[:, :, :], bo[:, :].unsqueeze(1).broadcast_to([P, 4, D]), ALU.add).then_inc(sem("xg_sum"), 1)
                if n + 1 < 2 * NB:
                    pows(0, n + 1)
                pows(1, n)
                if n >= 4:
                    put1((n - 4) // 2, n % 2)
            for n in range(2 * NB, 2 * NB + 4):
                put1((n - 4) // 2, n % 2)
            pool.wait_ge(sem("slot1_second"), 1)
            for i in range(NT):
                nc.gpsimd.indirect_dma_start(disp, bass.IndirectOffsetOnAxis(ap=slot1[:, i, 1:2], axis=0),
                                             xn[:, i, :], None).then_inc(sem("dispatched1"), 16)
            pool.wait_ge(sem("dispatched1"), 16 * 2 * NT)
            pool.sem_inc(sem("dispatch1_done"), 1)

            def load_w(k, e, r):
                src = (w1_v, w2_v)[k][ds(e, 1)].rearrange("o p k h -> p (o k) h")
                pool.dma_start(wr[:, :].rearrange("p (k h) -> p k h", k=(DK, HK)[k]), src).then_inc(sem("wr_in"), 16)

            def split(k, e, r):
                hi, lo = ((w1h, w1l), (w2h, w2l))[k]
                pool.wait_ge(sem("wr_in"), e * 32 + 16 * (k + 1))
                pool.sem_inc(sem("pool_passed"), 1)
                fl = "p a b -> p (a b)"
                nc.gpsimd.tensor_copy(hi[:, r, :, :].rearrange(fl), wr[:, :]).then_inc(sem("w_split"), 1)
                pool.wait_ge(sem("w_split"), e * 4 + 2 * k + 1)
                nc.gpsimd.tensor_tensor(lo[:, r, :, :].rearrange(fl), wr[:, :], hi[:, r, :, :].rearrange(fl), ALU.subtract).then_inc(sem("w_split"), 1)
                pool.wait_ge(sem("w_split"), e * 4 + 2 * k + 2)
                pool.sem_inc(sem("pool_passed"), 1)

            def load_b(e, r):
                pool.dma_start(b2r[:, r, :], b2_in[ds(e, 1), :].rearrange("o d -> (o d)").partition_broadcast(P)).then_inc(sem("b2_in"), 16)

            def put2(n):
                pool.wait_ge(sem("fy"), n + 1)
                pool.sem_inc(sem("pool_passed"), 1)
                for j in range(4):
                    nc.gpsimd.indirect_dma_start(yexp, bass.IndirectOffsetOnAxis(ap=idxu[:, j, :], axis=0), fy[:, j, :], None).then_inc(sem("f_out"), 16)

            pool.wait_ge(sem("att_add"), NB)
            load_w(0, 0, 0)
            split(0, 0, 0)
            load_w(1, 0, 0)
            load_b(0, 0)
            split(1, 0, 0)

            def expert(e, r, last=False):
                put2(e * 4)
                if not last:
                    load_w(0, e + 1, 1 - r)
                    load_b(e + 1, 1 - r)
                put2(e * 4 + 1)
                if not last:
                    split(0, e + 1, 1 - r)
                    load_w(1, e + 1, 1 - r)
                put2(e * 4 + 2)
                if not last:
                    split(1, e + 1, 1 - r)
                put2(e * 4 + 3)

            with pool.Fori(0, E // 2 - 1) as t:
                for r in range(2):
                    expert(t * 2 + r, r)
            expert(E - 2, 0)
            expert(E - 1, 1, True)
            pool.wait_ge(sem("f_out"), 64 * NBLK)
            pool.sem_inc(sem("f_stored"), 1)

        @block.scalar
        def _(act):
            with nc.allow_non_contiguous_dma(reason="rows of a state matrix"):
                act.dma_start(a_in, A_in.rearrange("(g l) n m -> (l n) g m", l=CG)).then_inc(sem("state_in"), 16)
            act.wait_ge(sem("consts"), 9)
            for c in range(NG // 4):
                act.wait_ge(sem("at_ps"), c + 1)
                nc.scalar.activation(vb[:, 4 * c:4 * c + 4, P:], bank[3 + c % 2][:, :].rearrange("p (g m) -> p g m", g=4), ACT.Copy).then_inc(sem("at_bd"), 1)
            act.wait_ge(sem("v0"), 1)
            nc.scalar.activation(vb[:, :, P - 1:P], bank[7][:, 2 * NG:3 * NG].unsqueeze(2), ACT.Copy).then_inc(sem("v_first"), 1)

            def ln_batch(b):
                act.wait_ge(sem("ln0_rows"), b + 1)
                nc.scalar.activation(xn[:, b * TB:(b + 1) * TB, 0:D], nst[:, b % 2, :, :], ACT.Copy).then_inc(sem("xn_done"), 1)
                for h in range(TB // 2):
                    n = b * TB // 2 + h
                    act.wait_ge(sem("tp_ready"), n + 1)
                    if n >= 2:
                        act.wait_ge(sem("xt_used"), n - 1)
                    nc.scalar.activation(xt[:, h % 2, :, :, :], view(h % 2, "p (a c m) -> p a c m", a=2, c=DK), ACT.Copy).then_inc(sem("xt_ready"), 1)

            def store_level(lv):
                m = 1 << lv
                if lv == LV - 1:
                    act.wait_ge(sem("v_done"), level(lv)[0][0])
                    nc.scalar.activation(vv[:, :, m:], vb[:, :, m:P], ACT.Copy).then_inc(sem("v_half"), 1)
                to = vb if lv < LV - 1 else vv
                for n, g, gr in level(lv):
                    ps = bank[4 + 2 * (n % 2)][:, 0:gr * (m + P)].rearrange("p (g w) -> p g w", g=gr)
                    act.wait_ge(sem("v_ps"), n + 1)
                    nc.scalar.activation(to[:, g:g + gr, P - 2 * m:P - m], ps[:, :, 0:m], ACT.Copy)
                    nc.scalar.activation(vb[:, g:g + gr, P:], ps[:, :, m:], ACT.Copy).then_inc(sem("v_done"), 1)

            for what, i in plan:
                if what == "batch":
                    ln_batch(i)
                else:
                    store_level(i)
                if (what, i) == ("batch", NB - 1):
                    act.wait_ge(sem("logits0"), 1)
                    nc.scalar.activation(rt[0][:, :, :], view(2, "p (a c) -> p a c", c=E), ACT.Sigmoid).then_inc(sem("sig0"), 1)
            for c in range(NG // 4):
                act.wait_ge(sem("k_ps"), c + 1)
                nc.scalar.activation(kev[:, 4 * c:4 * c + 4, :], bank[3 + c % 2][0:CG, :].rearrange("p (g j) -> p g j", g=4), ACT.Copy).then_inc(sem("k_out"), 1)
            for c in range(NG // 4):
                act.wait_ge(sem("pt_ps"), c + 1)
                nc.scalar.activation(pt[:, 4 * c:4 * c + 4, :], bank[5 + c % 2][:, :].rearrange("p (g j) -> p g j", g=4), ACT.Copy).then_inc(sem("pt"), 1)
            for c in range(TB - 1):
                act.wait_ge(sem("step_ps"), c + 1)
                nc.scalar.activation(hs[:, :, :, c + 1], bank[5][:, 0:NG * NB].rearrange("p (g b) -> p g b", g=NG), ACT.Copy).then_inc(sem("states"), 1)
            act.wait_ge(sem("routed0"), 2)
            def out_pair(t):
                for r in range(2):
                    if not isinstance(t, int):
                        act.wait_ge(sem("y_ps"), t * 2 + (r - 1))
                        act.sem_inc(sem("act_passed"), 1)
                    nc.scalar.activation(vst[:, r:r + 1, :], vv[:, ds(t * 2 + r, 1), :], ACT.Copy).then_inc(sem("vst"), 1)
                for r in range(2):
                    act.wait_ge(sem("y_ps"), t * 2 + (r + 1))
                    act.sem_inc(sem("act_passed"), 1)
                    nc.scalar.activation(yb[:, :, ds(t * 2 * CG + r * CG, CG)], view(6 + r, "p (l i) -> p i l", l=CG), ACT.Copy).then_inc(sem("y_done"), 1)

            out_pair(0)
            with act.Fori(1, NG // 2) as t:
                out_pair(t)

            nc.scalar.activation(warm[:, :], part[:, :], ACT.Silu).then_inc(sem("warm"), 1)

            def expert0(q, r, parts=(0, 1, 2)):
                if 0 in parts:
                    act.wait_ge(sem("eT_ps"), q + 1)
                    if not isinstance(q, int) or q >= 2:
                        act.wait_ge(sem("eg_ps"), q - 1)
                    nc.scalar.activation(eT[:, r, :, :], bank[r][:, 0:DK * P].rearrange("p (k m) -> p k m", k=DK), ACT.Copy).then_inc(sem("eT"), 1)
                if 1 in parts and (not isinstance(q, int) or q >= 1):
                    act.wait_ge(sem("eg_ps"), q)
                    if not isinstance(q, int) or q >= 3:
                        act.wait_ge(sem("eh"), q - 2)
                    nc.scalar.activation(esg[:, 1 - r, :], bank[3 - r][:, 0:I], ACT.Silu).then_inc(sem("esg"), 1)
                if 2 in parts and (not isinstance(q, int) or q >= 2):
                    act.wait_ge(sem("ehT_ps"), q - 1)
                    if not isinstance(q, int) or q >= 4:
                        act.wait_ge(sem("ey_ps"), q - 3)
                    nc.scalar.activation(ehT[:, r, :], bank[4 + r][:, 0:P], ACT.Copy).then_inc(sem("ehT"), 1)

            for q in range(8):
                expert0(q, q % 2)
            with act.Fori(1, Q0 // 8) as t:
                for a in range(8):
                    expert0(t * 8 + a, a % 2)
            expert0(Q0, Q0 % 2, (1, 2))
            expert0(Q0 + 1, (Q0 + 1) % 2, (2,))

            def end_copy(n):
                if not isinstance(n, int) or n >= 1:
                    act.wait_ge(sem("xT_ps"), n)
                    act.wait_ge(sem("xs4"), n)
                act.sem_inc(sem("act_passed"), 1)
                nc.scalar.activation(xs4[:, :, :], xn[:, ds(n * 4, 4), 0:D], ACT.Copy).then_inc(sem("xs4"), 1)

            def end_xT(n):
                act.wait_ge(sem("xT_ps"), n + 1)
                if not isinstance(n, int) or n >= 1:
                    act.wait_ge(sem("gu4_ps"), n)
                for k in range(DK):
                    nc.scalar.activation(xT4[:, k, :], bank[k][:, :], ACT.Copy).then_inc(sem("xT4"), 1)

            def end_gelu(n):
                act.wait_ge(sem("zT_ps"), n + 1)
                if not isinstance(n, int) or n >= 1:
                    act.wait_ge(sem("o_ps"), n)
                for k in range(DK):
                    nc.scalar.activation(gT4[:, k, :], bank[k][:, :], ACT.Gelu, bias=cols[:, 2 + k:3 + k],
                                         scale=cols[:, k:k + 1]).then_inc(sem("gT4"), 1)

            def end_silu(n):
                act.wait_ge(sem("gu4_ps"), n + 1)
                if not isinstance(n, int) or n >= 1:
                    act.wait_ge(sem("hT4"), n)
                nc.scalar.activation(sl4[:, :], bank[2][:, :], ACT.Silu).then_inc(sem("sl4"), 1)

            def end_rows(n):
                act.wait_ge(sem("n4"), n + 1)
                act.sem_inc(sem("act_passed"), 1)
                nc.scalar.activation(xn[:, ds(n * 4, 4), 0:D], n4[:, :, :], ACT.Copy).then_inc(sem("xn1"), 1)

            def end_nT(n, b, r):
                for j in range(2):
                    act.wait_ge(sem("nT_ps"), n * 2 + (j + 1))
                    if not isinstance(n, int) or n >= 1:
                        act.wait_ge(sem("lg_ps"), n * 2 + (j - 1))
                        act.wait_ge(sem("nT"), n * 4)
                    act.sem_inc(sem("act_passed"), 1)
                    for k in range(DK):
                        nc.scalar.activation(nT[:, j, k, :], bank[6][:, k * 2 * P:(k + 1) * 2 * P], ACT.Copy,
                                             accum_out=xsum[:, k, ds(b, 1), 2 * r + j]).then_inc(sem("nT"), 1)

            def end_step(b, r, last=False):
                n = b * 2 + r
                if not last:
                    end_copy(n + 1)
                end_silu(n)
                if not last:
                    end_xT(n + 1)
                if not isinstance(n, int) or n >= 1:
                    end_nT(n - 1, b - (1 - r), 1 - r)
                if not last:
                    end_gelu(n + 1)
                end_rows(n)

            act.wait_ge(sem("cols_in"), 32)
            act.wait_ge(sem("ey_ps"), Q0)
            end_copy(0)
            end_xT(0)
            end_gelu(0)
            for r in range(2):
                end_step(0, r)
            with act.Fori(1, NB - 1) as b:
                for r in range(2):
                    end_step(b, r)
            for r in range(2):
                end_step(NB - 1, r, r == 1)
            end_nT(2 * NB - 1, NB - 1, 1)

            act.sem_inc(sem("hf"), 2)
            act.wait_ge(sem("b1_in"), 16)
            nc.scalar.activation(warm[:, :], part[:, :], ACT.Relu).then_inc(sem("warm"), 1)

            def high(n):
                act.wait_ge(sem("fT_ps"), n + 1)
                act.wait_ge(sem("h_ps"), n * HK)
                for k in range(DK):
                    nc.scalar.activation(fTh[:, k, :], bank[k][:, :], ACT.Copy).then_inc(sem("fTh"), 1)

            def hidden(e, n, j):
                m = n * HK + j
                act.wait_ge(sem("h_ps"), m + 1)
                act.wait_ge(sem("h_lo"), m + 1)
                act.sem_inc(sem("act_passed"), 1)
                nc.scalar.activation(hf[:, j % 2, :], bank[2 + j % 2][:, :], ACT.Relu, bias=b1c[:, ds(e, 1), j]).then_inc(sem("hf"), 1)

            act.wait_ge(sem("fT_ps"), 1)
            for k in range(DK):
                nc.scalar.activation(fTh[:, k, :], bank[k][:, :], ACT.Copy).then_inc(sem("fTh"), 1)

            def block2(e, jb, last=False):
                n = e * 4 + jb
                for j in range(HK):
                    hidden(e, n, j)
                if not last:
                    high(n + 1)

            with act.Fori(0, E - 1) as e:
                for jb in range(4):
                    block2(e, jb)
            for jb in range(4):
                block2(E - 1, jb, jb == 3)

            act.wait_ge(sem("sg_diff"), 1)
            nc.scalar.activation(gates1[:, :, 0], rdiff[:, :], ACT.Sigmoid, scale=-1.0).then_inc(sem("gates1"), 1)
            nc.scalar.activation(gates1[:, :, 1], rdiff[:, :], ACT.Sigmoid).then_inc(sem("gates1"), 1)

            def store(t, r):
                act.wait_ge(sem("oo"), t * 2 + (r + 1))
                act.dma_start(o_h[ds(t * 2 + r, 1)].rearrange("o p t d -> p (o t) d"), oo[:, r, :, :]).then_inc(sem(f"stored{r}"), 16)

            with act.Fori(0, NB) as t:
                for r in range(2):
                    store(t, r)
            for r in range(2):
                act.wait_ge(sem(f"stored{r}"), 16 * NB)

        @block.tensor
        def _(pe):
            pe.wait_ge(sem("consts"), 9)
            pe.wait_ge(sem("rw_in"), 16 * DK)
            NH2 = TB // 2

            def turn(b, h):
                n = b * NH2 + h
                if n >= 2:
                    pe.wait_ge(sem("xt_ready"), n - 1)
                if h == 0:
                    pe.wait_ge(sem("ln0_rows"), b + 1)
                for a in range(2):
                    for c in range(DK):
                        last = nc.tensor.transpose(bank[h % 2][:, (a * DK + c) * P:(a * DK + c + 1) * P],
                                                   nst[:, b % 2, 2 * h + a, c * P:(c + 1) * P], ident[:, :])
                last.then_inc(sem("tp_ready"), 1)

            def logit(b, h):
                pe.wait_ge(sem("xt_ready"), b * NH2 + h + 1)
                for a in range(2):
                    o = (b * TB + 2 * h + a) * E
                    for c in range(DK):
                        last = nc.tensor.matmul(bank[2][:, o:o + E], xt[:, h % 2, a, c, :], rw[:, c, :],
                                                start=(c == 0), stop=(c == DK - 1))
                last.then_inc(sem("xt_used"), 1)

            def batch(b):
                turn(b, 0)
                for h in range(NH2):
                    if h + 1 < NH2:
                        turn(b, h + 1)
                    logit(b, h)

            def double(lv):
                m = 1 << lv
                for n, g0, gr in level(lv):
                    w = m + P
                    if before(n):
                        pe.wait_ge(sem("u_done"), before(n))
                        pe.wait_ge(sem("v_done"), before(n))
                    for side, mat, cols_, done in ((0, vb, ub, "u_ps"), (1, ub, vb, "v_ps")):
                        wm = m if side == 0 and lv == LV - 1 else w
                        for i in range(gr):
                            last = nc.tensor.matmul(bank[3 + 2 * (n % 2) + side][:, i * w:i * w + wm], mat[:, g0 + i, P:],
                                                    cols_[:, g0 + i, P - m:P - m + wm], start=True, stop=True)
                        last.then_inc(sem(done), 1)

            pe.wait_ge(sem("state_in"), 48)
            nc.tensor.transpose(bank[7][:, 0:2 * NG], bcg[:, :], ident[0:2 * NG, 0:2 * NG]).then_inc(sem("bc_ps"), 1)
            pe.wait_ge(sem("a_bd"), 1)
            for c in range(NG // 4):
                if c >= 2:
                    pe.wait_ge(sem("at_bd"), c - 1)
                for g in range(4):
                    last = nc.tensor.transpose(bank[3 + c % 2][:, g * P:(g + 1) * P], ub[:, 4 * c + g, P:], ident[:, :])
                last.then_inc(sem("at_ps"), 1)
            pe.wait_ge(sem("bc"), 1)
            for g in range(NG):
                last = nc.tensor.matmul(bank[7][:, 2 * NG + g:2 * NG + g + 1], ub[:, g, P:], bc[:, NG + g:NG + g + 1], start=True, stop=True)
            last.then_inc(sem("v0"), 1)
            for what, i in plan:
                if what == "batch":
                    batch(i)
                    if i == NB - 1:
                        pe.wait_ge(sem("xt_used"), NB * NH2)
                        pe.sem_inc(sem("logits0"), 1)
                else:
                    if i == 0:
                        pe.wait_ge(sem("at_bd"), NG // 4)
                        pe.wait_ge(sem("v_first"), 1)
                    double(i)
            for side in "uv":
                pe.wait_ge(sem(side + "_done"), len(chunks))
            pe.wait_ge(sem("v_half"), 1)
            for c in range(NG // 4):
                if c >= 2:
                    pe.wait_ge(sem("k_out"), c - 1)
                for g in range(4):
                    gg = 4 * c + g
                    nc.tensor.matmul(bank[3 + c % 2][0:CG, (g + 1) * P - 1:(g + 1) * P], bbd[:, gg, :], bc[:, NG + gg:NG + gg + 1], start=True, stop=True)
                    last = nc.tensor.matmul(bank[3 + c % 2][0:CG, g * P:(g + 1) * P - 1], bbd[:, gg, :], vv[:, gg, 1:P], start=True, stop=True)
                last.then_inc(sem("k_ps"), 1)
            for c in range(NG // 4):
                if c >= 2:
                    pe.wait_ge(sem("pt"), c - 1)
                for g in range(4):
                    last = nc.tensor.transpose(bank[5 + c % 2][:, g * P:(g + 1) * P], ub[:, 4 * c + g, 0:P], ident[:, :])
                last.then_inc(sem("pt_ps"), 1)
            pe.wait_ge(sem("pt"), NG // 4)
            pe.wait_ge(sem("k_out"), NG // 4)
            pe.wait_ge(sem("xn_done"), NB)
            for g in range(NG):
                if g >= 4:
                    pe.wait_ge(sem("g_used"), g - 3)
                nc.tensor.matmul(bank[3 + g % 4][:, :].rearrange("p (t c) -> p t c", c=CG), pt[:, g, :], xn[:, :, g * CG:(g + 1) * CG],
                                 start=True, stop=True).then_inc(sem("g_ps"), 1)
            pe.wait_ge(sem("g_used"), NG)
            pe.wait_ge(sem("gt"), NG)
            for c in range(TB - 1):
                pe.wait_ge(sem("states"), c + 1)
                nc.tensor.matmul(bank[5][:, 0:NG * NB].rearrange("p (g b) -> p g b", g=NG), ident[:, :],
                                 gt.rearrange("p g (b t) -> p g b t", b=NB)[:, :, :, c], start=True, stop=False, skip_group_check=True)
                for g in range(NG):
                    last = nc.tensor.matmul(bank[5][:, g * NB:(g + 1) * NB], vb[:, g, P:], hs[:, g, :, c],
                                            start=False, stop=(g == NG - 1), skip_group_check=True)
                last.then_inc(sem("step_ps"), 1)
                if c == 1:
                    pe.wait_ge(sem("chosen0"), 1)
                    nc.tensor.matmul(bank[0][:, :], tri[:, :], mb[:, :, :].rearrange("p a e -> p (a e)"), start=True, stop=True)
                    nc.tensor.matmul(bank[1][:, :], ones_b[:, :], mb[:, :, :].rearrange("p a e -> p (a e)"), start=True, stop=True).then_inc(sem("ranks0"), 1)
            def out_pair(u, h2):
                t = u * 2 + h2
                for r in range(2):
                    pe.wait_ge(sem("vst"), t * 2 + (r + 1))
                    pe.wait_ge(sem("hb"), t * 2 + (r + 1))
                    if not isinstance(t, int) or t:
                        pe.wait_ge(sem("y_done"), t * 2 + (r - 1))
                    nc.tensor.matmul(bank[6 + r][:, :], vst[:, r, :], hb[:, r, :, :].rearrange("p l i -> p (l i)"),
                                     start=True, stop=False, skip_group_check=True)
                    pe.wait_ge(sem(f"th_in{2 * h2 + r}"), u * 16 + 16)
                    for l in range(CG):
                        last = nc.tensor.matmul(bank[6 + r][:, l * NT:(l + 1) * NT], th[:, 2 * h2 + r, l, :],
                                                xn[:, :, ds(t * 2 * CG + (r * CG + l), 1)].rearrange("p i o -> p (i o)"),
                                                start=False, stop=(l == CG - 1), skip_group_check=True)
                    last.then_inc(sem("y_ps"), 1)

            for h2 in range(2):
                out_pair(0, h2)
            with pe.Fori(1, NG // TR) as u:
                for h2 in range(2):
                    out_pair(u, h2)

            pe.wait_ge(sem("wraw_in"), 48)
            for j in range(3):
                for kd in range(DK):
                    for ko in range(DK):
                        last = nc.tensor.transpose(bank[j][:, kd * D + ko * P:kd * D + (ko + 1) * P],
                                                   wraw[:, j, ko, kd * P:(kd + 1) * P], ident[:, :])
                last.then_inc(sem("wT_ps"), 1)
            pe.wait_ge(sem("wT"), 3)
            pe.wait_ge(sem("y_done"), NG)
            pe.wait_ge(sem("wgu_in"), 32)
            pe.wait_ge(sem("wdn_in"), 16)

            def expert_of(q):
                return pe.value_load(tile_e[0:1, ds(q, 1)], min_val=0, max_val=E - 1)

            def turn0(q, a, w):
                r = a % 2
                if a % 4 == 0:
                    pe.wait_ge(sem(f"er_in{a // 4}"), w)
                if not isinstance(q, int) or q >= 2:
                    pe.wait_ge(sem("eT"), q - 1)
                for k in range(DK):
                    last = nc.tensor.transpose(bank[r][:, k * P:(k + 1) * P], er[:, a // 4, a % 4, k * P:(k + 1) * P], ident[:, :])
                last.then_inc(sem("eT_ps"), 1)

            def up0(q, r, e):
                pe.wait_ge(sem("eT"), q + 1)
                if not isinstance(q, int) or q >= 2:
                    pe.wait_ge(sem("eh"), q - 1)
                for k in range(DK):
                    last = nc.tensor.matmul(bank[2 + r][:, 0:2 * I], eT[:, r, k, :],
                                            wgu[:, ds(e * DK + k, 1), :].rearrange("p o i -> p (o i)"), start=(k == 0), stop=(k == DK - 1))
                last.then_inc(sem("eg_ps"), 1)

            def back0(q, r):
                pe.wait_ge(sem("eh"), q + 1)
                if not isinstance(q, int) or q >= 2:
                    pe.wait_ge(sem("ehT"), q - 1)
                nc.tensor.transpose(bank[4 + r][:, 0:P], eh[:, r, :], ident[:, :]).then_inc(sem("ehT_ps"), 1)

            def down0(q, r, e):
                pe.wait_ge(sem("ehT"), q + 1)
                if not isinstance(q, int) or q >= 2:
                    pe.wait_ge(sem("ey"), q - 1)
                nc.tensor.matmul(bank[6 + r][:, 0:D], ehT[:, r, :], wdn[:, ds(e, 1), :].rearrange("p o d -> p (o d)"),
                                 start=True, stop=True).then_inc(sem("ey_ps"), 1)

            def eight(t, first=False):
                def experts(a):
                    q = t * 8 + a
                    return (expert_of(q - 1) if not first or a >= 1 else None,
                            expert_of(q - 3) if not first or a >= 3 else None)

                now = experts(0)
                for a in range(8):
                    q = t * 8 + a
                    if not first or a >= 1:
                        up0(q - 1, (a + 1) % 2, now[0])
                    nxt = experts(a + 1) if a < 7 else None
                    turn0(q, a, t * 16 + 16)
                    if not first or a >= 2:
                        back0(q - 2, a % 2)
                    if not first or a >= 3:
                        down0(q - 3, (a + 1) % 2, now[1])
                    now = nxt

            eight(0, True)
            with pe.Fori(1, Q0 // 8) as t:
                eight(t)
            up0(Q0 - 1, 1, expert_of(Q0 - 1))
            back0(Q0 - 2, 0)
            down0(Q0 - 3, 1, expert_of(Q0 - 3))
            back0(Q0 - 1, 1)
            down0(Q0 - 2, 0, expert_of(Q0 - 2))
            down0(Q0 - 1, 1, expert_of(Q0 - 1))

            def end_turn(n, src, turned, ready, free, freed, done):
                pe.wait_ge(sem(ready), n + 1)
                if free:
                    pe.wait_ge(sem(free), freed)
                for k in range(DK):
                    for a in range(4):
                        last = nc.tensor.matmul(bank[k][:, a * P:(a + 1) * P], src[:, a, k * P:(k + 1) * P], turned[:, :], start=True, stop=True)
                last.then_inc(sem(done), 1)

            def end_gu(n):
                pe.wait_ge(sem("xT4"), n * 2 + 2)
                if not isinstance(n, int) or n >= 1:
                    pe.wait_ge(sem("hT4"), n)
                for j in range(2):
                    for k in range(DK):
                        last = nc.tensor.matmul(bank[2 + j][:, :], sgu[:, k, j * I:(j + 1) * I], xT4[:, k, :], start=(k == 0), stop=(k == DK - 1))
                last.then_inc(sem("gu4_ps"), 1)

            def end_out(n):
                pe.wait_ge(sem("gT4"), n * 2 + 2)
                pe.wait_ge(sem("hT4"), n + 1)
                if not isinstance(n, int) or n >= 1:
                    pe.wait_ge(sem("x1_sum"), n)
                for a in range(4):
                    o = bank[4 + a // 2][:, (a % 2) * D:(a % 2 + 1) * D]
                    for k in range(DK):
                        nc.tensor.matmul(o, gT4[:, k, a * P:(a + 1) * P], woT[:, k, :], start=(k == 0), stop=False)
                    last = nc.tensor.matmul(o, hT4[:, a * P:(a + 1) * P], sdn[:, :], start=False, stop=True)
                last.then_inc(sem("o_ps"), 1)

            def end_router(n, b, r):
                for j in range(2):
                    pe.wait_ge(sem("n4"), n + 1)
                    if not isinstance(n, int) or n or j:
                        pe.wait_ge(sem("nT"), n * 4 + 2 * j)
                    for k in range(DK):
                        for a in range(2):
                            last = nc.tensor.transpose(bank[6][:, (2 * k + a) * P:(2 * k + a + 1) * P], n4[:, 2 * j + a, k * P:(k + 1) * P], ident[:, :])
                    last.then_inc(sem("nT_ps"), 1)
                    pe.wait_ge(sem("nT"), n * 4 + (2 * j + 2))
                    if j == 0 and not (isinstance(b, int) and b == 0):
                        pe.wait_ge(sem("slot1" if r else "lg1"), b)
                    for a in range(2):
                        o = (4 * r + 2 * j + a) * E
                        for k in range(DK):
                            last = nc.tensor.matmul(bank[7][:, o:o + E], nT[:, j, k, a * P:(a + 1) * P], wg1[:, k, :], start=(k == 0), stop=(k == DK - 1))
                    last.then_inc(sem("lg_ps"), 1)

            def end_ranks(b):
                pe.wait_ge(sem("mb1"), b + 1)
                mm = mb1[:, :, :, :].rearrange("p k t e -> p (k t e)")
                w = 2 * TB * E
                nc.tensor.matmul(bank[7][:, P:P + w], tri[:, :], mm, start=True, stop=True)
                nc.tensor.matmul(bank[7][:, P + w:P + 2 * w], ones_b[:, :], mm, start=True, stop=True).then_inc(sem("rk_ps"), 1)

            def end_step(b, r, last=False):
                n = b * 2 + r
                end_gu(n)
                if not last:
                    end_turn(n + 1, xs4, ident, "xs4", "gT4", n * 2 + 2, "xT_ps")
                end_out(n)
                if not last:
                    end_turn(n + 1, z4, flip, "z4", "xT4", n * 2 + 4, "zT_ps")
                if not isinstance(n, int) or n >= 1:
                    end_router(n - 1, b - (1 - r), 1 - r)
                if r and not (isinstance(b, int) and b == 0):
                    end_ranks(b - 1)

            pe.wait_ge(sem("shared_in"), 64)
            pe.wait_ge(sem("wg1_in"), 16)
            pe.wait_ge(sem("ey"), Q0)
            end_turn(0, xs4, ident, "xs4", None, 0, "xT_ps")
            end_turn(0, z4, flip, "z4", "xT4", 2, "zT_ps")
            for r in range(2):
                end_step(0, r)
            with pe.Fori(1, NB - 1) as b:
                for r in range(2):
                    end_step(b, r)
            for r in range(2):
                end_step(NB - 1, r, r == 1)
            end_router(2 * NB - 1, NB - 1, 1)
            end_ranks(NB - 1)

            pe.wait_ge(sem("xtot"), 1)
            for m in range(DK):
                for k in range(DK):
                    last = nc.tensor.matmul(bank[4][:, m * NB:(m + 1) * NB], wvT[:, k, m * P:(m + 1) * P], xtot[:, k, :],
                                            start=(k == 0), stop=(k == DK - 1))
            last.then_inc(sem("val_ps"), 1)
            pe.wait_ge(sem("vrep"), 1)
            for b in range(NB):
                if b >= 2:
                    pe.wait_ge(sem("att_add"), b - 1)
                for k in range(DK):
                    last = nc.tensor.matmul(bank[5 + b % 2][:, 0:D], vrep[:, k, b, :], waT[:, k, :], start=(k == 0), stop=(k == DK - 1))
                last.then_inc(sem("att_ps"), 1)

            def turn2(n, r, w):
                pe.wait_ge(sem(f"fr_in{r}"), w)
                pe.wait_ge(sem("fTl"), n * 2 + 2)
                for k in range(DK):
                    for a in range(4):
                        last = nc.tensor.transpose(bank[k][:, a * P:(a + 1) * P], fr[:, r, a, k * P:(k + 1) * P], ident[:, :])
                last.then_inc(sem("fT_ps"), 1)

            def up2(e, n, r):
                pe.wait_ge(sem("w_split"), e * 4 + 2)
                pe.wait_ge(sem("fTl"), n * 2 + 4)
                for j in range(HK):
                    pe.wait_ge(sem("hf"), n * HK + (j + 1))
                    o, w = bank[2 + j % 2], j * P
                    first = True
                    for k in range(DK):
                        for wt, xx in ((w1h, fTh), (w1l, fTh), (w1h, fTl)):
                            last = nc.tensor.matmul(o[:, :], wt[:, r, k, w:w + P], xx[:, k, :], start=first, stop=(k == DK - 1 and xx is fTl))
                            first = False
                    last.then_inc(sem("h_ps"), 1)

            def down2(e, n, r, par):
                pe.wait_ge(sem("w_split"), e * 4 + 4)
                pe.wait_ge(sem("fy_free"), n + 1)
                for j in range(HK):
                    pe.wait_ge(sem("h_lo"), n * HK + (j + 3))
                    for a in range(4):
                        o = bank[4 + 2 * par + a // 2][:, (a % 2) * D:(a % 2 + 1) * D]
                        hh, hl = hTh[:, j, a * P:(a + 1) * P], hTl[:, j, a * P:(a + 1) * P]
                        for i, (x, y) in enumerate(((hh, w2h), (hh, w2l), (hl, w2h))):
                            last = nc.tensor.matmul(o, x, y[:, r, j, :], start=(j == 0 and i == 0 and a % 2 == 0),
                                                    stop=(j == HK - 1 and i == 2), skip_group_check=True)
                last.then_inc(sem("f_ps"), 1)

            def block2(e, eh2, r, jb, last=False):
                n = e * 4 + jb
                up2(e, n, r)
                if not last:
                    turn2(n + 1, (jb + 1) % 2, e * 32 + 16 * ((jb + 1) // 2 + 1))
                down2(e, n, r, jb % 2)

            pe.wait_ge(sem("att_add"), NB)
            turn2(0, 0, 16)
            with pe.Fori(0, E // 2 - 1) as t:
                for r in range(2):
                    for jb in range(4):
                        block2(t * 2 + r, None, r, jb)
            for r in range(2):
                for jb in range(4):
                    block2(E - 2 + r, None, r, jb, r == 1 and jb == 3)

        @block.vector
        def _(dve):
            v = nc.vector
            for r in range(2):
                dve.sem_inc(sem(f"x_free{r}"), 1)
            st = Steps(dve, sem("dve_steps"))
            dve.wait_ge(sem("consts"), 9)

            dve.wait_ge(sem("state_in"), 48)
            w = st
            full = [P, NG, CG, ST]
            w.run(v.tensor_tensor(ub[:, :, P:].rearrange("p g (l m) -> p g l m", l=CG), a_in.unsqueeze(2).broadcast_to(full),
                                  mask8[:, :].unsqueeze(1).unsqueeze(3).broadcast_to(full), ALU.mult))
            dve.sem_inc(sem("a_bd"), 1)
            dve.wait_ge(sem("bc_ps"), 1)
            w.run(v.tensor_copy(bc[:, :], bank[7][:, 0:2 * NG]))
            w.mark(v.tensor_copy(ub[:, :, P - 1], bc[:, 0:NG]))
            fb = [P, NG, CG]
            w.run(v.tensor_tensor(bbd[:, :, :], bc[:, 0:NG].unsqueeze(2).broadcast_to(fb), mask8[:, :].unsqueeze(1).broadcast_to(fb), ALU.mult))
            dve.sem_inc(sem("bc"), 1)

            def ln_stats(b):
                r = b % 2
                dve.wait_ge(sem(f"x_in{r}"), b // 2 * 16 + 16)
                for j in range(TB):
                    st.mark(v.bn_stats(bst[:, r, j, :], xl[:, r, j, :]))
                st.settle()
                for j in range(TB):
                    st.mark(v.bn_aggr(mv[:, r, j, :], bst[:, r, j, :]))
                st.settle()
                st.run(v.tensor_scalar(vare[:, r, :], mv[:, r, :, 1], EPS, None, ALU.add))
                dve.sem_inc(sem("ln0_var"), 1)

            def ln_rows(b):
                r = b % 2
                dve.wait_ge(sem("ln0_rstd"), b + 1)
                if b >= 2:
                    dve.wait_ge(sem("tp_ready"), (b - 1) * (TB // 2))
                    dve.wait_ge(sem("xn_done"), b - 1)
                for j in range(TB):
                    st.mark(v.tensor_scalar(nst[:, r, j, :], xl[:, r, j, :], mv[:, r, j, 0:1], rstd[:, r, j:j + 1],
                                            ALU.subtract, ALU.mult))
                st.settle()
                dve.sem_inc(sem("ln0_rows"), 1)
                dve.sem_inc(sem(f"x_free{r}"), 1)

            def store_level(lv, part):
                m = 1 << lv
                for n, g, gr in part:
                    ps = bank[3 + 2 * (n % 2)][:, 0:gr * (m + P)].rearrange("p (g w) -> p g w", g=gr)
                    dve.wait_ge(sem("u_ps"), n + 1)
                    last = v.tensor_copy(ub[:, g:g + gr, P - 2 * m:P - m], ps[:, :, 0:m])
                    if lv < LV - 1:
                        dve.wait_ge(sem("v_ps"), n + 1)
                        last = v.tensor_copy(ub[:, g:g + gr, P:], ps[:, :, m:])
                    last.then_inc(sem("u_done"), 1)

            for b in range(2):
                ln_stats(b)
                ln_rows(b)
            for i, (what, k) in enumerate(plan):
                if what == "level":
                    after = plan[i + 1][1] if plan[i + 1:] and plan[i + 1][0] == "batch" else None
                    if after is not None:
                        ln_stats(after)
                    cs_ = level(k)
                    store_level(k, cs_[:len(cs_) // 2])
                    if after is not None:
                        ln_rows(after)
                    store_level(k, cs_[len(cs_) // 2:])
                elif k == NB - 1:
                    ln_stats(k)
                    ln_rows(k)
            for g in range(NG + 1):
                if g < NG:
                    dve.wait_ge(sem("g_ps"), g + 1)
                    if g >= 2:
                        dve.wait_ge(sem("gt"), g - 1)
                    v.tensor_tensor(gm[:, g % 2, :, :], bank[3 + g % 4][:, :].rearrange("p (t c) -> p t c", c=CG),
                                    mask8[:, :].unsqueeze(1).broadcast_to([P, NT, CG]), ALU.mult).then_inc(sem("g_used"), 1)
                if g >= 1:
                    dve.wait_ge(sem("g_used"), g)
                    v.tensor_reduce(gt[:, g - 1, :], gm[:, (g - 1) % 2, :, :], AX.X, ALU.add).then_inc(sem("gt"), 1)

            c = st
            sg, sc, t2, t3, t4, t5, t6 = rt
            G2 = E // 2
            H2 = G2 // 2

            def bce(ap):
                return ap.unsqueeze(1).broadcast_to([P, NT, E])

            def bct(ap):
                return ap.unsqueeze(2).broadcast_to([P, NT, E])

            def first_max(m, oh, tmp, val, key):
                c.run(v.reduce_max(val, m, AX.X))
                c.run(v.tensor_tensor(tmp, m, bct(val), ALU.is_equal))
                c.run(v.tensor_tensor(tmp, tmp, bce(w8[:, :]), ALU.mult))
                c.run(v.reduce_max(key, tmp, AX.X))
                c.run(v.tensor_tensor(oh, bce(w8[:, :]), bct(key), ALU.is_equal))

            dve.wait_ge(sem("sig0"), 1)
            dve.wait_ge(sem("cb_in"), 16)
            c.run(v.tensor_tensor(sc[:, :, :], sg[:, :, :], bce(cb[:, :]), ALU.add))
            pair = sc[:, :, :].rearrange("p t (g h k) -> p (t g) h k", g=2, h=H2)
            hi = t2[:, :, :].rearrange("p t (g h k) -> p (t g) h k", g=2, h=H2)
            c.mark(v.tensor_tensor(hi[:, :, :, 0], pair[:, :, :, 0], pair[:, :, :, 1], ALU.max))
            c.run(v.tensor_tensor(hi[:, :, :, 1], pair[:, :, :, 0], pair[:, :, :, 1], ALU.min))
            a, b, d_, e_ = r1[0], r1[1], r1[2], r1[3]
            fl = "p t g -> p (t g)"
            c.mark(v.tensor_tensor(a[:, :, :].rearrange(fl), hi[:, :, 0, 0], hi[:, :, 1, 0], ALU.max))
            c.mark(v.tensor_tensor(b[:, :, :].rearrange(fl), hi[:, :, 0, 0], hi[:, :, 1, 0], ALU.min))
            c.run(v.tensor_tensor(d_[:, :, :].rearrange(fl), hi[:, :, 0, 1], hi[:, :, 1, 1], ALU.max))
            c.run(v.tensor_tensor(b[:, :, :], b[:, :, :], d_[:, :, :], ALU.max))
            c.run(v.tensor_tensor(a[:, :, :], a[:, :, :], b[:, :, :], ALU.add))
            c.run(v.tensor_tensor(e_[:, :, 0], a[:, :, 0], a[:, :, 1], ALU.is_ge))
            c.run(v.tensor_scalar(e_[:, :, 1], e_[:, :, 0], -1.0, 1.0, ALU.mult, ALU.add))
            c.run(v.tensor_tensor(t3[:, :, :].rearrange("p t (g k) -> p (t g) k", g=2), sc[:, :, :].rearrange("p t (g k) -> p (t g) k", g=2),
                                  e_[:, :, :].rearrange(fl).unsqueeze(2).broadcast_to([P, 2 * NT, G2]), ALU.mult))
            oh0, oh1 = t4, t5
            top, key = r1[4][:, :, 0], r1[4][:, :, 1]
            first_max(t3[:, :, :], oh0[:, :, :], t6[:, :, :], top, key)
            c.run(v.scalar_tensor_tensor(out=t3[:, :, :], in0=oh0[:, :, :], scalar=-BIG, in1=t3[:, :, :], op0=ALU.mult, op1=ALU.add))
            first_max(t3[:, :, :], oh1[:, :, :], t6[:, :, :], top, key)
            c.run(v.tensor_scalar(xn[:, :, D + 1], key, -1.0, float(E), ALU.mult, ALU.add))
            c.run(v.tensor_tensor(mb[:, :, :], oh0[:, :, :], oh1[:, :, :], ALU.add))
            dve.sem_inc(sem("chosen0"), 1)
            for k, oh in enumerate((oh0, oh1)):
                c.run(v.tensor_tensor(t6[:, :, :], oh[:, :, :], sg[:, :, :], ALU.mult))
                c.run(v.tensor_reduce(r1[5][:, :, k], t6[:, :, :], AX.X, ALU.add))
            c.run(v.tensor_tensor(a[:, :, 0], r1[5][:, :, 0], r1[5][:, :, 1], ALU.add))
            c.run(v.tensor_scalar(a[:, :, 0], a[:, :, 0], 1e-20, None, ALU.add))
            c.run(v.reciprocal(a[:, :, 1], a[:, :, 0]))
            for k in range(2):
                c.run(v.tensor_tensor(gates[:, :, k], r1[5][:, :, k], a[:, :, 1], ALU.mult))
            dve.wait_ge(sem("ranks0"), 1)
            tot, run, one = t2, t3, sc
            et = "p (e t) -> p e t"

            def flat(x):
                return x[:, :, :].rearrange("p t e -> p (t e)")

            c.run(v.tensor_copy(flat(tot).rearrange(et, e=E), view(1, "p (t e) -> p e t", e=E)))
            c.run(v.memset(flat(one), 1.0))
            c.run(v.memset(flat(one).rearrange(et, e=E)[:, :, 0], 0.0))
            c.run(v.tensor_tensor_scan(out=flat(run), data0=flat(one), data1=flat(tot), initial=0.0, op0=ALU.mult, op1=ALU.add))
            cnt, tiles, ends, starts, tmp8, base8 = se
            c.run(v.tensor_copy(cnt[:, :], flat(run).rearrange(et, e=E)[:, :, NT - 1]))
            c.run(v.tensor_tensor(flat(run), flat(run), flat(tot), ALU.subtract))
            dve.wait_ge(sem("iotas"), 4)
            c.run(v.tensor_tensor(flat(tot).rearrange(et, e=E), cnt[:, :].unsqueeze(2).broadcast_to([P, E, NT]),
                                  i64[:, :].unsqueeze(1).broadcast_to([P, E, NT]), ALU.is_gt))
            c.run(v.tensor_reduce(tiles[:, :], flat(tot).rearrange(et, e=E), AX.X, ALU.add))
            c.run(v.memset(tmp8[:, :], 1.0))
            c.run(v.tensor_tensor_scan(out=ends[:, :], data0=tmp8[:, :], data1=tiles[:, :], initial=0.0, op0=ALU.mult, op1=ALU.add))
            c.run(v.tensor_tensor(starts[:, :], ends[:, :], tiles[:, :], ALU.subtract))
            c.run(v.tensor_scalar(base8[:, :], starts[:, :], float(P), None, ALU.mult))
            c.run(v.tensor_tensor(t6[:, :, :], view(0, "p (t e) -> p t e", e=E), flat(run).rearrange("p (e t) -> p t e", e=E), ALU.add))
            c.run(v.tensor_tensor(t6[:, :, :], t6[:, :, :], bce(base8[:, :]), ALU.add))
            for k, oh in enumerate((oh0, oh1)):
                c.run(v.tensor_tensor(oh[:, :, :], oh[:, :, :], t6[:, :, :], ALU.mult))
                c.run(v.tensor_reduce(r1[5][:, :, k], oh[:, :, :], AX.X, ALU.add))
            c.run(v.tensor_copy(slot_u[:, :, :], r1[5][:, :, :]))
            dve.sem_inc(sem("routed0"), 1)
            qe = [P, Q0, E]
            c.run(v.tensor_tensor(q8[:, :, :], iq[:, :].unsqueeze(2).broadcast_to(qe), ends[:, :].unsqueeze(1).broadcast_to(qe), ALU.is_ge))
            c.run(v.tensor_reduce(ef[:, :], q8[:, :, :], AX.X, ALU.add))
            c.run(v.tensor_scalar(ef[:, :], ef[:, :], float(E - 1), None, ALU.min))
            c.run(v.tensor_copy(tile_e[:, :], ef[0:1, :]))
            c.run(v.tensor_tensor(tmp8[:, :], cnt[:, :], base8[:, :], ALU.add))
            c.run(v.tensor_tensor(q8[:, :, :], ef[:, :].unsqueeze(2).broadcast_to(qe), iota8[:, :].unsqueeze(1).broadcast_to(qe), ALU.is_equal))
            c.run(v.tensor_tensor(q8[:, :, :], q8[:, :, :], tmp8[:, :].unsqueeze(1).broadcast_to(qe), ALU.mult))
            c.run(v.tensor_reduce(nvq[:, :], q8[:, :, :], AX.X, ALU.add))
            c.run(v.tensor_tensor(nvq[:, :], nvq[:, :], iq128[:, :], ALU.subtract))
            c.run(v.tensor_scalar(vq[:, :], nvq[:, :], part[:, 0:1], None, ALU.is_gt))
            c.run(v.tensor_tensor(tq[:, :], vq[:, :], trq[:, :], ALU.mult))
            c.run(v.tensor_tensor(tq[:, :], trq[:, :], tq[:, :], ALU.subtract))
            dve.sem_inc(sem("routed0"), 1)

            dve.wait_ge(sem("states"), TB)
            def spread(t):
                for r in range(2):
                    if not isinstance(t, int):
                        dve.wait_ge(sem("y_ps"), t * 2 + (r - 1))
                    sh = [P, CG, NT]
                    v.tensor_tensor(hb[:, r, :, :], hs[:, ds(t * 2 + r, 1), :, :].rearrange("p o b t -> p o (b t)").broadcast_to(sh),
                                    mask8[:, :].unsqueeze(2).broadcast_to(sh), ALU.mult).then_inc(sem("hb"), 1)

            spread(0)
            with dve.Fori(1, NG // 2) as t:
                spread(t)

            for j, w in enumerate((woT, wvT, waT)):
                dve.wait_ge(sem("wT_ps"), j + 1)
                v.tensor_copy(w[:, :, :].rearrange("p k d -> p (k d)"), bank[j][:, :]).then_inc(sem("wT"), 1)

            z = st

            def numbers(u, r, t):
                z.run(v.tensor_tensor(idx[:, :], er[:, r, :, D + 1], ef[:, ds(u * 4, 4)], ALU.is_equal))
                z.run(v.tensor_tensor(idx[:, :], idx[:, :], er[:, r, :, D], ALU.add))
                dve.sem_inc(sem("e_idx"), 1)
                z.run(v.tensor_tensor(idx[:, :], idx[:, :], vq[:, ds(u * 4, 4)], ALU.mult))
                z.run(v.tensor_tensor(eidx[:, r, :, 0], idx[:, :], tq[:, ds(u * 4, 4)], ALU.add))
                dve.sem_inc(sem("e_idxu"), 1)

            def expert0(q, a, t, parts=(0, 1)):
                loop = not isinstance(q, int)
                r = a % 2
                if 0 in parts:
                    dve.wait_ge(sem("esg"), q + 1)
                    if loop or q >= 2:
                        dve.wait_ge(sem("ehT_ps"), q - 1)
                    v.tensor_tensor(eh[:, r, :], bank[2 + r][:, I:2 * I], esg[:, r, :], ALU.mult).then_inc(sem("eh"), 1)
                if 1 in parts and (loop or q >= 2):
                    b = (a - 2) % 8
                    half, u = b // 4, (t - 1 if a < 2 else t) * 2 + b // 4
                    if b % 4 == 0:
                        dve.wait_ge(sem(f"er_in{half}"), t * 16 + 16)
                        if loop:
                            dve.wait_ge(sem(f"e_out{half}"), t * 64)
                        numbers(u, half, t)
                    dve.wait_ge(sem("ey_ps"), q - 1)
                    v.tensor_copy(ey[:, half, b % 4, :], bank[6 + r][:, 0:D]).then_inc(sem("ey"), 1)

            for q in range(8):
                expert0(q, q, 0)
            with dve.Fori(1, Q0 // 8) as t:
                z.enter(t, 8, 1)
                for a in range(8):
                    expert0(t * 8 + a, a, t)
            z.leave(Q0 // 8 - 1)
            for a in range(2):
                expert0(Q0 + a, a, Q0 // 8, (1,))

            y = st

            def norm(src, k, n, dst, free):
                for a in range(4):
                    y.mark(v.bn_stats(est[:, a, :], src(a)))
                y.settle()
                dve.sem_inc(sem("dve_passed"), 1)
                for a in range(4):
                    y.mark(v.bn_aggr(emv[:, a, :], est[:, a, :]))
                y.settle()
                y.run(v.tensor_scalar(evar[:, k, :], emv[:, :, 1], EPS, None, ALU.add))
                dve.sem_inc(sem(("z_var", "x1_var")[k]), 1)
                dve.wait_ge(sem(("z_rstd", "x1_rstd")[k]), n + 1)
                free()
                for a in range(4):
                    y.mark(v.tensor_scalar(dst[:, a, :], src(a), emv[:, a, 0:1], erstd[:, k, a:a + 1], ALU.subtract, ALU.mult))
                y.settle()
                dve.sem_inc(sem(("z4", "n4")[k]), 1)

            def row(n, a):
                return yb[:, ds(n * 4 + a, 1), :].rearrange("p o d -> p (o d)")

            def end_z(n):
                def free():
                    if not isinstance(n, int) or n >= 1:
                        dve.wait_ge(sem("zT_ps"), n)
                norm(lambda a: row(n, a), 0, n, z4, free)

            def end_hidden(n):
                dve.wait_ge(sem("sl4"), n + 1)
                if not isinstance(n, int) or n >= 1:
                    dve.wait_ge(sem("o_ps"), n)
                v.tensor_tensor(hT4[:, :], sl4[:, :], bank[3][:, :], ALU.mult).then_inc(sem("hT4"), 1)

            def end_sum(n, b, r):
                dve.wait_ge(sem("xg_sum"), n * 2 + 2)
                dve.wait_ge(sem(f"yl_in{r}"), b * 16 + 16)
                for k in range(2):
                    for a in range(4):
                        y.mark(v.scalar_tensor_tensor(out=xg[:, a, :], in0=yl[:, r, a, k, :], scalar=gates[:, ds(n * 4 + a, 1), k],
                                                      in1=xg[:, a, :], op0=ALU.mult, op1=ALU.add))
                    y.settle()
                dve.wait_ge(sem("o_ps"), n + 1)
                for h in range(2):
                    y.mark(v.tensor_tensor(yb[:, ds(n * 4 + 2 * h, 2), :].rearrange("p a d -> p (a d)"),
                                           xg[:, 2 * h:2 * h + 2, :].rearrange("p a d -> p (a d)"), bank[4 + h][:, :], ALU.add))
                y.settle()
                dve.sem_inc(sem("x1_sum"), 1)

            def end_norm(n):
                def free():
                    if not isinstance(n, int) or n >= 1:
                        dve.wait_ge(sem("nT_ps"), n * 2)
                        dve.wait_ge(sem("xn1"), n)
                norm(lambda a: row(n, a), 1, n, n4, free)

            s3 = [P, TB, E]

            def be(ap):
                return ap.unsqueeze(1).broadcast_to(s3)

            def bt(ap):
                return ap.unsqueeze(2).broadcast_to(s3)

            def pick(m, oh, tmp, val, key):
                y.run(v.reduce_max(val, m, AX.X))
                y.run(v.tensor_tensor(tmp, m, bt(val), ALU.is_equal))
                y.run(v.tensor_tensor(tmp, tmp, be(w8[:, :]), ALU.mult))
                y.run(v.reduce_max(key, tmp, AX.X))
                y.run(v.tensor_tensor(oh, be(w8[:, :]), bt(key), ALU.is_equal))

            o0, o1, qa, qb, qc, qd = (x[:, :, :] for x in q1[0:6])
            v0, v1, key0, key1, ps0, va = (x[:, :] for x in k1[0:6])

            def end_choose(b):
                dve.wait_ge(sem("lg_ps"), b * 4 + 4)
                y.run(v.tensor_copy(lg1[:, :, :].rearrange("p t e -> p (t e)"), bank[7][:, 0:TB * E]))
                dve.sem_inc(sem("lg1"), 1)
                pick(lg1[:, :, :], o0, qa, v0, key0)
                y.run(v.scalar_tensor_tensor(out=lg1[:, :, :], in0=o0, scalar=-BIG, in1=lg1[:, :, :], op0=ALU.mult, op1=ALU.add))
                pick(lg1[:, :, :], o1, qa, v1, key1)
                y.mark(v.tensor_tensor(rdiff[:, ds(b * TB, TB)], v1, v0, ALU.subtract))
                y.mark(v.tensor_copy(oh1s[:, ds(b * TB, TB), :], o1))
                y.mark(v.tensor_copy(key1s[:, ds(b * TB, TB)], key1))
                y.mark(v.tensor_copy(mb1[:, 0, :, :], o0))
                y.run(v.tensor_copy(mb1[:, 1, :, :], o1))
                dve.sem_inc(sem("mb1"), 1)

            et3 = "p (e t) -> p e t"

            def end_slots(b):
                dve.wait_ge(sem("rk_ps"), b + 1)
                w = TB * E
                for k, oh in enumerate((o0, o1)):
                    tot, run = qa, qb
                    ft, fn = (x.rearrange("p t e -> p (t e)") for x in (tot, run))
                    y.run(v.tensor_copy(ft.rearrange(et3, e=E), bank[7][:, P + 2 * w + k * w:P + 3 * w + k * w].rearrange("p (t e) -> p e t", e=E)))
                    y.run(v.tensor_tensor_scan(out=fn, data0=one64[:, :], data1=ft, initial=0.0, op0=ALU.mult, op1=ALU.add))
                    y.run(v.tensor_tensor(ft, fn, ft, ALU.subtract))
                    y.run(v.tensor_tensor(qc, bank[7][:, P + k * w:P + (k + 1) * w].rearrange("p (t e) -> p t e", e=E), ft.rearrange("p (e t) -> p t e", e=E), ALU.add))
                    y.run(v.tensor_tensor(qc, qc, be(carry[:, k, :]), ALU.add))
                    y.run(v.tensor_tensor(qc, qc, oh, ALU.mult))
                    dst = ps0 if k == 0 else pos1s[:, ds(b * TB, TB)]
                    y.mark(v.tensor_reduce(dst, qc, AX.X, ALU.add))
                    y.run(v.tensor_tensor(carry[:, k, :], carry[:, k, :], fn.rearrange(et3, e=E)[:, :, TB - 1], ALU.add))
                y.run(v.tensor_scalar(va, ps0, float(CAP), None, ALU.is_lt))
                y.mark(v.tensor_copy(valid1[:, ds(b * TB, TB), 0], va))
                y.run(v.tensor_scalar(key0, key0, -float(CAP), float(E * CAP), ALU.mult, ALU.add))
                y.run(v.tensor_tensor(ps0, ps0, key0, ALU.add))
                y.run(v.tensor_tensor(ps0, ps0, f64[2][:, ds(b * TB, TB)], ALU.subtract))
                y.run(v.tensor_tensor(ps0, ps0, va, ALU.mult))
                y.run(v.tensor_tensor(slot1[:, ds(b * TB, TB), 0], ps0, f64[2][:, ds(b * TB, TB)], ALU.add))
                dve.wait_ge(sem("xn1"), b * 2 + 2)
                y.run(v.tensor_scalar(xn[:, ds(b * TB, TB), D + 1], key1s[:, ds(b * TB, TB)], -1.0, float(E), ALU.mult, ALU.add))
                dve.sem_inc(sem("slot1"), 1)

            NORM = 13
            PICK = 5

            def end_step(b, r, last=False):
                n = b * 2 + r
                end_hidden(n)
                if not last:
                    end_z(n + 1)
                end_sum(n, b, r)
                end_norm(n)
                if not (isinstance(b, int) and b == 0):
                    if r == 0:
                        end_choose(b - 1)
                    else:
                        end_slots(b - 1)

            dve.wait_ge(sem("consts1"), 6)
            dve.wait_ge(sem("ey"), Q0)
            y.run(v.memset(one64[:, :].rearrange(et3, e=E)[:, :, 0], 0.0))
            end_z(0)
            for r in range(2):
                end_step(0, r)
            per = 2 * (2 * NORM + 10) + (1 + 2 * PICK + 1 + 5) + (2 * 8 + 8)
            with dve.Fori(1, NB - 1) as b:
                y.enter(b, per, 1)
                for r in range(2):
                    end_step(b, r)
            y.leave(NB - 2)
            for r in range(2):
                end_step(NB - 1, r, r == 1)
            end_choose(NB - 1)
            end_slots(NB - 1)
            y.run(v.tensor_tensor(g64, oh1s[:, :, :], carry[:, 0, :].unsqueeze(1).broadcast_to([P, NT, E]), ALU.mult))
            y.run(v.tensor_reduce(f64[0][:, :], g64, AX.X, ALU.add))
            y.run(v.tensor_tensor(pos1s[:, :], pos1s[:, :], f64[0][:, :], ALU.add))
            y.run(v.tensor_scalar(valid1[:, :, 1], pos1s[:, :], float(CAP), None, ALU.is_lt))
            y.run(v.tensor_scalar(key1s[:, :], key1s[:, :], -float(CAP), float(E * CAP), ALU.mult, ALU.add))
            y.run(v.tensor_scalar(f64[2][:, :], f64[2][:, :], float(N), None, ALU.add))
            y.run(v.tensor_tensor(pos1s[:, :], pos1s[:, :], key1s[:, :], ALU.add))
            y.run(v.tensor_tensor(pos1s[:, :], pos1s[:, :], f64[2][:, :], ALU.subtract))
            y.run(v.tensor_tensor(pos1s[:, :], pos1s[:, :], valid1[:, :, 1], ALU.mult))
            y.run(v.tensor_tensor(slot1[:, :, 1], pos1s[:, :], f64[2][:, :], ALU.add))
            dve.sem_inc(sem("slot1_second"), 1)
            y.run(v.tensor_tensor(c8[:, :], carry[:, 0, :], carry[:, 1, :], ALU.add))
            y.run(v.tensor_tensor(vq1[:, :].rearrange("p (e t) -> p e t", e=E), t128[:, :, :], c8[:, :].unsqueeze(2).broadcast_to([P, E, CT]), ALU.is_lt))
            y.run(v.tensor_tensor(t128[:, :, :].rearrange("p e t -> p (e t)"), vq1[:, :], tq1[:, :], ALU.mult))
            y.run(v.tensor_tensor(tq1[:, :], tq1[:, :], t128[:, :, :].rearrange("p e t -> p (e t)"), ALU.subtract))
            dve.wait_ge(sem("nT"), 8 * NB)
            y.run(v.tensor_reduce(xtot[:, :, :].rearrange("p k b -> p (k b)"), xsum[:, :, :, :].rearrange("p k b j -> p (k b) j"), AX.X, ALU.add))
            dve.sem_inc(sem("xtot"), 1)
            dve.wait_ge(sem("val_ps"), 1)
            y.run(v.tensor_copy(val[:, :, :].rearrange("p k b -> p (k b)"), bank[4][:, 0:DK * NB]))
            y.run(v.tensor_copy(vrep[:, :, :, :].rearrange("p k b m -> p (k b) m"), val[:, :, :].rearrange("p k b -> p (k b)").unsqueeze(2).broadcast_to([P, DK * NB, P])))
            dve.sem_inc(sem("vrep"), 1)
            for b in range(NB):
                dve.wait_ge(sem("att_ps"), b + 1)
                rows_ = yb[:, b * TB:(b + 1) * TB, :]
                v.tensor_tensor(rows_, rows_, bank[5 + b % 2][:, 0:D].unsqueeze(1).broadcast_to([P, TB, D]), ALU.add).then_inc(sem("att_add"), 1)
            dve.sem_inc(sem("sg_diff"), 1)

            dve.sem_inc(sem("h_lo"), 2)
            dve.sem_inc(sem("fTl"), 2)
            dve.sem_inc(sem("fy_free"), 2)
            u = st

            def low(n, r, w):
                dve.wait_ge(sem("fTh"), n * 2 + 2)
                for k in range(DK):
                    v.tensor_tensor(fTl[:, k, :], bank[k][:, :], fTh[:, k, :], ALU.subtract).then_inc(sem("fTl"), 1)
                dve.wait_ge(sem(f"fr_in{r}"), w)
                u.run(v.tensor_tensor(idf[:, r, :], fr[:, r, :, D + 1], ef[:, ds(n * 4, 4)], ALU.is_equal))
                u.run(v.tensor_tensor(idf[:, r, :], idf[:, r, :], fr[:, r, :, D], ALU.add))
                dve.sem_inc(sem("f_idx"), 1)
                u.run(v.tensor_tensor(idf[:, r, :], idf[:, r, :], vq1[:, ds(n * 4, 4)], ALU.mult))
                u.run(v.tensor_tensor(idf[:, r, :], idf[:, r, :], tq1[:, ds(n * 4, 4)], ALU.add))

            def hidden(n):
                if not isinstance(n, int) or n >= 1:
                    dve.wait_ge(sem("f_ps"), n)
                for j in range(HK):
                    dve.wait_ge(sem("hf"), n * HK + (j + 3))
                    u.run(v.tensor_copy(hTh[:, j, :], hf[:, j % 2, :]))
                    v.tensor_tensor(hTl[:, j, :], hf[:, j % 2, :], hTh[:, j, :], ALU.subtract).then_inc(sem("h_lo"), 1)

            def results(e, n, r, par):
                dve.wait_ge(sem("f_ps"), n + 1)
                dve.wait_ge(sem("b2_in"), e * 16 + 16)
                if not isinstance(n, int) or n >= 1:
                    dve.wait_ge(sem("f_out"), n * 64)
                for h in range(2):
                    u.mark(v.tensor_tensor(fy[:, 2 * h:2 * h + 2, :], bank[4 + 2 * par + h][:, :].rearrange("p (a d) -> p a d", a=2),
                                           b2r[:, r, :].unsqueeze(1).broadcast_to([P, 2, D]), ALU.add))
                u.run(v.tensor_copy(idxu[:, :, 0], idf[:, par, :]))
                dve.sem_inc(sem("fy"), 1)
                dve.sem_inc(sem("fy_free"), 1)

            def block2(e, r, jb, last=False):
                n = e * 4 + jb
                hidden(n)
                if not last:
                    low(n + 1, (jb + 1) % 2, e * 32 + 16 * ((jb + 1) // 2 + 1))
                results(e, n, r, jb % 2)

            dve.wait_ge(sem("fT_ps"), 1)
            low(0, 0, 16)
            first = (HK + 4 + 3)
            with dve.Fori(0, E // 2 - 1) as t:
                u.enter(t, 8 * first, 0)
                for r in range(2):
                    for jb in range(4):
                        block2(t * 2 + r, r, jb)
            u.leave(E // 2 - 1)
            for r in range(2):
                for jb in range(4):
                    block2(E - 2 + r, r, jb, r == 1 and jb == 3)

            dve.wait_ge(sem("gates1"), 2)
            u.run(v.tensor_tensor(gates1[:, :, :], gates1[:, :, :], valid1[:, :, :], ALU.mult))

            def output(t, r):
                n = t * 2 + r
                dve.wait_ge(sem(f"ol_in{r}"), t * 16 + 16)
                if not isinstance(t, int):
                    dve.wait_ge(sem(f"stored{r}"), t * 16)
                for a in range(4):
                    u.mark(v.scalar_tensor_tensor(out=oo[:, r, a, :], in0=ol[:, r, a, 0, :], scalar=gates1[:, ds(n * 4 + a, 1), 0],
                                                  in1=row(n, a), op0=ALU.mult, op1=ALU.add))
                u.settle()
                for a in range(4):
                    u.mark(v.scalar_tensor_tensor(out=oo[:, r, a, :], in0=ol[:, r, a, 1, :], scalar=gates1[:, ds(n * 4 + a, 1), 1],
                                                  in1=oo[:, r, a, :], op0=ALU.mult, op1=ALU.add))
                u.settle()
                dve.sem_inc(sem("oo"), 1)

            for r in range(2):
                output(0, r)
            with dve.Fori(1, NB) as t:
                u.enter(t, 16, 1)
                for r in range(2):
                    output(t, r)
            u.leave(NB - 1)


_INS = ['L0_attn_x', 'L0_attn_A', 'L0_attn_Bm', 'L0_attn_Cm', 'L0_attn_Dm', 'L0_attn_ln_w', 'L0_attn_ln_b', 'L0_attn_W_out',
        'L0_attn_b_out', 'L0_ffn_router_weight', 'L0_ffn_correction_bias', 'L0_ffn_w_gate', 'L0_ffn_w_up', 'L0_ffn_w_down',
        'L0_ffn_sw_gate', 'L0_ffn_sw_up', 'L0_ffn_sw_down', 'L1_attn_w_qkv', 'L1_attn_w_o', 'L1_ffn_wg', 'L1_ffn_w1',
        'L1_ffn_b1', 'L1_ffn_w2', 'L1_ffn_b2']
_OUTS = [((8, 1024, 256), 'float32')]


def kernel(**inputs):
    import numpy as _np
    import concourse.bacc as _bacc
    from concourse import mybir as _mybir
    from concourse.bass_utils import run_bass_kernel_spmd as _run

    nc = _bacc.Bacc("TRN2", target_bir_lowering=False, num_devices=1)
    arrays, args = {}, []
    for name in _INS:
        a = _np.ascontiguousarray(inputs[name])
        arrays[f"in_{name}_dram"] = a
        args.append(nc.dram_tensor(f"in_{name}_dram", a.shape, _mybir.dt.from_np(a.dtype), kind="ExternalInput").ap())
    for i, (shape, dtype) in enumerate(_OUTS):
        dt = _mybir.dt.from_np(_np.dtype(dtype))
        args.append(nc.dram_tensor(f"out_{i}_dram", shape, dt, kind="ExternalOutput").ap())
    bass_ssm_moe_then_attention_moe(nc, *args)
    r = _run(nc, [arrays], core_ids=[0])
    return r.results[0]["out_0_dram"]
```

```python
import concourse.bass as bass
from concourse import mybir
from contextlib import ExitStack


class Steps:

    def __init__(self, eng, sem):
        self.eng, self.sem, self.n, self.trip, self.per, self.base, self.first = eng, sem, 0, None, 0, 0, 0

    def mark(self, ins):
        ins.then_inc(self.sem, 1)
        self.n += 1

    def value(self):
        return self.n if self.trip is None else self.trip * self.per + (self.n - self.first * self.per)

    def settle(self):
        self.eng.wait_ge(self.sem, self.value())

    def run(self, ins):
        self.mark(ins)
        self.settle()

    def enter(self, trip, per, first=0):
        self.trip, self.per, self.base, self.first = trip, per, self.n, first

    def leave(self, trips):
        assert self.n == self.base + self.per, (self.n, self.base, self.per)
        self.n, self.trip = self.base + self.per * trips, None


def bass_ssm_moe_then_attention_moe(
    nc, x_in, A_in, Bm_in, Cm_in, Dm_in, lnw_in, lnb_in, Wout_in, bout_in, rw_in, cb_in, wg_in, wu_in,
    wd_in, swg_in, swu_in, swd_in, wqkv_in, wo_in, wgate_in, w1_in, b1_in, w2_in, b2_in, out,
):
    f32, f32r, bf16 = mybir.dt.float32, mybir.dt.float32r, mybir.dt.bfloat16
    u32, i32 = mybir.dt.uint32, mybir.dt.int32
    ALU, ACT, AX = mybir.AluOpType, mybir.ActivationFunctionType, mybir.AxisListType
    ds = bass.ds

    P = 128
    NB, S, D = x_in.shape
    TB = S // P
    NT = NB * TB
    N = NB * S
    ST = A_in.shape[1]
    CG = P // ST
    NG = D // CG
    DK = D // P
    E, _, I = wg_in.shape
    H = w1_in.shape[2]
    HK = H // P
    EPS = 1e-5
    ROW = D + 2
    Q0 = 2 * NT + E
    CAP = 2 * N // E
    CT = CAP // P
    TRASH = Q0 * P
    BIG = 3e38
    TR = 4

    x_v = x_in.rearrange("b (t p) d -> b p t d", p=P)
    x_h = x_in.rearrange("b (u t p) d -> (b u) p t d", p=P, t=4)
    o_h = out.rearrange("b (u t p) d -> (b u) p t d", p=P, t=4)
    w1_v = w1_in.rearrange("e (k p) h -> e p k h", p=P)
    w2_v = w2_in.rearrange("e (k p) d -> e p k d", p=P)
    kpad = nc.dram_tensor("conv_kernels", [D, 2 * P], f32).ap()
    disp = nc.dram_tensor("dispatched", [TRASH + 2 * N, ROW], f32).ap()
    yexp = nc.dram_tensor("expert_rows", [2 * N + Q0 * P, D], f32).ap()

    y_h = yexp[0:2 * N, :].rearrange("(h t p k) d -> h p t k d", p=P, t=4, k=2)
    disp1 = disp[0:E * CAP, :].rearrange("(n t p) c -> n p t c", p=P, t=4)
    NBLK = E * CT // 4

    ctx = ExitStack()
    with ctx:
        def sb(name, shape, dt=f32, c=ctx):
            return c.enter_context(nc.sbuf_tensor(name, shape, dt))

        def pb(name, shape, dt=f32, c=ctx):
            return c.enter_context(nc.psum_tensor(name, shape, dt))

        sems = {}

        def sem(name):
            if name not in sems:
                sems[name] = ctx.enter_context(nc.semaphore(name))
            return sems[name]

        ident = sb("ident", [P, P])
        flip = sb("flip", [P, P])
        tri = sb("tri", [P, P], bf16)
        ones_b = sb("ones_b", [P, P], bf16)
        mask8 = sb("mask8", [P, CG])
        warm = sb("warm", [P, 1])
        half_neg = sb("half_neg", [P, TB])
        zeros = sb("zeros", [P, 2 * ROW])
        part = sb("part", [P, 1])
        w8 = sb("w8", [P, E])
        iota8 = sb("iota8", [P, E])
        cb = sb("cb", [P, E])
        rw = sb("rw", [P, DK, E])
        cols = sb("cols", [P, 16])
        gates = sb("gates", [P, NT, 2])
        slot_u = sb("slot_u", [P, NT, 2], u32)
        tile_e = sb("tile_e", [1, Q0], i32)
        ef = sb("ef", [P, Q0])
        vq = sb("vq", [P, Q0])
        tq = sb("tq", [P, Q0])
        mv = sb("mv", [P, 2, TB, 2])
        bst = sb("bst", [P, 2, TB, 6])
        vare = sb("vare", [P, 2, TB])
        rstd = sb("rstd", [P, 2, TB])

        cB = ExitStack()
        ub = sb("ub", [P, NG, 2 * P], f32, cB)
        vb = sb("vb", [P, NG, 2 * P], f32, cB)
        a_in = vb[:, :, 0:ST]
        pt = ub[:, :, P:2 * P]
        gt = ub[:, :, 0:NT]
        gm = ub[:, :, NT:2 * NT].rearrange("p (r c) t -> p r t c", c=CG)
        kev = vb[0:CG, :, 0:P]
        cB.close()
        yb = sb("yb", [P, NT, D])
        rdiff = sb("rdiff", [P, NT])
        valid1 = sb("valid1", [P, NT, 2])
        gates1 = sb("gates1", [P, NT, 2])
        vq1 = sb("vq1", [P, E * CT])
        tq1 = sb("tq1", [P, E * CT])
        idx = sb("idx", [P, 4])
        eidx = sb("eidx", [P, 2, 4, 1], u32)
        idf = sb("idf", [P, 2, 4])
        idxu = sb("idxu", [P, 4, 1], u32)
        cX = ExitStack()
        xn = sb("xn", [P, NT, ROW], f32, cX)
        sgu = sb("sgu", [P, DK, 2 * I], f32, cX)
        sdn = sb("sdn", [P, D], f32, cX)
        bo = sb("bo", [P, D], f32, cX)
        cW = ExitStack()
        xl = sb("xl", [P, 2, TB, D], f32, cW)
        cW.close()
        cW = ExitStack()
        q8 = sb("q8", [P, Q0, E], f32, cW)
        cW.close()
        cW = ExitStack()
        wgu = sb("wgu", [P, E * DK, 2 * I], f32, cW)

        cW.close()
        cE1 = ExitStack()
        yl = sb("yl", [P, 2, 4, 2, D], f32, cE1)

        cS = ExitStack()
        vv = sb("vv", [P, NG, P + 1], f32, cS)
        bcg = sb("bcg", [2 * NG, P], f32, cS)
        bc = sb("bc", [P, 2 * NG], f32, cS)
        bbd = sb("bbd", [P, NG, CG], f32, cS)
        dcg = sb("dcg", [CG, NG], f32, cS)
        cR = ExitStack()
        nst = sb("nst", [P, 2, TB, D], f32, cR)
        xt = sb("xt", [P, 2, 2, DK, P], f32, cR)
        cR.close()
        hs = sb("hs", [P, NG, NB, TB], f32, cS)
        cQ = ExitStack()
        rt = [sb(f"rt{i}", [P, NT, E], f32, cQ) for i in range(7)]
        mb = sb("mb", [P, NT, E], bf16, cQ)
        r1 = [sb(f"r1_{i}", [P, NT, 2], f32, cQ) for i in range(6)]
        iq = sb("iq", [P, Q0], f32, cQ)
        iq128 = sb("iq128", [P, Q0], f32, cQ)
        trq = sb("trq", [P, Q0], f32, cQ)
        nvq = sb("nvq", [P, Q0], f32, cQ)
        i64 = sb("i64", [P, NT], f32, cQ)
        se = [sb(f"se{i}", [P, E], f32, cQ) for i in range(6)]
        cQ.close()
        th = sb("th", [P, TR, CG, P], f32, cS)
        vst = sb("vst", [P, 2, P], f32, cS)
        hb = sb("hb", [P, 2, CG, NT], f32, cS)
        cS.close()

        woT = sb("woT", [P, DK, D], f32, cE1)
        wvT = sb("wvT", [P, DK, D], f32, cE1)
        waT = sb("waT", [P, DK, D], f32, cE1)
        cM = ExitStack()
        wdn = sb("wdn", [P, E, D], f32, cM)
        er = sb("er", [P, 2, 4, ROW], f32, cM)
        eT = sb("eT", [P, 2, DK, P], f32, cM)
        esg = sb("esg", [P, 2, I], f32, cM)
        eh = sb("eh", [P, 2, I], f32, cM)
        ehT = sb("ehT", [P, 2, P], f32, cM)
        ey = sb("ey", [P, 2, 4, D], f32, cM)
        wraw = sb("wraw", [P, 3, DK, D], f32, cM)
        cM.close()

        cE = ExitStack()
        xg = sb("xg", [P, 4, D], f32, cE)
        xs4 = sb("xs4", [P, 4, D], f32, cE)
        z4 = sb("z4", [P, 4, D], f32, cE)
        n4 = sb("n4", [P, 4, D], f32, cE)
        pair = sb("pair", [P, 2, DK, 4 * P], f32, cE)
        xT4, gT4 = pair[:, 0, :, :], pair[:, 1, :, :]
        vrep = pair[:, :, :, :].rearrange("p a k c -> p (a k c)").rearrange("p (k b m) -> p k b m", k=DK, b=NB)
        sl4 = sb("sl4", [P, 4 * P], f32, cE)
        hT4 = sb("hT4", [P, 4 * P], f32, cE)
        nT = sb("nT", [P, 2, DK, 2 * P], f32, cE)
        wg1 = sb("wg1", [P, DK, E], f32, cE)
        bo_r = sb("bo_r", [33, D], f32r, cE)
        bo_h = sb("bo_h", [33, D], f32r, cE)
        one_r = sb("one_r", [33, P], f32r, cE)
        xsum = sb("xsum", [P, DK, NB, TB // 2], f32, cE)
        xtot = sb("xtot", [P, DK, NB], f32, cE)
        val = sb("val", [P, DK, NB], f32, cE)
        est = sb("est", [P, 4, 6], f32, cE)
        emv = sb("emv", [P, 4, 2], f32, cE)
        evar = sb("evar", [P, 2, 4], f32, cE)
        erstd = sb("erstd", [P, 2, 4], f32, cE)
        lg1 = sb("lg1", [P, TB, E], f32, cE)
        q1 = [sb(f"q1_{i}", [P, TB, E], f32, cE) for i in range(9)]
        k1 = [sb(f"k1_{i}", [P, TB], f32, cE) for i in range(8)]
        mb1 = sb("mb1", [P, 2, TB, E], bf16, cE)
        oh1s = sb("oh1s", [P, NT, E], f32, cE)
        key1s = sb("key1s", [P, NT], f32, cE)
        pos1s = sb("pos1s", [P, NT], f32, cE)
        carry = sb("carry", [P, 2, E], f32, cE)
        one64 = sb("one64", [P, E * TB], f32, cE)
        slot1 = sb("slot1", [P, NT, 2], u32, cE)
        f64 = [sb(f"f64_{i}", [P, NT], f32, cE) for i in range(3)]
        g64 = z4[:, :, :].rearrange("p a d -> p (a d)")[:, 0:NT * E].rearrange("p (t e) -> p t e", e=E)
        t128 = sb("t128", [P, E, CT], f32, cE)
        c8 = sb("c8", [P, E], f32, cE)
        cE.close()
        cE1.close()
        cX.close()

        cF = ExitStack()
        hTh = sb("hTh", [P, HK, 4 * P], f32r, cF)
        hTl = sb("hTl", [P, HK, 4 * P], f32r, cF)
        hf = sb("hf", [P, 2, 4 * P], f32, cF)
        w1h = sb("w1h", [P, 2, DK, H], f32r, cF)
        w1l = sb("w1l", [P, 2, DK, H], f32r, cF)
        w2h = sb("w2h", [P, 2, HK, D], f32r, cF)
        w2l = sb("w2l", [P, 2, HK, D], f32r, cF)
        wr = sb("wr", [P, HK * D], f32, cF)
        fr = sb("fr", [P, 2, 4, ROW], f32, cF)
        fTh = sb("fTh", [P, DK, 4 * P], f32r, cF)
        fTl = sb("fTl", [P, DK, 4 * P], f32r, cF)
        fy = sb("fy", [P, 4, D], f32, cF)
        b1c = sb("b1c", [P, E, HK], f32, cF)
        b2r = sb("b2r", [P, 2, D], f32, cF)
        cF.close()
        cO = ExitStack()
        ol = sb("ol", [P, 2, 4, 2, D], f32, cO)
        oo = sb("oo", [P, 2, 4, D], f32, cO)
        cO.close()

        bank = [pb(f"bank{i}", [P, 512]) for i in range(8)]

        def view(i, pat, **k):
            return bank[i][:, :].rearrange(pat, **k)

        LV = 7
        chunks = []
        for lv in range(LV):
            gr = 512 // ((1 << lv) + P)
            chunks += [(lv, g, min(gr, NG - g)) for g in range(0, NG, gr)]

        def level(lv):
            return [(n, g, gr) for n, (l, g, gr) in enumerate(chunks) if l == lv]

        def before(n):
            lv, g, gr = chunks[n]
            own = [i for i, g0, gr0 in level(lv - 1) if g0 < g + gr] if lv else []
            return max(own + [n - 2, -1]) + 1

        LNP = TB // 2 + 1
        plan = []
        for lv in range(LV):
            for c, (n, _, _) in enumerate(level(lv)):
                plan.append(("chunk", n, 0))
                b = 2 * lv + c // LNP
                if b < NB and c < 2 * LNP:
                    plan.append(("ln", b, c % LNP))

        RANKS_BEFORE = level(LV - 2)[4][0]

        block = ctx.enter_context(nc.Block())
        disp_fill = disp[0:TRASH, :].rearrange("(a p) c -> p a c", p=P)

        @block.sync
        def _(sp):
            sp.dma_start(bcg[0:NG, :], Bm_in.rearrange("(g l) n -> g (l n)", l=CG)).then_inc(sem("state_in"), 16)
            sp.dma_start(bcg[NG:2 * NG, :], Cm_in.rearrange("(g l) n -> g (l n)", l=CG)).then_inc(sem("state_in"), 16)
            sp.dma_start(cb[:, :], cb_in.partition_broadcast(P)).then_inc(sem("cb_in"), 16)
            with nc.allow_non_contiguous_dma(reason="small"):
                for k in range(DK):
                    sp.dma_start(rw[:, k, :], rw_in[:, k * P:(k + 1) * P].rearrange("e p -> p e")).then_inc(sem("rw_in"), 16)
                for j, v in enumerate((lnw_in, lnb_in)):
                    sp.dma_start(cols[:, 2 * j:2 * j + 2], v.rearrange("(k p) -> p k", p=P)).then_inc(sem("cols_in"), 16)
                with sp.Fori(0, NB // 2) as t:
                    for r in range(2):
                        sp.wait_ge(sem(f"x_free{r}"), t + 1)
                        sp.dma_start(xl[:, r, :, :], x_v[ds(2 * t + r, 1)].rearrange("o p t d -> p (o t) d")).then_inc(sem(f"x_in{r}"), 16)
                sp.dma_start(dcg[:, :], Dm_in.rearrange("(g l) -> l g", l=CG)).then_inc(sem("dcg_in"), 16)
                for k, wd in ((0, swg_in), (1, swu_in)):
                    sp.dma_start(sgu[:, :, k * I:(k + 1) * I], wd.rearrange("(k p) i -> p k i", p=P)).then_inc(sem("shared_in"), 16)
                sp.dma_start(sdn[:, :], swd_in).then_inc(sem("shared_in"), 16)
                sp.dma_start(bo[:, :], bout_in.partition_broadcast(P)).then_inc(sem("shared_in"), 16)
                sp.wait_ge(sem("zeros"), 1)
                with sp.Fori(0, Q0 // 2) as j:
                    sp.dma_start(disp_fill[:, ds(2 * j, 2), :], zeros[:, :].rearrange("p (a c) -> p a c", a=2)).then_inc(sem("filled0"), 16)
                sp.dma_start(kpad.rearrange("(a p) c -> p a c", p=P), zeros[:, 0:4 * P].rearrange("p (a c) -> p a c", a=2)).then_inc(sem("kpad_zero"), 16)
                sp.wait_ge(sem("kpad_zero"), 16)
                sp.wait_ge(sem("kernels"), 1)
                sp.dma_start(kpad[:, 0:P].rearrange("(g l) j -> l g j", l=CG), kev[:, :, :]).then_inc(sem("kpad_in"), 16)
                sp.wait_ge(sem("kpad_in"), 16)
                sp.wait_ge(sem("routed0"), 2)
                for k, wd in ((0, wg_in), (1, wu_in)):
                    sp.dma_start(wgu[:, :, k * I:(k + 1) * I], wd.rearrange("e (k p) i -> p (e k) i", p=P)).then_inc(sem("wgu_in"), 16)
                toep = bass.AP(kpad.tensor, 0, [[CG * 2 * P, NG], [1, P], [2 * P, CG], [1, P]])
                for r in range(TR):
                    sp.dma_start(th[:, r, :, :], toep[r]).then_inc(sem(f"th_in{r}"), 16)
                with sp.Fori(1, NG // TR) as t:
                    for r in range(TR):
                        sp.wait_ge(sem("y_ps"), t * TR + (r - TR + 1))
                        sp.dma_start(th[:, r, :, :], toep[ds(t * TR + r, 1)].rearrange("o s l i -> s (o l) i")).then_inc(sem(f"th_in{r}"), 16)
                sp.wait_ge(sem("y_ps"), NG)
                for j, w in enumerate((Wout_in, wqkv_in[2 * D:3 * D, :], wo_in)):
                    sp.dma_start(wraw[:, j, :, :], w.rearrange("(k p) d -> p k d", p=P)).then_inc(sem("wraw_in"), 16)
                sp.dma_start(wdn[:, :, :], wd_in.rearrange("e i d -> i e d")).then_inc(sem("wdn_in"), 16)
                sp.wait_ge(sem("scattered0"), 1)
                disp0 = disp[0:TRASH, :].rearrange("(u a p) c -> u p a c", p=P, a=4)
                for r in range(2):
                    sp.dma_start(er[:, r, :, :], disp0[r]).then_inc(sem(f"er_in{r}"), 16)
                with sp.Fori(1, Q0 // 8) as t:
                    for r in range(2):
                        sp.wait_ge(sem("eT_ps"), t * 8 + (4 * r - 4))
                        sp.wait_ge(sem("e_idx"), t * 2 + (r - 1))
                        sp.dma_start(er[:, r, :, :], disp0[ds(t * 2 + r, 1)].rearrange("o p a c -> p (o a) c")).then_inc(sem(f"er_in{r}"), 16)
                sp.wait_ge(sem("e_stored"), 1)
                sp.dma_start(wg1[:, :, :], wgate_in.rearrange("(k p) e -> p k e", p=P)).then_inc(sem("wg1_in"), 16)

                def end_load(t, r):
                    if not isinstance(t, int) or r:
                        sp.wait_ge(sem("x1_sum"), t * 2 + r)
                    sp.dma_start(xg[:, :, :], x_h[ds(t * 2 + r, 1)].rearrange("o p t d -> p (o t) d")).then_inc(sem("xg_in"), 16)
                    sp.dma_start(yl[:, r, :, :, :], y_h[ds(t * 2 + r, 1)].rearrange("o p t k d -> p (o t) k d")).then_inc(sem(f"yl_in{r}"), 16)

                for r in range(2):
                    end_load(0, r)
                with sp.Fori(1, NB) as t:
                    for r in range(2):
                        end_load(t, r)
                sp.wait_ge(sem("dispatch1_done"), 1)
                sp.wait_ge(sem("att_add"), NB)
                sp.dma_start(b1c[:, :, :], b1_in.rearrange("e (k p) -> p e k", p=P)).then_inc(sem("b1_in"), 16)

                def rows(n, r, first):
                    if not first:
                        sp.wait_ge(sem("fT_ps"), n - 1)
                        sp.wait_ge(sem("f_idx"), n - 1)
                    sp.dma_start(fr[:, r, :, :], disp1[ds(n, 1)].rearrange("o p t c -> p (o t) c")).then_inc(sem(f"fr_in{r}"), 16)

                rows(0, 0, True)
                rows(1, 1, True)
                with sp.Fori(1, NBLK // 2) as n:
                    for r in range(2):
                        rows(n * 2 + r, r, False)
                sp.wait_ge(sem("f_stored"), 1)

                def out_load(t, r):
                    sp.dma_start(ol[:, r, :, :, :], y_h[ds(t * 2 + r, 1)].rearrange("o p t k d -> p (o t) k d")).then_inc(sem(f"ol_in{r}"), 16)

                for r in range(2):
                    out_load(0, r)
                with sp.Fori(1, NB) as t:
                    for r in range(2):
                        sp.wait_ge(sem("oo"), t * 2 + (r - 1))
                        out_load(t, r)

        @block.gpsimd
        def _(pool):
            for j, (ap, v) in enumerate(((ident, 0.0), (flip, 0.0), (tri, 1.0), (ones_b, 1.0), (mask8, 1.0), (half_neg, -0.5), (zeros, 0.0))):
                last = nc.gpsimd.memset(ap[:, :], v)
                if ap is zeros:
                    last.then_inc(sem("zeros"), 1)
                else:
                    last.then_inc(sem("consts0"), 1)
            pool.wait_ge(sem("consts0"), 6)
            nc.gpsimd.affine_select(out=ident[:, :], in_=ident[:, :], compare_op=ALU.not_equal, fill=1.0, base=0,
                                    pattern=[[-1, P]], channel_multiplier=1).then_inc(sem("consts"), 1)
            nc.gpsimd.affine_select(out=flip[:, :], in_=flip[:, :], compare_op=ALU.not_equal, fill=1.0, base=1 - P,
                                    pattern=[[1, P]], channel_multiplier=1).then_inc(sem("consts"), 1)
            nc.gpsimd.affine_select(out=tri[:, :], in_=tri[:, :], compare_op=ALU.is_gt, fill=0.0, base=0,
                                    pattern=[[1, P]], channel_multiplier=-1).then_inc(sem("consts"), 1)
            nc.gpsimd.affine_select(out=mask8[:, :], in_=mask8[:, :], compare_op=ALU.is_ge, fill=0.0, base=0,
                                    pattern=[[-ST, CG]], channel_multiplier=1).then_inc(sem("consts"), 1)
            pool.wait_ge(sem("consts"), 4)
            nc.gpsimd.affine_select(out=mask8[:, :], in_=mask8[:, :], compare_op=ALU.is_gt, fill=0.0, base=ST,
                                    pattern=[[ST, CG]], channel_multiplier=-1).then_inc(sem("consts"), 1)
            io = dict(allow_small_or_imprecise_dtypes=True)
            nc.gpsimd.iota(part[:, :], [[0, 1]], base=0, channel_multiplier=1, **io).then_inc(sem("consts"), 1)
            nc.gpsimd.iota(iota8[:, :], [[1, E]], base=0, channel_multiplier=0, **io).then_inc(sem("consts"), 1)
            nc.gpsimd.iota(w8[:, :], [[-1, E]], base=E, channel_multiplier=0, **io).then_inc(sem("consts"), 1)
            nc.gpsimd.iota(xn[:, :, D:D + 1], [[2 * P, NT], [0, 1]], base=0, channel_multiplier=2, **io).then_inc(sem("consts"), 1)
            for b in range(NB):
                pool.wait_ge(sem("ln0_var"), b + 1)
                nc.gpsimd.tensor_tensor(rstd[:, b % 2, :], vare[:, b % 2, :], half_neg[:, :], ALU.pow).then_inc(sem("ln0_rstd"), 1)
            pool.wait_ge(sem("logits0"), 1)
            pool.wait_ge(sem("xn_done"), NB)
            nc.gpsimd.iota(iq[:, :], [[1, Q0]], base=0, channel_multiplier=0, **io).then_inc(sem("iotas"), 1)
            nc.gpsimd.iota(iq128[:, :], [[P, Q0]], base=0, channel_multiplier=0, **io).then_inc(sem("iotas"), 1)
            nc.gpsimd.iota(trq[:, :], [[P, Q0]], base=2 * N, channel_multiplier=1, **io).then_inc(sem("iotas"), 1)
            nc.gpsimd.iota(i64[:, :], [[P, NT]], base=0, channel_multiplier=0, **io).then_inc(sem("iotas"), 1)
            nc.gpsimd.memset(hs[:, :, :, 0], 0.0).then_inc(sem("states"), 1)
            pool.wait_ge(sem("routed0"), 1)
            pool.wait_ge(sem("xn_done"), NB)
            pool.wait_ge(sem("filled0"), 16 * (Q0 // 2))
            for i in range(NT):
                for k in range(2):
                    nc.gpsimd.indirect_dma_start(disp, bass.IndirectOffsetOnAxis(ap=slot_u[:, i, k:k + 1], axis=0),
                                                 xn[:, i, :], None).then_inc(sem("dispatched0"), 16)
            pool.wait_ge(sem("dispatched0"), 16 * 2 * NT)
            pool.sem_inc(sem("scattered0"), 1)

            with pool.Fori(0, Q0 // 8) as t:
                for r in range(2):
                    pool.wait_ge(sem("e_idxu"), t * 2 + (r + 1))
                    for a in range(4):
                        pool.wait_ge(sem("ey"), t * 8 + (4 * r + a + 1))
                        pool.sem_inc(sem("pool_passed"), 1)
                        nc.gpsimd.indirect_dma_start(yexp, bass.IndirectOffsetOnAxis(ap=eidx[:, r, a, :], axis=0), ey[:, r, a, :], None).then_inc(sem(f"e_out{r}"), 16)
            for r in range(2):
                pool.wait_ge(sem(f"e_out{r}"), 64 * (Q0 // 8))
            pool.sem_inc(sem("e_stored"), 1)

            nc.gpsimd.memset(one64[:, :], 1.0).then_inc(sem("consts1"), 1)
            nc.gpsimd.memset(carry[:, :, :], 0.0).then_inc(sem("consts1"), 1)
            nc.gpsimd.iota(f64[2][:, :], [[P, NT]], base=TRASH, channel_multiplier=1, **io).then_inc(sem("consts1"), 1)
            nc.gpsimd.iota(t128[:, :, :], [[0, E], [P, CT]], base=0, channel_multiplier=1, **io).then_inc(sem("consts1"), 1)
            nc.gpsimd.iota(tq1[:, :], [[P, E * CT]], base=2 * N, channel_multiplier=1, **io).then_inc(sem("consts1"), 1)
            nc.gpsimd.iota(ef[:, 0:E * CT], [[1, E], [0, CT]], base=0, channel_multiplier=0, **io).then_inc(sem("consts1"), 1)

            def pows(k, n):
                pool.wait_ge(sem(("z_var", "x1_var")[k]), n + 1)
                nc.gpsimd.tensor_tensor(erstd[:, k, :], evar[:, k, :], half_neg[:, 0:4], ALU.pow).then_inc(sem(("z_rstd", "x1_rstd")[k]), 1)

            def put1(b, half):
                pool.wait_ge(sem("slot1"), b + 1)
                for i in range(b * TB + half * 4, b * TB + half * 4 + 4):
                    nc.gpsimd.indirect_dma_start(disp, bass.IndirectOffsetOnAxis(ap=slot1[:, i, 0:1], axis=0),
                                                 xn[:, i, :], None).then_inc(sem("dispatched1"), 16)

            pows(0, 0)
            for n in range(2 * NB):
                pool.wait_ge(sem("xg_in"), 16 * (n + 1))
                nc.gpsimd.tensor_tensor(xg[:, :, :], xg[:, :, :], xn[:, 4 * n:4 * n + 4, 0:D], ALU.add).then_inc(sem("xg_sum"), 1)
                if n >= 5:
                    put1((n - 5) // 2, (n - 5) % 2)
                if n + 1 < 2 * NB:
                    pows(0, n + 1)
                pows(1, n)
            for n in range(2 * NB - 1, 2 * NB + 4):
                put1((n - 4) // 2, n % 2)
            pool.wait_ge(sem("slot1_second"), 1)
            for i in range(NT):
                nc.gpsimd.indirect_dma_start(disp, bass.IndirectOffsetOnAxis(ap=slot1[:, i, 1:2], axis=0),
                                             xn[:, i, :], None).then_inc(sem("dispatched1"), 16)
            pool.wait_ge(sem("dispatched1"), 16 * 2 * NT)
            pool.sem_inc(sem("dispatch1_done"), 1)

            def load_w(k, e, r):
                src = (w1_v, w2_v)[k][ds(e, 1)].rearrange("o p k h -> p (o k) h")
                pool.dma_start(wr[:, :].rearrange("p (k h) -> p k h", k=(DK, HK)[k]), src).then_inc(sem("wr_in"), 16)

            def split(k, e, r):
                hi, lo = ((w1h, w1l), (w2h, w2l))[k]
                pool.wait_ge(sem("wr_in"), e * 32 + 16 * (k + 1))
                pool.sem_inc(sem("pool_passed"), 1)
                fl = "p a b -> p (a b)"
                nc.gpsimd.tensor_copy(hi[:, r, :, :].rearrange(fl), wr[:, :]).then_inc(sem("w_split"), 1)
                pool.wait_ge(sem("w_split"), e * 4 + 2 * k + 1)
                nc.gpsimd.tensor_tensor(lo[:, r, :, :].rearrange(fl), wr[:, :], hi[:, r, :, :].rearrange(fl), ALU.subtract).then_inc(sem("w_split"), 1)
                pool.wait_ge(sem("w_split"), e * 4 + 2 * k + 2)
                pool.sem_inc(sem("pool_passed"), 1)

            def load_b(e, r):
                pool.dma_start(b2r[:, r, :], b2_in[ds(e, 1), :].rearrange("o d -> (o d)").partition_broadcast(P)).then_inc(sem("b2_in"), 16)

            def put2(n):
                pool.wait_ge(sem("fy"), n + 1)
                pool.sem_inc(sem("pool_passed"), 1)
                for j in range(4):
                    nc.gpsimd.indirect_dma_start(yexp, bass.IndirectOffsetOnAxis(ap=idxu[:, j, :], axis=0), fy[:, j, :], None).then_inc(sem("f_out"), 16)

            pool.wait_ge(sem("att_add"), NB)
            load_w(0, 0, 0)
            split(0, 0, 0)
            load_w(1, 0, 0)
            load_b(0, 0)
            split(1, 0, 0)

            def expert(e, r, last=False):
                put2(e * 4)
                if not last:
                    load_w(0, e + 1, 1 - r)
                    load_b(e + 1, 1 - r)
                put2(e * 4 + 1)
                if not last:
                    split(0, e + 1, 1 - r)
                    load_w(1, e + 1, 1 - r)
                put2(e * 4 + 2)
                if not last:
                    split(1, e + 1, 1 - r)
                put2(e * 4 + 3)

            with pool.Fori(0, E // 2 - 1) as t:
                for r in range(2):
                    expert(t * 2 + r, r)
            expert(E - 2, 0)
            expert(E - 1, 1, True)
            pool.wait_ge(sem("f_out"), 64 * NBLK)
            pool.sem_inc(sem("f_stored"), 1)

        @block.scalar
        def _(act):
            with nc.allow_non_contiguous_dma(reason="rows of a state matrix"):
                act.dma_start(a_in, A_in.rearrange("(g l) n m -> (l n) g m", l=CG)).then_inc(sem("state_in"), 16)
            act.wait_ge(sem("consts"), 9)
            for c in range(NG // 4):
                act.wait_ge(sem("at_ps"), c + 1)
                nc.scalar.activation(vb[:, 4 * c:4 * c + 4, P:], bank[3 + c % 2][:, :].rearrange("p (g m) -> p g m", g=4), ACT.Copy).then_inc(sem("at_bd"), 1)
            act.wait_ge(sem("v0"), 1)
            nc.scalar.activation(vb[:, :, P - 1:P], bank[7][:, 2 * NG:3 * NG].unsqueeze(2), ACT.Copy).then_inc(sem("v_first"), 1)

            def ln_part(b, h):
                if h == TB // 2:
                    act.wait_ge(sem("ln0_rows"), b + 1)
                    nc.scalar.activation(xn[:, b * TB:(b + 1) * TB, 0:D], nst[:, b % 2, :, :], ACT.Copy).then_inc(sem("xn_done"), 1)
                else:
                    n = b * TB // 2 + h
                    act.wait_ge(sem("tp_ready"), n + 1)
                    if n >= 2:
                        act.wait_ge(sem("xt_used"), n - 1)
                    nc.scalar.activation(xt[:, h % 2, :, :, :], view(h % 2, "p (a c m) -> p a c m", a=2, c=DK), ACT.Copy).then_inc(sem("xt_ready"), 1)

            def store_chunk(n):
                lv, g, gr = chunks[n]
                m = 1 << lv
                if n == level(LV - 1)[0][0]:
                    act.wait_ge(sem("v_done"), n)
                    nc.scalar.activation(vv[:, :, m:P], vb[:, :, m:P], ACT.Copy).then_inc(sem("v_half"), 1)
                    nc.scalar.activation(vv[:, :, P:P + 1], bc[:, NG:2 * NG].unsqueeze(2), ACT.Copy).then_inc(sem("v_half"), 1)
                to = vb if lv < LV - 1 else vv
                ps = bank[4 + 2 * (n % 2)][:, 0:gr * (m + P)].rearrange("p (g w) -> p g w", g=gr)
                act.wait_ge(sem("v_ps"), n + 1)
                nc.scalar.activation(to[:, g:g + gr, P - 2 * m:P - m], ps[:, :, 0:m], ACT.Copy)
                nc.scalar.activation(vb[:, g:g + gr, P:], ps[:, :, m:], ACT.Copy).then_inc(sem("v_done"), 1)

            for what, i, h in plan:
                if what == "chunk":
                    store_chunk(i)
                else:
                    ln_part(i, h)
                if (what, i, h) == ("ln", NB - 1, LNP - 1):
                    act.wait_ge(sem("logits0"), 1)
                    act.wait_ge(sem("xn_done"), NB)
                    nc.scalar.activation(rt[0][:, :, :], view(2, "p (a c) -> p a c", c=E), ACT.Sigmoid).then_inc(sem("sig0"), 1)
            for c in range(NG // 4):
                act.wait_ge(sem("k_ps"), c + 1)
                nc.scalar.activation(kev[:, 4 * c:4 * c + 4, :], bank[3 + c % 2][0:CG, :].rearrange("p (g j) -> p g j", g=4), ACT.Copy).then_inc(sem("k_out"), 1)
            for c in range(NG // 4):
                act.wait_ge(sem("pt_ps"), c + 1)
                nc.scalar.activation(pt[:, 4 * c:4 * c + 4, :], bank[5 + c % 2][:, :].rearrange("p (g j) -> p g j", g=4), ACT.Copy).then_inc(sem("pt"), 1)
            for c in range(TB - 1):
                act.wait_ge(sem("step_ps"), c + 1)
                nc.scalar.activation(hs[:, :, :, c + 1], bank[5][:, 0:NG * NB].rearrange("p (g b) -> p g b", g=NG), ACT.Copy).then_inc(sem("states"), 1)
            act.wait_ge(sem("routed0"), 2)
            def copy_v(g, r):
                if not isinstance(g, int) or g >= 2:
                    act.wait_ge(sem("y_ps"), g - 1)
                    act.sem_inc(sem("act_passed"), 1)
                nc.scalar.activation(vst[:, r:r + 1, :], vv[:, ds(g, 1), 0:P], ACT.Copy).then_inc(sem("vst"), 1)

            def store_y(g, r):
                act.wait_ge(sem("y_ps"), g + 1)
                act.sem_inc(sem("act_passed"), 1)
                nc.scalar.activation(yb[:, :, ds(g * CG, CG)], view(6 + r, "p (l i) -> p i l", l=CG), ACT.Copy).then_inc(sem("y_done"), 1)

            for r in range(2):
                copy_v(r, r)
            with act.Fori(0, NG // 2 - 1) as t:
                for r in range(2):
                    copy_v(t * 2 + (r + 2), r)
                    store_y(t * 2 + r, r)
            for r in range(2):
                store_y(NG - 2 + r, r)

            nc.scalar.activation(warm[:, :], part[:, :], ACT.Silu).then_inc(sem("warm"), 1)

            def expert0(q, r, parts=(0, 1, 2)):
                if 0 in parts:
                    act.wait_ge(sem("eT_ps"), q + 1)
                    if not isinstance(q, int) or q >= 2:
                        act.wait_ge(sem("eg_ps"), q - 1)
                    nc.scalar.activation(eT[:, r, :, :], bank[r][:, 0:DK * P].rearrange("p (k m) -> p k m", k=DK), ACT.Copy).then_inc(sem("eT"), 1)
                if 1 in parts and (not isinstance(q, int) or q >= 1):
                    act.wait_ge(sem("eg_ps"), q)
                    if not isinstance(q, int) or q >= 3:
                        act.wait_ge(sem("eh"), q - 2)
                    nc.scalar.activation(esg[:, 1 - r, :], bank[3 - r][:, 0:I], ACT.Silu).then_inc(sem("esg"), 1)
                if 2 in parts and (not isinstance(q, int) or q >= 2):
                    act.wait_ge(sem("ehT_ps"), q - 1)
                    if not isinstance(q, int) or q >= 4:
                        act.wait_ge(sem("ey_ps"), q - 3)
                    nc.scalar.activation(ehT[:, r, :], bank[4 + r][:, 0:P], ACT.Copy).then_inc(sem("ehT"), 1)

            for q in range(8):
                expert0(q, q % 2)
            with act.Fori(1, Q0 // 8) as t:
                for a in range(8):
                    expert0(t * 8 + a, a % 2)
            expert0(Q0, Q0 % 2, (1, 2))
            expert0(Q0 + 1, (Q0 + 1) % 2, (2,))

            def end_copy(n):
                if not isinstance(n, int) or n >= 1:
                    act.wait_ge(sem("xT_ps"), n)
                    act.wait_ge(sem("xs4"), n)
                act.sem_inc(sem("act_passed"), 1)
                nc.scalar.activation(xs4[:, :, :], xn[:, ds(n * 4, 4), 0:D], ACT.Copy).then_inc(sem("xs4"), 1)

            def end_xT(n):
                act.wait_ge(sem("xT_ps"), n + 1)
                if not isinstance(n, int) or n >= 1:
                    act.wait_ge(sem("gu4_ps"), n)
                for k in range(DK):
                    nc.scalar.activation(xT4[:, k, :], bank[k][:, :], ACT.Copy).then_inc(sem("xT4"), 1)

            def end_gelu(n):
                act.wait_ge(sem("zT_ps"), n + 1)
                if not isinstance(n, int) or n >= 1:
                    act.wait_ge(sem("o_ps"), n)
                for k in range(DK):
                    nc.scalar.activation(gT4[:, k, :], bank[k][:, :], ACT.Gelu, bias=cols[:, 2 + k:3 + k],
                                         scale=cols[:, k:k + 1]).then_inc(sem("gT4"), 1)

            def end_silu(n):
                act.wait_ge(sem("gu4_ps"), n + 1)
                if not isinstance(n, int) or n >= 1:
                    act.wait_ge(sem("hT4"), n)
                nc.scalar.activation(sl4[:, :], bank[2][:, :], ACT.Silu).then_inc(sem("sl4"), 1)

            def end_rows(n):
                act.wait_ge(sem("n4"), n + 1)
                act.sem_inc(sem("act_passed"), 1)
                nc.scalar.activation(xn[:, ds(n * 4, 4), 0:D], n4[:, :, :], ACT.Copy).then_inc(sem("xn1"), 1)

            def end_nT(n, b, r):
                for j in range(2):
                    act.wait_ge(sem("nT_ps"), n * 2 + (j + 1))
                    if not isinstance(n, int) or n >= 1:
                        act.wait_ge(sem("lg_ps"), n * 2 + (j - 1))
                        act.wait_ge(sem("nT"), n * 4)
                    act.sem_inc(sem("act_passed"), 1)
                    for k in range(DK):
                        nc.scalar.activation(nT[:, j, k, :], bank[6][:, k * 2 * P:(k + 1) * 2 * P], ACT.Copy,
                                             accum_out=xsum[:, k, ds(b, 1), 2 * r + j]).then_inc(sem("nT"), 1)

            def end_step(b, r, last=False):
                n = b * 2 + r
                if not last:
                    end_xT(n + 1)
                    end_gelu(n + 1)
                    end_silu(n + 1)
                if not isinstance(n, int) or n >= 1:
                    end_nT(n - 1, b - (1 - r), 1 - r)
                if not last and not (isinstance(n, int) and n == 2 * NB - 2):
                    end_copy(n + 2)
                end_rows(n)

            act.wait_ge(sem("cols_in"), 32)
            act.wait_ge(sem("ey_ps"), Q0)
            end_copy(0)
            end_xT(0)
            end_gelu(0)
            end_silu(0)
            end_copy(1)
            for r in range(2):
                end_step(0, r)
            with act.Fori(1, NB - 1) as b:
                for r in range(2):
                    end_step(b, r)
            for r in range(2):
                end_step(NB - 1, r, r == 1)
            end_nT(2 * NB - 1, NB - 1, 1)

            act.sem_inc(sem("hf"), 2)
            act.wait_ge(sem("b1_in"), 16)
            nc.scalar.activation(warm[:, :], part[:, :], ACT.Relu).then_inc(sem("warm"), 1)

            def high(n):
                act.wait_ge(sem("fT_ps"), n + 1)
                act.wait_ge(sem("h_ps"), n * HK)
                for k in range(DK):
                    nc.scalar.activation(fTh[:, k, :], bank[k][:, :], ACT.Copy).then_inc(sem("fTh"), 1)

            def hidden(e, n, j):
                m = n * HK + j
                act.wait_ge(sem("h_ps"), m + 1)
                act.wait_ge(sem("h_lo"), m + 1)
                act.sem_inc(sem("act_passed"), 1)
                nc.scalar.activation(hf[:, j % 2, :], bank[2 + j % 2][:, :], ACT.Relu, bias=b1c[:, ds(e, 1), j]).then_inc(sem("hf"), 1)

            act.wait_ge(sem("fT_ps"), 1)
            for k in range(DK):
                nc.scalar.activation(fTh[:, k, :], bank[k][:, :], ACT.Copy).then_inc(sem("fTh"), 1)

            def block2(e, jb, last=False):
                n = e * 4 + jb
                for j in range(HK):
                    hidden(e, n, j)
                if not last:
                    high(n + 1)

            with act.Fori(0, E - 1) as e:
                for jb in range(4):
                    block2(e, jb)
            for jb in range(4):
                block2(E - 1, jb, jb == 3)

            act.wait_ge(sem("sg_diff"), 1)
            nc.scalar.activation(gates1[:, :, 0], rdiff[:, :], ACT.Sigmoid, scale=-1.0).then_inc(sem("gates1"), 1)
            nc.scalar.activation(gates1[:, :, 1], rdiff[:, :], ACT.Sigmoid).then_inc(sem("gates1"), 1)

            def store(t, r):
                act.wait_ge(sem("oo"), t * 2 + (r + 1))
                act.dma_start(o_h[ds(t * 2 + r, 1)].rearrange("o p t d -> p (o t) d"), oo[:, r, :, :]).then_inc(sem(f"stored{r}"), 16)

            with act.Fori(0, NB) as t:
                for r in range(2):
                    store(t, r)
            for r in range(2):
                act.wait_ge(sem(f"stored{r}"), 16 * NB)

        @block.tensor
        def _(pe):
            pe.wait_ge(sem("consts"), 9)
            pe.wait_ge(sem("rw_in"), 16 * DK)
            NH2 = TB // 2

            def turn(b, h):
                n = b * NH2 + h
                if n >= 2:
                    pe.wait_ge(sem("xt_ready"), n - 1)
                if h == 0:
                    pe.wait_ge(sem("ln0_rows"), b + 1)
                for a in range(2):
                    for c in range(DK):
                        last = nc.tensor.transpose(bank[h % 2][:, (a * DK + c) * P:(a * DK + c + 1) * P],
                                                   nst[:, b % 2, 2 * h + a, c * P:(c + 1) * P], ident[:, :])
                last.then_inc(sem("tp_ready"), 1)

            def logit(b, h):
                pe.wait_ge(sem("xt_ready"), b * NH2 + h + 1)
                for a in range(2):
                    o = (b * TB + 2 * h + a) * E
                    for c in range(DK):
                        last = nc.tensor.matmul(bank[2][:, o:o + E], xt[:, h % 2, a, c, :], rw[:, c, :],
                                                start=(c == 0), stop=(c == DK - 1))
                last.then_inc(sem("xt_used"), 1)

            def ln_part(b, h):
                if h < NH2:
                    turn(b, h)
                if h:
                    logit(b, h - 1)
                if b == NB - 1 and h == NH2:
                    pe.wait_ge(sem("xt_used"), NB * NH2)
                    pe.sem_inc(sem("logits0"), 1)

            def double(n):
                lv, g0, gr = chunks[n]
                m = 1 << lv
                w = m + P
                if before(n):
                    pe.wait_ge(sem("u_done"), before(n))
                    pe.wait_ge(sem("v_done"), before(n))
                for side, mat, cols_, done in ((0, vb, ub, "u_ps"), (1, ub, vb, "v_ps")):
                    wm = m if side == 0 and lv == LV - 1 else w
                    for i in range(gr):
                        last = nc.tensor.matmul(bank[3 + 2 * (n % 2) + side][:, i * w:i * w + wm], mat[:, g0 + i, P:],
                                                cols_[:, g0 + i, P - m:P - m + wm], start=True, stop=True)
                    last.then_inc(sem(done), 1)

            pe.wait_ge(sem("state_in"), 48)
            nc.tensor.transpose(bank[7][:, 0:2 * NG], bcg[:, :], ident[0:2 * NG, 0:2 * NG]).then_inc(sem("bc_ps"), 1)
            pe.wait_ge(sem("a_bd"), 1)
            for c in range(NG // 4):
                if c >= 2:
                    pe.wait_ge(sem("at_bd"), c - 1)
                for g in range(4):
                    last = nc.tensor.transpose(bank[3 + c % 2][:, g * P:(g + 1) * P], ub[:, 4 * c + g, P:], ident[:, :])
                last.then_inc(sem("at_ps"), 1)
            pe.wait_ge(sem("bc"), 1)
            for g in range(NG):
                last = nc.tensor.matmul(bank[7][:, 2 * NG + g:2 * NG + g + 1], ub[:, g, P:], bc[:, NG + g:NG + g + 1], start=True, stop=True)
            last.then_inc(sem("v0"), 1)
            pe.wait_ge(sem("at_bd"), NG // 4)
            pe.wait_ge(sem("v_first"), 1)
            for what, i, h in plan:
                if what == "ln":
                    ln_part(i, h)
                    continue
                if i == RANKS_BEFORE:
                    pe.wait_ge(sem("chosen0"), 1)
                    nc.tensor.matmul(bank[0][:, :], tri[:, :], mb[:, :, :].rearrange("p a e -> p (a e)"), start=True, stop=True)
                    nc.tensor.matmul(bank[1][:, :], ones_b[:, :], mb[:, :, :].rearrange("p a e -> p (a e)"), start=True, stop=True).then_inc(sem("ranks0"), 1)
                double(i)
            for side in "uv":
                pe.wait_ge(sem(side + "_done"), len(chunks))
            pe.wait_ge(sem("v_half"), 2)
            for c in range(NG // 4):
                if c >= 2:
                    pe.wait_ge(sem("k_out"), c - 1)
                for g in range(4):
                    gg = 4 * c + g
                    last = nc.tensor.matmul(bank[3 + c % 2][0:CG, g * P:(g + 1) * P], bbd[:, gg, :], vv[:, gg, 1:P + 1], start=True, stop=True)
                last.then_inc(sem("k_ps"), 1)
            for c in range(NG // 4):
                if c >= 2:
                    pe.wait_ge(sem("pt"), c - 1)
                for g in range(4):
                    last = nc.tensor.transpose(bank[5 + c % 2][:, g * P:(g + 1) * P], ub[:, 4 * c + g, 0:P], ident[:, :])
                last.then_inc(sem("pt_ps"), 1)
            pe.wait_ge(sem("pt"), NG // 4)
            pe.wait_ge(sem("k_out"), NG // 4)
            pe.wait_ge(sem("xn_done"), NB)
            for g in range(NG):
                if g >= 4:
                    pe.wait_ge(sem("g_used"), g - 3)
                nc.tensor.matmul(bank[3 + g % 4][:, :].rearrange("p (t c) -> p t c", c=CG), pt[:, g, :], xn[:, :, g * CG:(g + 1) * CG],
                                 start=True, stop=True).then_inc(sem("g_ps"), 1)
            pe.wait_ge(sem("g_used"), NG)
            pe.wait_ge(sem("gt"), NG)
            for c in range(TB - 1):
                pe.wait_ge(sem("states"), c + 1)
                nc.tensor.matmul(bank[5][:, 0:NG * NB].rearrange("p (g b) -> p g b", g=NG), ident[:, :],
                                 gt.rearrange("p g (b t) -> p g b t", b=NB)[:, :, :, c], start=True, stop=False, skip_group_check=True)
                for g in range(NG):
                    last = nc.tensor.matmul(bank[5][:, g * NB:(g + 1) * NB], vb[:, g, P:], hs[:, g, :, c],
                                            start=False, stop=(g == NG - 1), skip_group_check=True)
                last.then_inc(sem("step_ps"), 1)
            def out_pair(u, h2):
                t = u * 2 + h2
                for r in range(2):
                    pe.wait_ge(sem("vst"), t * 2 + (r + 1))
                    pe.wait_ge(sem("hb"), t * 2 + (r + 1))
                    if not isinstance(t, int) or t:
                        pe.wait_ge(sem("y_done"), t * 2 + (r - 1))
                    nc.tensor.matmul(bank[6 + r][:, :], vst[:, r, :], hb[:, r, :, :].rearrange("p l i -> p (l i)"),
                                     start=True, stop=False, skip_group_check=True)
                    pe.wait_ge(sem(f"th_in{2 * h2 + r}"), u * 16 + 16)
                    for l in range(CG):
                        last = nc.tensor.matmul(bank[6 + r][:, l * NT:(l + 1) * NT], th[:, 2 * h2 + r, l, :],
                                                xn[:, :, ds(t * 2 * CG + (r * CG + l), 1)].rearrange("p i o -> p (i o)"),
                                                start=False, stop=(l == CG - 1), skip_group_check=True)
                    last.then_inc(sem("y_ps"), 1)

            for h2 in range(2):
                out_pair(0, h2)
            with pe.Fori(1, NG // TR) as u:
                for h2 in range(2):
                    out_pair(u, h2)

            pe.wait_ge(sem("wraw_in"), 48)
            for j in range(3):
                for kd in range(DK):
                    for ko in range(DK):
                        last = nc.tensor.transpose(bank[j][:, kd * D + ko * P:kd * D + (ko + 1) * P],
                                                   wraw[:, j, ko, kd * P:(kd + 1) * P], ident[:, :])
                last.then_inc(sem("wT_ps"), 1)
            pe.wait_ge(sem("wT"), 3)
            pe.wait_ge(sem("y_done"), NG)
            pe.wait_ge(sem("wgu_in"), 32)
            pe.wait_ge(sem("wdn_in"), 16)

            def expert_registers(name):
                regs = [pe.alloc_register(f"{name}{i}") for i in range(3 + 8)]

                def read(t, a):
                    pe.reg_load(regs[a + 3], tile_e[0:1, ds(t * 8 + a, 1)])

                def value(a):
                    return bass.RuntimeValue.of_register_unchecked(regs[a + 3], min_val=0, max_val=E - 1)

                return regs, read, value

            def turn0(q, a, w):
                r = a % 2
                if a % 4 == 0:
                    pe.wait_ge(sem(f"er_in{a // 4}"), w)
                if not isinstance(q, int) or q >= 2:
                    pe.wait_ge(sem("eT"), q - 1)
                for k in range(DK):
                    last = nc.tensor.transpose(bank[r][:, k * P:(k + 1) * P], er[:, a // 4, a % 4, k * P:(k + 1) * P], ident[:, :])
                last.then_inc(sem("eT_ps"), 1)

            def up0(q, r, e):
                pe.wait_ge(sem("eT"), q + 1)
                if not isinstance(q, int) or q >= 2:
                    pe.wait_ge(sem("eh"), q - 1)
                for k in range(DK):
                    w = wgu[:, :, :].rearrange("p (e k) i -> p e (k i)", k=DK)[:, ds(e, 1), k * 2 * I:(k + 1) * 2 * I]
                    last = nc.tensor.matmul(bank[2 + r][:, 0:2 * I], eT[:, r, k, :], w.rearrange("p o i -> p (o i)"),
                                            start=(k == 0), stop=(k == DK - 1))
                last.then_inc(sem("eg_ps"), 1)

            def back0(q, r):
                pe.wait_ge(sem("eh"), q + 1)
                if not isinstance(q, int) or q >= 2:
                    pe.wait_ge(sem("ehT"), q - 1)
                nc.tensor.transpose(bank[4 + r][:, 0:P], eh[:, r, :], ident[:, :]).then_inc(sem("ehT_ps"), 1)

            def down0(q, r, e):
                pe.wait_ge(sem("ehT"), q + 1)
                if not isinstance(q, int) or q >= 2:
                    pe.wait_ge(sem("ey"), q - 1)
                nc.tensor.matmul(bank[6 + r][:, 0:D], ehT[:, r, :], wdn[:, ds(e, 1), :].rearrange("p o d -> p (o d)"),
                                 start=True, stop=True).then_inc(sem("ey_ps"), 1)

            def eight(t, first=False):
                regs, read_expert, expert_of = expert_registers("first_expert" if first else "expert")
                if not first:
                    read_expert(t, -1)
                for a in range(8):
                    q = t * 8 + a
                    if not first or a >= 1:
                        up0(q - 1, (a + 1) % 2, expert_of(a - 1))
                    if a < 2 and not first:
                        read_expert(t, a - 3)
                    read_expert(t, a)
                    turn0(q, a, t * 16 + 16)
                    if not first or a >= 2:
                        back0(q - 2, a % 2)
                    if not first or a >= 3:
                        down0(q - 3, (a + 1) % 2, expert_of(a - 3))
                for reg in regs:
                    pe.free_register(reg)

            eight(0, True)
            with pe.Fori(1, Q0 // 8) as t:
                eight(t)
            regs, read_expert, expert_of = expert_registers("last_expert")
            for a in (-3, -2, -1):
                read_expert(Q0 // 8, a)
            up0(Q0 - 1, 1, expert_of(-1))
            back0(Q0 - 2, 0)
            down0(Q0 - 3, 1, expert_of(-3))
            back0(Q0 - 1, 1)
            down0(Q0 - 2, 0, expert_of(-2))
            down0(Q0 - 1, 1, expert_of(-1))
            for reg in regs:
                pe.free_register(reg)

            def end_turn(n, src, turned, ready, free, freed, done):
                pe.wait_ge(sem(ready), n + 1)
                if free:
                    pe.wait_ge(sem(free), freed)
                for k in range(DK):
                    for a in range(4):
                        o, rows_ = bank[k][:, a * P:(a + 1) * P], src[:, a, k * P:(k + 1) * P]
                        if turned is ident:
                            last = nc.tensor.transpose(o, rows_, ident[:, :])
                        else:
                            last = nc.tensor.matmul(o, rows_, turned[:, :], start=True, stop=True)
                last.then_inc(sem(done), 1)

            def end_gu(n):
                pe.wait_ge(sem("xT4"), n * 2 + 2)
                if not isinstance(n, int) or n >= 1:
                    pe.wait_ge(sem("hT4"), n)
                for j in range(2):
                    for k in range(DK):
                        last = nc.tensor.matmul(bank[2 + j][:, :], sgu[:, k, j * I:(j + 1) * I], xT4[:, k, :], start=(k == 0), stop=(k == DK - 1))
                last.then_inc(sem("gu4_ps"), 1)

            def end_out(n):
                pe.wait_ge(sem("gT4"), n * 2 + 2)
                pe.wait_ge(sem("hT4"), n + 1)
                if not isinstance(n, int) or n >= 1:
                    pe.wait_ge(sem("x1_sum"), n)
                for a in range(4):
                    o = bank[4 + a // 2][:, (a % 2) * D:(a % 2 + 1) * D]
                    nc.tensor.matmul(o, one_r[:, :], bo_r[:, :], start=True, stop=False)
                    for k in range(DK):
                        nc.tensor.matmul(o, gT4[:, k, a * P:(a + 1) * P], woT[:, k, :], start=False, stop=False)
                    last = nc.tensor.matmul(o, hT4[:, a * P:(a + 1) * P], sdn[:, :], start=False, stop=True)
                last.then_inc(sem("o_ps"), 1)

            def end_router(n, b, r):
                for j in range(2):
                    pe.wait_ge(sem("n4"), n + 1)
                    if not isinstance(n, int) or n or j:
                        pe.wait_ge(sem("nT"), n * 4 + 2 * j)
                    for k in range(DK):
                        for a in range(2):
                            last = nc.tensor.transpose(bank[6][:, (2 * k + a) * P:(2 * k + a + 1) * P], n4[:, 2 * j + a, k * P:(k + 1) * P], ident[:, :])
                    last.then_inc(sem("nT_ps"), 1)
                    pe.wait_ge(sem("nT"), n * 4 + (2 * j + 2))
                    if j == 0 and not (isinstance(b, int) and b == 0):
                        pe.wait_ge(sem("slot1" if r else "lg1"), b)
                    for a in range(2):
                        o = (4 * r + 2 * j + a) * E
                        for k in range(DK):
                            last = nc.tensor.matmul(bank[7][:, o:o + E], nT[:, j, k, a * P:(a + 1) * P], wg1[:, k, :], start=(k == 0), stop=(k == DK - 1))
                    last.then_inc(sem("lg_ps"), 1)

            def end_ranks(b):
                pe.wait_ge(sem("mb1"), b + 1)
                mm = mb1[:, :, :, :].rearrange("p k t e -> p (k t e)")
                w = 2 * TB * E
                nc.tensor.matmul(bank[7][:, P:P + w], tri[:, :], mm, start=True, stop=True)
                nc.tensor.matmul(bank[7][:, P + w:P + 2 * w], ones_b[:, :], mm, start=True, stop=True).then_inc(sem("rk_ps"), 1)

            def end_step(b, r, last=False):
                n = b * 2 + r
                if not last:
                    end_turn(n + 1, xs4, ident, "xs4", "gT4", n * 2 + 2, "xT_ps")
                end_out(n)
                if not last:
                    end_turn(n + 1, z4, flip, "z4", "xT4", n * 2 + 4, "zT_ps")
                    end_gu(n + 1)
                if not isinstance(n, int) or n >= 1:
                    end_router(n - 1, b - (1 - r), 1 - r)
                if r and not (isinstance(b, int) and b == 0):
                    end_ranks(b - 1)

            pe.wait_ge(sem("shared_in"), 64)
            pe.wait_ge(sem("wg1_in"), 16)
            pe.wait_ge(sem("bo_r"), 1)
            pe.wait_ge(sem("ey"), Q0)
            end_turn(0, xs4, ident, "xs4", None, 0, "xT_ps")
            end_turn(0, z4, flip, "z4", "xT4", 2, "zT_ps")
            end_gu(0)
            for r in range(2):
                end_step(0, r)
            with pe.Fori(1, NB - 1) as b:
                for r in range(2):
                    end_step(b, r)
            for r in range(2):
                end_step(NB - 1, r, r == 1)
            end_router(2 * NB - 1, NB - 1, 1)
            end_ranks(NB - 1)

            pe.wait_ge(sem("xtot"), 1)
            for m in range(DK):
                for k in range(DK):
                    last = nc.tensor.matmul(bank[4][:, m * NB:(m + 1) * NB], wvT[:, k, m * P:(m + 1) * P], xtot[:, k, :],
                                            start=(k == 0), stop=(k == DK - 1))
            last.then_inc(sem("val_ps"), 1)
            pe.wait_ge(sem("vrep"), 1)
            for b in range(NB):
                if b >= 2:
                    pe.wait_ge(sem("att_add"), b - 1)
                for k in range(DK):
                    last = nc.tensor.matmul(bank[5 + b % 2][:, 0:D], vrep[:, k, b, :], waT[:, k, :], start=(k == 0), stop=(k == DK - 1))
                last.then_inc(sem("att_ps"), 1)

            def turn2(n, r, w):
                pe.wait_ge(sem(f"fr_in{r}"), w)
                pe.wait_ge(sem("fTl"), n * 2 + 2)
                for k in range(DK):
                    for a in range(4):
                        last = nc.tensor.transpose(bank[k][:, a * P:(a + 1) * P], fr[:, r, a, k * P:(k + 1) * P], ident[:, :])
                last.then_inc(sem("fT_ps"), 1)

            def up2(e, n, r):
                pe.wait_ge(sem("w_split"), e * 4 + 2)
                pe.wait_ge(sem("fTl"), n * 2 + 4)
                for j in range(HK):
                    pe.wait_ge(sem("hf"), n * HK + (j + 1))
                    o, w = bank[2 + j % 2], j * P
                    first = True
                    for k in range(DK):
                        for wt, xx in ((w1h, fTh), (w1l, fTh), (w1h, fTl)):
                            last = nc.tensor.matmul(o[:, :], wt[:, r, k, w:w + P], xx[:, k, :], start=first, stop=(k == DK - 1 and xx is fTl))
                            first = False
                    last.then_inc(sem("h_ps"), 1)

            def down2(e, n, r, par):
                pe.wait_ge(sem("w_split"), e * 4 + 4)
                pe.wait_ge(sem("fy_free"), n + 1)
                for j in range(HK):
                    pe.wait_ge(sem("h_lo"), n * HK + (j + 3))
                    for a in range(4):
                        o = bank[4 + 2 * par + a // 2][:, (a % 2) * D:(a % 2 + 1) * D]
                        hh, hl = hTh[:, j, a * P:(a + 1) * P], hTl[:, j, a * P:(a + 1) * P]
                        for i, (x, y) in enumerate(((hh, w2h), (hh, w2l), (hl, w2h))):
                            last = nc.tensor.matmul(o, x, y[:, r, j, :], start=(j == 0 and i == 0 and a % 2 == 0),
                                                    stop=(j == HK - 1 and i == 2), skip_group_check=True)
                last.then_inc(sem("f_ps"), 1)

            def block2(e, eh2, r, jb, last=False):
                n = e * 4 + jb
                up2(e, n, r)
                if not last:
                    turn2(n + 1, (jb + 1) % 2, e * 32 + 16 * ((jb + 1) // 2 + 1))
                down2(e, n, r, jb % 2)

            pe.wait_ge(sem("att_add"), NB)
            turn2(0, 0, 16)
            with pe.Fori(0, E // 2 - 1) as t:
                for r in range(2):
                    for jb in range(4):
                        block2(t * 2 + r, None, r, jb)
            for r in range(2):
                for jb in range(4):
                    block2(E - 2 + r, None, r, jb, r == 1 and jb == 3)

        @block.vector
        def _(dve):
            v = nc.vector
            for r in range(2):
                dve.sem_inc(sem(f"x_free{r}"), 1)
            st = Steps(dve, sem("dve_steps"))
            dve.wait_ge(sem("consts"), 9)

            dve.wait_ge(sem("state_in"), 48)
            w = st
            full = [P, NG, CG, ST]
            w.run(v.tensor_tensor(ub[:, :, P:].rearrange("p g (l m) -> p g l m", l=CG), a_in.unsqueeze(2).broadcast_to(full),
                                  mask8[:, :].unsqueeze(1).unsqueeze(3).broadcast_to(full), ALU.mult))
            dve.sem_inc(sem("a_bd"), 1)
            dve.wait_ge(sem("bc_ps"), 1)
            w.run(v.tensor_copy(bc[:, :], bank[7][:, 0:2 * NG]))
            w.mark(v.tensor_copy(ub[:, :, P - 1], bc[:, 0:NG]))
            fb = [P, NG, CG]
            w.run(v.tensor_tensor(bbd[:, :, :], bc[:, 0:NG].unsqueeze(2).broadcast_to(fb), mask8[:, :].unsqueeze(1).broadcast_to(fb), ALU.mult))
            dve.sem_inc(sem("bc"), 1)

            def ln_stats(b):
                r = b % 2
                dve.wait_ge(sem(f"x_in{r}"), b // 2 * 16 + 16)
                for j in range(TB):
                    st.mark(v.bn_stats(bst[:, r, j, :], xl[:, r, j, :]))
                st.settle()
                for j in range(TB):
                    st.mark(v.bn_aggr(mv[:, r, j, :], bst[:, r, j, :]))
                st.settle()
                st.run(v.tensor_scalar(vare[:, r, :], mv[:, r, :, 1], EPS, None, ALU.add))
                dve.sem_inc(sem("ln0_var"), 1)

            def ln_rows(b):
                r = b % 2
                dve.wait_ge(sem("ln0_rstd"), b + 1)
                if b >= 2:
                    dve.wait_ge(sem("tp_ready"), (b - 1) * (TB // 2))
                    dve.wait_ge(sem("xn_done"), b - 1)
                for j in range(TB):
                    st.mark(v.tensor_scalar(nst[:, r, j, :], xl[:, r, j, :], mv[:, r, j, 0:1], rstd[:, r, j:j + 1],
                                            ALU.subtract, ALU.mult))
                st.settle()
                dve.sem_inc(sem("ln0_rows"), 1)
                dve.sem_inc(sem(f"x_free{r}"), 1)

            def store_chunk(n):
                lv, g, gr = chunks[n]
                m = 1 << lv
                ps = bank[3 + 2 * (n % 2)][:, 0:gr * (m + P)].rearrange("p (g w) -> p g w", g=gr)
                dve.wait_ge(sem("u_ps"), n + 1)
                last = v.tensor_copy(ub[:, g:g + gr, P - 2 * m:P - m], ps[:, :, 0:m])
                if lv < LV - 1:
                    dve.wait_ge(sem("v_ps"), n + 1)
                    last = v.tensor_copy(ub[:, g:g + gr, P:], ps[:, :, m:])
                last.then_inc(sem("u_done"), 1)

            c = st
            sg, sc, t2, t3, t4, t5, t6 = rt
            G2 = E // 2
            H2 = G2 // 2

            def bce(ap):
                return ap.unsqueeze(1).broadcast_to([P, NT, E])

            def bct(ap):
                return ap.unsqueeze(2).broadcast_to([P, NT, E])

            def first_max(m, oh, tmp, val, key):
                c.run(v.reduce_max(val, m, AX.X))
                yield
                c.run(v.tensor_tensor(tmp, m, bct(val), ALU.is_equal))
                yield
                c.run(v.tensor_tensor(tmp, tmp, bce(w8[:, :]), ALU.mult))
                yield
                c.run(v.reduce_max(key, tmp, AX.X))
                yield
                c.run(v.tensor_tensor(oh, bce(w8[:, :]), bct(key), ALU.is_equal))
                yield

            chosen = []

            def routing():
                dve.wait_ge(sem("xn_done"), NB)
                dve.wait_ge(sem("sig0"), 1)
                dve.wait_ge(sem("cb_in"), 16)
                c.run(v.tensor_tensor(sc[:, :, :], sg[:, :, :], bce(cb[:, :]), ALU.add))
                yield
                pair = sc[:, :, :].rearrange("p t (g h k) -> p (t g) h k", g=2, h=H2)
                hi = t2[:, :, :].rearrange("p t (g h k) -> p (t g) h k", g=2, h=H2)
                c.mark(v.tensor_tensor(hi[:, :, :, 0], pair[:, :, :, 0], pair[:, :, :, 1], ALU.max))
                c.run(v.tensor_tensor(hi[:, :, :, 1], pair[:, :, :, 0], pair[:, :, :, 1], ALU.min))
                yield
                a, b, d_, e_ = r1[0], r1[1], r1[2], r1[3]
                fl = "p t g -> p (t g)"
                c.mark(v.tensor_tensor(a[:, :, :].rearrange(fl), hi[:, :, 0, 0], hi[:, :, 1, 0], ALU.max))
                c.mark(v.tensor_tensor(b[:, :, :].rearrange(fl), hi[:, :, 0, 0], hi[:, :, 1, 0], ALU.min))
                c.run(v.tensor_tensor(d_[:, :, :].rearrange(fl), hi[:, :, 0, 1], hi[:, :, 1, 1], ALU.max))
                yield
                c.run(v.tensor_tensor(b[:, :, :], b[:, :, :], d_[:, :, :], ALU.max))
                yield
                c.run(v.tensor_tensor(a[:, :, :], a[:, :, :], b[:, :, :], ALU.add))
                yield
                c.run(v.tensor_tensor(e_[:, :, 0], a[:, :, 0], a[:, :, 1], ALU.is_ge))
                yield
                c.run(v.tensor_scalar(e_[:, :, 1], e_[:, :, 0], -1.0, 1.0, ALU.mult, ALU.add))
                yield
                c.run(v.tensor_tensor(t3[:, :, :].rearrange("p t (g k) -> p (t g) k", g=2), sc[:, :, :].rearrange("p t (g k) -> p (t g) k", g=2),
                                      e_[:, :, :].rearrange(fl).unsqueeze(2).broadcast_to([P, 2 * NT, G2]), ALU.mult))
                yield
                oh0, oh1 = t4, t5
                top, key = r1[4][:, :, 0], r1[4][:, :, 1]
                yield from first_max(t3[:, :, :], oh0[:, :, :], t6[:, :, :], top, key)
                c.run(v.scalar_tensor_tensor(out=t3[:, :, :], in0=oh0[:, :, :], scalar=-BIG, in1=t3[:, :, :], op0=ALU.mult, op1=ALU.add))
                yield
                yield from first_max(t3[:, :, :], oh1[:, :, :], t6[:, :, :], top, key)
                c.run(v.tensor_scalar(xn[:, :, D + 1], key, -1.0, float(E), ALU.mult, ALU.add))
                yield
                c.run(v.tensor_tensor(mb[:, :, :], oh0[:, :, :], oh1[:, :, :], ALU.add))
                yield
                dve.sem_inc(sem("chosen0"), 1)
                chosen.append(True)
                for k, oh in enumerate((oh0, oh1)):
                    c.run(v.tensor_tensor(t6[:, :, :], oh[:, :, :], sg[:, :, :], ALU.mult))
                    yield
                    c.run(v.tensor_reduce(r1[5][:, :, k], t6[:, :, :], AX.X, ALU.add))
                    yield
                c.run(v.tensor_tensor(a[:, :, 0], r1[5][:, :, 0], r1[5][:, :, 1], ALU.add))
                yield
                c.run(v.tensor_scalar(a[:, :, 0], a[:, :, 0], 1e-20, None, ALU.add))
                yield
                c.run(v.reciprocal(a[:, :, 1], a[:, :, 0]))
                yield
                for k in range(2):
                    c.run(v.tensor_tensor(gates[:, :, k], r1[5][:, :, k], a[:, :, 1], ALU.mult))
                    yield
                dve.wait_ge(sem("ranks0"), 1)
                tot, run, one = t2, t3, sc
                et = "p (e t) -> p e t"

                def flat(x):
                    return x[:, :, :].rearrange("p t e -> p (t e)")

                c.run(v.tensor_copy(flat(tot).rearrange(et, e=E), view(1, "p (t e) -> p e t", e=E)))
                yield
                c.run(v.memset(flat(one), 1.0))
                yield
                c.run(v.memset(flat(one).rearrange(et, e=E)[:, :, 0], 0.0))
                yield
                c.run(v.tensor_tensor_scan(out=flat(run), data0=flat(one), data1=flat(tot), initial=0.0, op0=ALU.mult, op1=ALU.add))
                yield
                cnt, tiles, ends, starts, tmp8, base8 = se
                c.run(v.tensor_copy(cnt[:, :], flat(run).rearrange(et, e=E)[:, :, NT - 1]))
                yield
                c.run(v.tensor_tensor(flat(run), flat(run), flat(tot), ALU.subtract))
                yield
                dve.wait_ge(sem("iotas"), 4)
                c.run(v.tensor_tensor(flat(tot).rearrange(et, e=E), cnt[:, :].unsqueeze(2).broadcast_to([P, E, NT]),
                                      i64[:, :].unsqueeze(1).broadcast_to([P, E, NT]), ALU.is_gt))
                yield
                c.run(v.tensor_reduce(tiles[:, :], flat(tot).rearrange(et, e=E), AX.X, ALU.add))
                yield
                c.run(v.memset(tmp8[:, :], 1.0))
                yield
                c.run(v.tensor_tensor_scan(out=ends[:, :], data0=tmp8[:, :], data1=tiles[:, :], initial=0.0, op0=ALU.mult, op1=ALU.add))
                yield
                c.run(v.tensor_tensor(starts[:, :], ends[:, :], tiles[:, :], ALU.subtract))
                yield
                c.run(v.tensor_scalar(base8[:, :], starts[:, :], float(P), None, ALU.mult))
                yield
                c.run(v.tensor_tensor(t6[:, :, :], view(0, "p (t e) -> p t e", e=E), flat(run).rearrange("p (e t) -> p t e", e=E), ALU.add))
                yield
                c.run(v.tensor_tensor(t6[:, :, :], t6[:, :, :], bce(base8[:, :]), ALU.add))
                yield
                for k, oh in enumerate((oh0, oh1)):
                    c.run(v.tensor_tensor(oh[:, :, :], oh[:, :, :], t6[:, :, :], ALU.mult))
                    yield
                    c.run(v.tensor_reduce(r1[5][:, :, k], oh[:, :, :], AX.X, ALU.add))
                    yield
                c.run(v.tensor_copy(slot_u[:, :, :], r1[5][:, :, :]))
                yield
                dve.sem_inc(sem("routed0"), 1)
                qe = [P, Q0, E]
                c.run(v.tensor_tensor(q8[:, :, :], iq[:, :].unsqueeze(2).broadcast_to(qe), ends[:, :].unsqueeze(1).broadcast_to(qe), ALU.is_ge))
                yield
                c.run(v.tensor_reduce(ef[:, :], q8[:, :, :], AX.X, ALU.add))
                yield
                c.run(v.tensor_scalar(ef[:, :], ef[:, :], float(E - 1), None, ALU.min))
                yield
                c.run(v.tensor_copy(tile_e[:, :], ef[0:1, :]))
                yield
                c.run(v.tensor_tensor(tmp8[:, :], cnt[:, :], base8[:, :], ALU.add))
                yield
                c.run(v.tensor_tensor(q8[:, :, :], ef[:, :].unsqueeze(2).broadcast_to(qe), iota8[:, :].unsqueeze(1).broadcast_to(qe), ALU.is_equal))
                yield
                c.run(v.tensor_tensor(q8[:, :, :], q8[:, :, :], tmp8[:, :].unsqueeze(1).broadcast_to(qe), ALU.mult))
                yield
                c.run(v.tensor_reduce(nvq[:, :], q8[:, :, :], AX.X, ALU.add))
                yield
                c.run(v.tensor_tensor(nvq[:, :], nvq[:, :], iq128[:, :], ALU.subtract))
                yield
                c.run(v.tensor_scalar(vq[:, :], nvq[:, :], part[:, 0:1], None, ALU.is_gt))
                yield
                c.run(v.tensor_tensor(tq[:, :], vq[:, :], trq[:, :], ALU.mult))
                yield
                c.run(v.tensor_tensor(tq[:, :], trq[:, :], tq[:, :], ALU.subtract))
                yield
                dve.sem_inc(sem("routed0"), 1)

            ln_stats(0)
            ln_rows(0)
            ln_stats(1)
            steps = routing()
            for what, i, h in plan:
                if what == "ln":
                    continue
                lv, c_ = chunks[i][0], i - level(chunks[i][0])[0][0]
                if i == RANKS_BEFORE:
                    while not chosen:
                        next(steps)
                store_chunk(i)
                if 2 * lv < NB:
                    if c_ == 2:
                        ln_rows(2 * lv + 1)
                    if 2 * lv + 2 < NB:
                        if c_ == 4:
                            ln_stats(2 * lv + 2)
                        if c_ == 8:
                            ln_rows(2 * lv + 2)
                        if c_ == 9:
                            ln_stats(2 * lv + 3)
                else:
                    for _ in range(2):
                        next(steps, None)
            for _ in steps:
                pass
            dve.wait_ge(sem("k_out"), NG // 4)
            dve.wait_ge(sem("dcg_in"), 16)
            v.tensor_tensor(kev[:, :, P - 1], kev[:, :, P - 1], dcg[:, :], ALU.add).then_inc(sem("kernels"), 1)
            for g in range(NG + 1):
                if g < NG:
                    dve.wait_ge(sem("g_ps"), g + 1)
                    if g >= 2:
                        dve.wait_ge(sem("gt"), g - 1)
                    v.tensor_tensor(gm[:, g % 2, :, :], bank[3 + g % 4][:, :].rearrange("p (t c) -> p t c", c=CG),
                                    mask8[:, :].unsqueeze(1).broadcast_to([P, NT, CG]), ALU.mult).then_inc(sem("g_used"), 1)
                if g >= 1:
                    dve.wait_ge(sem("g_used"), g)
                    v.tensor_reduce(gt[:, g - 1, :], gm[:, (g - 1) % 2, :, :], AX.X, ALU.add).then_inc(sem("gt"), 1)

            dve.wait_ge(sem("states"), TB)
            def spread(t):
                for r in range(2):
                    if not isinstance(t, int):
                        dve.wait_ge(sem("y_ps"), t * 2 + (r - 1))
                    sh = [P, CG, NT]
                    v.tensor_tensor(hb[:, r, :, :], hs[:, ds(t * 2 + r, 1), :, :].rearrange("p o b t -> p o (b t)").broadcast_to(sh),
                                    mask8[:, :].unsqueeze(2).broadcast_to(sh), ALU.mult).then_inc(sem("hb"), 1)

            spread(0)
            with dve.Fori(1, NG // 2) as t:
                spread(t)

            for j, w in enumerate((woT, wvT, waT)):
                dve.wait_ge(sem("wT_ps"), j + 1)
                v.tensor_copy(w[:, :, :].rearrange("p k d -> p (k d)"), bank[j][:, :]).then_inc(sem("wT"), 1)

            z = st

            def numbers(u, r, t):
                z.run(v.tensor_tensor(idx[:, :], er[:, r, :, D + 1], ef[:, ds(u * 4, 4)], ALU.is_equal))
                z.run(v.tensor_tensor(idx[:, :], idx[:, :], er[:, r, :, D], ALU.add))
                dve.sem_inc(sem("e_idx"), 1)
                z.run(v.tensor_tensor(idx[:, :], idx[:, :], vq[:, ds(u * 4, 4)], ALU.mult))
                z.run(v.tensor_tensor(eidx[:, r, :, 0], idx[:, :], tq[:, ds(u * 4, 4)], ALU.add))
                dve.sem_inc(sem("e_idxu"), 1)

            def expert0(q, a, t, parts=(0, 1)):
                loop = not isinstance(q, int)
                r = a % 2
                if 0 in parts:
                    dve.wait_ge(sem("esg"), q + 1)
                    if loop or q >= 2:
                        dve.wait_ge(sem("ehT_ps"), q - 1)
                    v.tensor_tensor(eh[:, r, :], bank[2 + r][:, I:2 * I], esg[:, r, :], ALU.mult).then_inc(sem("eh"), 1)
                if 1 in parts and (loop or q >= 2):
                    b = (a - 2) % 8
                    half, u = b // 4, (t - 1 if a < 2 else t) * 2 + b // 4
                    if b % 4 == 0:
                        dve.wait_ge(sem(f"er_in{half}"), t * 16 + 16)
                        if loop:
                            dve.wait_ge(sem(f"e_out{half}"), t * 64)
                        numbers(u, half, t)
                    dve.wait_ge(sem("ey_ps"), q - 1)
                    v.tensor_copy(ey[:, half, b % 4, :], bank[6 + r][:, 0:D]).then_inc(sem("ey"), 1)

            for q in range(8):
                expert0(q, q, 0)
            with dve.Fori(1, Q0 // 8) as t:
                z.enter(t, 8, 1)
                for a in range(8):
                    expert0(t * 8 + a, a, t)
            z.leave(Q0 // 8 - 1)
            for a in range(2):
                expert0(Q0 + a, a, Q0 // 8, (1,))

            y = st

            def row(n, a):
                return yb[:, ds(n * 4 + a, 1), :].rearrange("p o d -> p (o d)")

            def stats(k, n):
                for a in range(4):
                    y.mark(v.bn_stats(est[:, a, :], row(n, a)))
                y.settle()
                dve.sem_inc(sem("dve_passed"), 1)
                for a in range(4):
                    y.mark(v.bn_aggr(emv[:, a, :], est[:, a, :]))
                y.settle()
                y.run(v.tensor_scalar(evar[:, k, :], emv[:, :, 1], EPS, None, ALU.add))
                dve.sem_inc(sem(("z_var", "x1_var")[k]), 1)

            def norm(k, n, dst):
                dve.wait_ge(sem(("z_rstd", "x1_rstd")[k]), n + 1)
                if not isinstance(n, int) or n >= 1:
                    if k == 0:
                        dve.wait_ge(sem("zT_ps"), n)
                    else:
                        dve.wait_ge(sem("nT_ps"), n * 2)
                        dve.wait_ge(sem("xn1"), n)
                for a in range(4):
                    y.mark(v.tensor_scalar(dst[:, a, :], row(n, a), emv[:, a, 0:1], erstd[:, k, a:a + 1], ALU.subtract, ALU.mult))
                y.settle()
                dve.sem_inc(sem(("z4", "n4")[k]), 1)

            def end_hidden(n):
                dve.wait_ge(sem("sl4"), n + 1)
                if not isinstance(n, int) or n >= 1:
                    dve.wait_ge(sem("o_ps"), n)
                v.tensor_tensor(hT4[:, :], sl4[:, :], bank[3][:, :], ALU.mult).then_inc(sem("hT4"), 1)

            def end_experts(n, b, r):
                dve.wait_ge(sem("xg_sum"), n + 1)
                dve.wait_ge(sem(f"yl_in{r}"), b * 16 + 16)
                for k in range(2):
                    for a in range(4):
                        y.mark(v.scalar_tensor_tensor(out=xg[:, a, :], in0=yl[:, r, a, k, :], scalar=gates[:, ds(n * 4 + a, 1), k],
                                                      in1=xg[:, a, :], op0=ALU.mult, op1=ALU.add))
                    y.settle()

            def end_sum(n):
                dve.wait_ge(sem("o_ps"), n + 1)
                for h in range(2):
                    y.mark(v.tensor_tensor(yb[:, ds(n * 4 + 2 * h, 2), :].rearrange("p a d -> p (a d)"),
                                           xg[:, 2 * h:2 * h + 2, :].rearrange("p a d -> p (a d)"), bank[4 + h][:, :], ALU.add))
                y.settle()
                dve.sem_inc(sem("x1_sum"), 1)

            s3 = [P, TB, E]

            def be(ap):
                return ap.unsqueeze(1).broadcast_to(s3)

            def bt(ap):
                return ap.unsqueeze(2).broadcast_to(s3)

            def pick(m, oh, tmp, val, key):
                y.run(v.reduce_max(val, m, AX.X))
                y.run(v.tensor_tensor(tmp, m, bt(val), ALU.is_equal))
                y.run(v.tensor_tensor(tmp, tmp, be(w8[:, :]), ALU.mult))
                y.run(v.reduce_max(key, tmp, AX.X))
                y.run(v.tensor_tensor(oh, be(w8[:, :]), bt(key), ALU.is_equal))

            o0, o1, qa, qb, qc, qd = (x[:, :, :] for x in q1[0:6])
            v0, v1, key0, key1, ps0, va = (x[:, :] for x in k1[0:6])

            def end_choose(b):
                dve.wait_ge(sem("lg_ps"), b * 4 + 4)
                y.run(v.tensor_copy(lg1[:, :, :].rearrange("p t e -> p (t e)"), bank[7][:, 0:TB * E]))
                dve.sem_inc(sem("lg1"), 1)
                pick(lg1[:, :, :], o0, qa, v0, key0)
                y.run(v.scalar_tensor_tensor(out=lg1[:, :, :], in0=o0, scalar=-BIG, in1=lg1[:, :, :], op0=ALU.mult, op1=ALU.add))
                pick(lg1[:, :, :], o1, qa, v1, key1)
                y.mark(v.tensor_tensor(rdiff[:, ds(b * TB, TB)], v1, v0, ALU.subtract))
                y.mark(v.tensor_copy(oh1s[:, ds(b * TB, TB), :], o1))
                y.mark(v.tensor_copy(key1s[:, ds(b * TB, TB)], key1))
                y.mark(v.tensor_copy(mb1[:, 0, :, :], o0))
                y.run(v.tensor_copy(mb1[:, 1, :, :], o1))
                dve.sem_inc(sem("mb1"), 1)

            et3 = "p (e t) -> p e t"

            def end_slots(b):
                dve.wait_ge(sem("rk_ps"), b + 1)
                w = TB * E
                for k, oh in enumerate((o0, o1)):
                    tot, run = qa, qb
                    ft, fn = (x.rearrange("p t e -> p (t e)") for x in (tot, run))
                    y.run(v.tensor_copy(ft.rearrange(et3, e=E), bank[7][:, P + 2 * w + k * w:P + 3 * w + k * w].rearrange("p (t e) -> p e t", e=E)))
                    y.run(v.tensor_tensor_scan(out=fn, data0=one64[:, :], data1=ft, initial=0.0, op0=ALU.mult, op1=ALU.add))
                    y.run(v.tensor_tensor(ft, fn, ft, ALU.subtract))
                    y.run(v.tensor_tensor(qc, bank[7][:, P + k * w:P + (k + 1) * w].rearrange("p (t e) -> p t e", e=E), ft.rearrange("p (e t) -> p t e", e=E), ALU.add))
                    y.run(v.tensor_tensor(qc, qc, be(carry[:, k, :]), ALU.add))
                    y.run(v.tensor_tensor(qc, qc, oh, ALU.mult))
                    dst = ps0 if k == 0 else pos1s[:, ds(b * TB, TB)]
                    y.mark(v.tensor_reduce(dst, qc, AX.X, ALU.add))
                    y.run(v.tensor_tensor(carry[:, k, :], carry[:, k, :], fn.rearrange(et3, e=E)[:, :, TB - 1], ALU.add))
                y.run(v.tensor_scalar(va, ps0, float(CAP), None, ALU.is_lt))
                y.mark(v.tensor_copy(valid1[:, ds(b * TB, TB), 0], va))
                y.run(v.tensor_scalar(key0, key0, -float(CAP), float(E * CAP), ALU.mult, ALU.add))
                y.run(v.tensor_tensor(ps0, ps0, key0, ALU.add))
                y.run(v.tensor_tensor(ps0, ps0, f64[2][:, ds(b * TB, TB)], ALU.subtract))
                y.run(v.tensor_tensor(ps0, ps0, va, ALU.mult))
                y.run(v.tensor_tensor(slot1[:, ds(b * TB, TB), 0], ps0, f64[2][:, ds(b * TB, TB)], ALU.add))
                dve.wait_ge(sem("xn1"), b * 2 + 2)
                y.run(v.tensor_scalar(xn[:, ds(b * TB, TB), D + 1], key1s[:, ds(b * TB, TB)], -1.0, float(E), ALU.mult, ALU.add))
                dve.sem_inc(sem("slot1"), 1)

            NORM = 13
            PICK = 5

            def end_step(b, r, last=False):
                n = b * 2 + r
                if not last:
                    stats(0, n + 1)
                end_experts(n, b, r)
                if not last:
                    norm(0, n + 1, z4)
                if r == 1 and not (isinstance(b, int) and b == 0):
                    end_choose(b - 1)
                if r == 0 and not (isinstance(b, int) and b <= 1):
                    end_slots(b - 2)
                end_sum(n)
                stats(1, n)
                if not last:
                    end_hidden(n + 1)
                norm(1, n, n4)

            dve.wait_ge(sem("consts1"), 6)
            dve.wait_ge(sem("ey"), Q0)
            y.run(v.memset(one64[:, :].rearrange(et3, e=E)[:, :, 0], 0.0))
            dve.wait_ge(sem("shared_in"), 64)
            y.run(v.memset(hT4[0:33, 0:D], 0.0))
            y.run(v.tensor_copy(bo_r[:, :], hT4[0:33, 0:D]))
            y.mark(v.tensor_copy(bo_r[0:1, :], bo[0:1, :]))
            y.run(v.tensor_copy(bo_h[:, :], bo[0:33, :]))
            y.run(v.tensor_tensor(bo_r[32:33, :], bo[32:33, :], bo_h[32:33, :], ALU.subtract))
            y.run(v.memset(hT4[0:33, 0:P], 1.0))
            y.run(v.tensor_copy(one_r[:, :], hT4[0:33, 0:P]))
            dve.sem_inc(sem("bo_r"), 1)
            stats(0, 0)
            norm(0, 0, z4)
            end_hidden(0)
            for b in range(2):
                for r in range(2):
                    end_step(b, r)
            per = 2 * (2 * NORM + 10) + (1 + 2 * PICK + 1 + 5) + (2 * 8 + 8)
            with dve.Fori(2, NB - 1) as b:
                y.enter(b, per, 2)
                for r in range(2):
                    end_step(b, r)
            y.leave(NB - 3)
            for r in range(2):
                end_step(NB - 1, r, r == 1)
            end_slots(NB - 2)
            end_choose(NB - 1)
            end_slots(NB - 1)
            y.run(v.tensor_tensor(g64, oh1s[:, :, :], carry[:, 0, :].unsqueeze(1).broadcast_to([P, NT, E]), ALU.mult))
            y.run(v.tensor_reduce(f64[0][:, :], g64, AX.X, ALU.add))
            y.run(v.tensor_tensor(pos1s[:, :], pos1s[:, :], f64[0][:, :], ALU.add))
            y.run(v.tensor_scalar(valid1[:, :, 1], pos1s[:, :], float(CAP), None, ALU.is_lt))
            y.run(v.tensor_scalar(key1s[:, :], key1s[:, :], -float(CAP), float(E * CAP), ALU.mult, ALU.add))
            y.run(v.tensor_scalar(f64[2][:, :], f64[2][:, :], float(N), None, ALU.add))
            y.run(v.tensor_tensor(pos1s[:, :], pos1s[:, :], key1s[:, :], ALU.add))
            y.run(v.tensor_tensor(pos1s[:, :], pos1s[:, :], f64[2][:, :], ALU.subtract))
            y.run(v.tensor_tensor(pos1s[:, :], pos1s[:, :], valid1[:, :, 1], ALU.mult))
            y.run(v.tensor_tensor(slot1[:, :, 1], pos1s[:, :], f64[2][:, :], ALU.add))
            dve.sem_inc(sem("slot1_second"), 1)
            y.run(v.tensor_tensor(c8[:, :], carry[:, 0, :], carry[:, 1, :], ALU.add))
            y.run(v.tensor_tensor(vq1[:, :].rearrange("p (e t) -> p e t", e=E), t128[:, :, :], c8[:, :].unsqueeze(2).broadcast_to([P, E, CT]), ALU.is_lt))
            y.run(v.tensor_tensor(t128[:, :, :].rearrange("p e t -> p (e t)"), vq1[:, :], tq1[:, :], ALU.mult))
            y.run(v.tensor_tensor(tq1[:, :], tq1[:, :], t128[:, :, :].rearrange("p e t -> p (e t)"), ALU.subtract))
            dve.wait_ge(sem("nT"), 8 * NB)
            y.run(v.tensor_reduce(xtot[:, :, :].rearrange("p k b -> p (k b)"), xsum[:, :, :, :].rearrange("p k b j -> p (k b) j"), AX.X, ALU.add))
            dve.sem_inc(sem("xtot"), 1)
            dve.wait_ge(sem("val_ps"), 1)
            y.run(v.tensor_copy(val[:, :, :].rearrange("p k b -> p (k b)"), bank[4][:, 0:DK * NB]))
            y.run(v.tensor_copy(vrep[:, :, :, :].rearrange("p k b m -> p (k b) m"), val[:, :, :].rearrange("p k b -> p (k b)").unsqueeze(2).broadcast_to([P, DK * NB, P])))
            dve.sem_inc(sem("vrep"), 1)
            for b in range(NB):
                dve.wait_ge(sem("att_ps"), b + 1)
                rows_ = yb[:, b * TB:(b + 1) * TB, :]
                v.tensor_tensor(rows_, rows_, bank[5 + b % 2][:, 0:D].unsqueeze(1).broadcast_to([P, TB, D]), ALU.add).then_inc(sem("att_add"), 1)
            dve.sem_inc(sem("sg_diff"), 1)

            dve.sem_inc(sem("h_lo"), 2)
            dve.sem_inc(sem("fTl"), 2)
            dve.sem_inc(sem("fy_free"), 2)
            u = st

            def low(n, r, w):
                dve.wait_ge(sem("fTh"), n * 2 + 2)
                for k in range(DK):
                    v.tensor_tensor(fTl[:, k, :], bank[k][:, :], fTh[:, k, :], ALU.subtract).then_inc(sem("fTl"), 1)
                dve.wait_ge(sem(f"fr_in{r}"), w)
                u.run(v.tensor_tensor(idf[:, r, :], fr[:, r, :, D + 1], ef[:, ds(n * 4, 4)], ALU.is_equal))
                u.run(v.tensor_tensor(idf[:, r, :], idf[:, r, :], fr[:, r, :, D], ALU.add))
                dve.sem_inc(sem("f_idx"), 1)
                u.run(v.tensor_tensor(idf[:, r, :], idf[:, r, :], vq1[:, ds(n * 4, 4)], ALU.mult))
                u.run(v.tensor_tensor(idf[:, r, :], idf[:, r, :], tq1[:, ds(n * 4, 4)], ALU.add))

            def hidden(n):
                if not isinstance(n, int) or n >= 1:
                    dve.wait_ge(sem("f_ps"), n)
                for j in range(HK):
                    dve.wait_ge(sem("hf"), n * HK + (j + 3))
                    u.run(v.tensor_copy(hTh[:, j, :], hf[:, j % 2, :]))
                    v.tensor_tensor(hTl[:, j, :], hf[:, j % 2, :], hTh[:, j, :], ALU.subtract).then_inc(sem("h_lo"), 1)

            def results(e, n, r, par):
                dve.wait_ge(sem("f_ps"), n + 1)
                dve.wait_ge(sem("b2_in"), e * 16 + 16)
                if not isinstance(n, int) or n >= 1:
                    dve.wait_ge(sem("f_out"), n * 64)
                for h in range(2):
                    u.mark(v.tensor_tensor(fy[:, 2 * h:2 * h + 2, :], bank[4 + 2 * par + h][:, :].rearrange("p (a d) -> p a d", a=2),
                                           b2r[:, r, :].unsqueeze(1).broadcast_to([P, 2, D]), ALU.add))
                u.run(v.tensor_copy(idxu[:, :, 0], idf[:, par, :]))
                dve.sem_inc(sem("fy"), 1)
                dve.sem_inc(sem("fy_free"), 1)

            def block2(e, r, jb, last=False):
                n = e * 4 + jb
                hidden(n)
                if not last:
                    low(n + 1, (jb + 1) % 2, e * 32 + 16 * ((jb + 1) // 2 + 1))
                results(e, n, r, jb % 2)

            dve.wait_ge(sem("fT_ps"), 1)
            low(0, 0, 16)
            first = (HK + 4 + 3)
            with dve.Fori(0, E // 2 - 1) as t:
                u.enter(t, 8 * first, 0)
                for r in range(2):
                    for jb in range(4):
                        block2(t * 2 + r, r, jb)
            u.leave(E // 2 - 1)
            for r in range(2):
                for jb in range(4):
                    block2(E - 2 + r, r, jb, r == 1 and jb == 3)

            dve.wait_ge(sem("gates1"), 2)
            u.run(v.tensor_tensor(gates1[:, :, :], gates1[:, :, :], valid1[:, :, :], ALU.mult))

            def output(t, r):
                n = t * 2 + r
                dve.wait_ge(sem(f"ol_in{r}"), t * 16 + 16)
                if not isinstance(t, int):
                    dve.wait_ge(sem(f"stored{r}"), t * 16)
                for a in range(4):
                    u.mark(v.scalar_tensor_tensor(out=oo[:, r, a, :], in0=ol[:, r, a, 0, :], scalar=gates1[:, ds(n * 4 + a, 1), 0],
                                                  in1=row(n, a), op0=ALU.mult, op1=ALU.add))
                u.settle()
                for a in range(4):
                    u.mark(v.scalar_tensor_tensor(out=oo[:, r, a, :], in0=ol[:, r, a, 1, :], scalar=gates1[:, ds(n * 4 + a, 1), 1],
                                                  in1=oo[:, r, a, :], op0=ALU.mult, op1=ALU.add))
                u.settle()
                dve.sem_inc(sem("oo"), 1)

            for r in range(2):
                output(0, r)
            with dve.Fori(1, NB) as t:
                u.enter(t, 16, 1)
                for r in range(2):
                    output(t, r)
            u.leave(NB - 1)


_INS = ['L0_attn_x', 'L0_attn_A', 'L0_attn_Bm', 'L0_attn_Cm', 'L0_attn_Dm', 'L0_attn_ln_w', 'L0_attn_ln_b', 'L0_attn_W_out',
        'L0_attn_b_out', 'L0_ffn_router_weight', 'L0_ffn_correction_bias', 'L0_ffn_w_gate', 'L0_ffn_w_up', 'L0_ffn_w_down',
        'L0_ffn_sw_gate', 'L0_ffn_sw_up', 'L0_ffn_sw_down', 'L1_attn_w_qkv', 'L1_attn_w_o', 'L1_ffn_wg', 'L1_ffn_w1',
        'L1_ffn_b1', 'L1_ffn_w2', 'L1_ffn_b2']
_OUTS = [((8, 1024, 256), 'float32')]


def kernel(**inputs):
    import numpy as _np
    import concourse.bacc as _bacc
    from concourse import mybir as _mybir
    from concourse.bass_utils import run_bass_kernel_spmd as _run

    nc = _bacc.Bacc("TRN2", target_bir_lowering=False, num_devices=1)
    arrays, args = {}, []
    for name in _INS:
        a = _np.ascontiguousarray(inputs[name])
        arrays[f"in_{name}_dram"] = a
        args.append(nc.dram_tensor(f"in_{name}_dram", a.shape, _mybir.dt.from_np(a.dtype), kind="ExternalInput").ap())
    for i, (shape, dtype) in enumerate(_OUTS):
        dt = _mybir.dt.from_np(_np.dtype(dtype))
        args.append(nc.dram_tensor(f"out_{i}_dram", shape, dt, kind="ExternalOutput").ap())
    bass_ssm_moe_then_attention_moe(nc, *args)
    r = _run(nc, [arrays], core_ids=[0])
    return r.results[0]["out_0_dram"]
```
